# Optimizing a Trainium2 kernel written in Bass

```python
import numpy as np
import jax
import jax.numpy as jnp

def _softmax(x, axis=-1):
    return jax.nn.softmax(x, axis=axis)

def _gelu(x):
    return jax.nn.gelu(x, approximate=True)

def _silu(x):
    return jax.nn.silu(x)

def _sigmoid(x):
    return jax.nn.sigmoid(x)

def _layernorm(x, axis=-1, eps=1e-05):
    m = jnp.mean(x, axis=axis, keepdims=True)
    v = jnp.var(x, axis=axis, keepdims=True)
    return (x - m) / jnp.sqrt(v + eps)

def _scatter_add(tgt, idx, src, axis=0):
    return tgt.at[idx].add(src)

def _segment_sum(src, seg, n):
    return jax.ops.segment_sum(src, seg, n)
kernel_name = 'mk_gps_d1_gnn_r8_674c07'

def setup_inputs(seed: int=0):
    np.random.seed(seed)
    _w = jnp.asarray

    def _rec_inputs():
        import jax
        import jax.numpy as jnp
        _gk = jax.random.key(seed)
        x = -0.0002117 + 1 * jax.random.normal(jax.random.fold_in(_gk, 1), (1250, 512), jnp.float32)
        src = jax.random.randint(jax.random.fold_in(_gk, 2), (20000,), 0, 1250, jnp.int32)
        dst = jax.random.randint(jax.random.fold_in(_gk, 3), (20000,), 0, 1250, jnp.int32)
        _o = jnp.argsort(dst, stable=True)
        src = src[_o]
        dst = dst[_o]
        return (x, src, dst)
    x, src, dst = _rec_inputs()

    def _L0_gnn_setup():
        import jax, jax.numpy as jnp
        import numpy as np
        N = 6250
        DIM = 512
        E = 18750
        key = jax.random.key(seed)
        k_x, k_src, k_dst, k_w, k_b = jax.random.split(key, 5)
        x = jax.random.normal(k_x, (N, DIM), dtype=jnp.float32)
        src = jax.random.randint(k_src, (E,), 0, N)
        dst = jax.random.randint(k_dst, (E,), 0, N)
        edge_index = jnp.stack([src, dst], axis=0)
        bound = 1.0 / np.sqrt(DIM)
        W = jax.random.uniform(k_w, (DIM, DIM), minval=-bound, maxval=bound, dtype=jnp.float32)
        b = jax.random.uniform(k_b, (DIM,), minval=-bound, maxval=bound, dtype=jnp.float32)
        alpha = jnp.float32(0.5)
        return {'x': x, 'edge_index': edge_index, 'num_nodes': N, 'alpha': alpha, 'W': W, 'b': b}
    _L0_gnn_all = _L0_gnn_setup()
    _L0_gnn_in = {k: v for k, v in _L0_gnn_all.items() if k in ('alpha', 'W', 'b')}
    del _L0_gnn_all

    def _L0_mix_setup():
        import jax, jax.numpy as jnp
        import numpy as np
        import math
        B, N, DIM = (4, 512, 512)
        HEADS, DH, NBF = (8, 64, 256)
        MLP_H = DIM * 2

        def layernorm(x, g, b, eps=1e-05):
            mu = jnp.mean(x, axis=-1, keepdims=True)
            var = jnp.mean(jnp.square(x - mu), axis=-1, keepdims=True)
            return (x - mu) * jax.lax.rsqrt(var + eps) * g + b

        def softmax_kernel(x, pmat):
            xp = jnp.einsum('bhnd,df->bhnf', x, pmat)
            xp = xp - jnp.max(xp, axis=-1, keepdims=True)
            return jnp.exp(xp) / math.sqrt(pmat.shape[-1])
        key = jax.random.key(seed)
        ks = jax.random.split(key, 8)
        s = lambda d: 1.0 / math.sqrt(d)
        return {'x': jax.random.normal(ks[0], (B, N, DIM), jnp.float32), 'Wqkv': jax.random.normal(ks[1], (DIM, 3 * HEADS * DH), jnp.float32) * s(DIM), 'bqkv': jnp.zeros((3 * HEADS * DH,), jnp.float32), 'Pmat': jax.random.normal(ks[2], (DH, NBF), jnp.float32), 'Wproj': jax.random.normal(ks[3], (HEADS * DH, DIM), jnp.float32) * s(HEADS * DH), 'bproj': jnp.zeros((DIM,), jnp.float32), 'W1': jax.random.normal(ks[4], (DIM, MLP_H), jnp.float32) * s(DIM), 'b1': jnp.zeros((MLP_H,), jnp.float32), 'W2': jax.random.normal(ks[5], (MLP_H, DIM), jnp.float32) * s(MLP_H), 'b2': jnp.zeros((DIM,), jnp.float32), 'g1': jnp.ones((DIM,), jnp.float32), 'be1': jnp.zeros((DIM,), jnp.float32), 'g2': jnp.ones((DIM,), jnp.float32), 'be2': jnp.zeros((DIM,), jnp.float32)}
    _L0_mix_all = _L0_mix_setup()
    _L0_mix_in = {k: v for k, v in _L0_mix_all.items() if k in ('Wqkv', 'bqkv', 'Pmat', 'Wproj', 'bproj', 'W1', 'b1', 'W2', 'b2', 'g1', 'be1', 'g2', 'be2')}
    del _L0_mix_all

    def _L0_ffn_setup():
        import jax, jax.numpy as jnp
        import numpy as np
        BINS = jnp.array([-1.5, -1.0, -0.5, 0.0, 0.5, 1.0, 1.5], dtype=jnp.float32)
        N_BINS = BINS.shape[0] + 1
        INDEX = 0
        key = jax.random.key(seed)
        k1, k2 = jax.random.split(key)
        x = jax.random.normal(k1, (8, 512, 512), dtype=jnp.float32)
        W = jax.random.normal(k2, (N_BINS, 512, 512), dtype=jnp.float32) * 0.02
        return {'x': x, 'W': W}
    _L0_ffn_all = _L0_ffn_setup()
    _L0_ffn_in = {k: v for k, v in _L0_ffn_all.items() if k in ('W',)}
    del _L0_ffn_all
    return {'x': x, 'src': src, 'dst': dst, 'L0_gnn_alpha': _L0_gnn_in['alpha'], 'L0_gnn_W': _L0_gnn_in['W'], 'L0_gnn_b': _L0_gnn_in['b'], 'L0_mix_Wqkv': _L0_mix_in['Wqkv'], 'L0_mix_bqkv': _L0_mix_in['bqkv'], 'L0_mix_Pmat': _L0_mix_in['Pmat'], 'L0_mix_Wproj': _L0_mix_in['Wproj'], 'L0_mix_bproj': _L0_mix_in['bproj'], 'L0_mix_W1': _L0_mix_in['W1'], 'L0_mix_b1': _L0_mix_in['b1'], 'L0_mix_W2': _L0_mix_in['W2'], 'L0_mix_b2': _L0_mix_in['b2'], 'L0_mix_g1': _L0_mix_in['g1'], 'L0_mix_be1': _L0_mix_in['be1'], 'L0_mix_g2': _L0_mix_in['g2'], 'L0_mix_be2': _L0_mix_in['be2'], 'L0_ffn_W': _L0_ffn_in['W']}

def reference(x, src, dst, L0_gnn_alpha, L0_gnn_W, L0_gnn_b, L0_mix_Wqkv, L0_mix_bqkv, L0_mix_Pmat, L0_mix_Wproj, L0_mix_bproj, L0_mix_W1, L0_mix_b1, L0_mix_W2, L0_mix_b2, L0_mix_g1, L0_mix_be1, L0_mix_g2, L0_mix_be2, L0_ffn_W):
    import jax
    import jax.numpy as jnp

    def _L0_gnn_ref(x, edge_index, num_nodes, alpha, W, b):
        import jax, jax.numpy as jnp
        import numpy as np
        N = 6250
        DIM = 512
        E = 18750
        src = edge_index[0]
        dst = edge_index[1]
        agg = jax.ops.segment_sum(x[src], dst, num_segments=num_nodes)
        deg = jax.ops.segment_sum(jnp.ones_like(dst, dtype=x.dtype), dst, num_segments=num_nodes)
        deg = jnp.maximum(deg, 1.0)
        agg = agg / deg[:, None]
        return x + alpha * (agg @ W.T + b)

    def _L0_mix_ref(x, Wqkv, bqkv, Pmat, Wproj, bproj, W1, b1, W2, b2, g1, be1, g2, be2):
        import jax, jax.numpy as jnp
        import numpy as np
        import math
        B, N, DIM = (4, 512, 512)
        HEADS, DH, NBF = (8, 64, 256)
        MLP_H = DIM * 2

        def layernorm(x, g, b, eps=1e-05):
            mu = jnp.mean(x, axis=-1, keepdims=True)
            var = jnp.mean(jnp.square(x - mu), axis=-1, keepdims=True)
            return (x - mu) * jax.lax.rsqrt(var + eps) * g + b

        def softmax_kernel(x, pmat):
            xp = jnp.einsum('bhnd,df->bhnf', x, pmat)
            xp = xp - jnp.max(xp, axis=-1, keepdims=True)
            return jnp.exp(xp) / math.sqrt(pmat.shape[-1])
        b, n, d = x.shape
        h = layernorm(x, g1, be1)
        qkv = h @ Wqkv + bqkv
        q, k, v = jnp.split(qkv, 3, axis=-1)
        to_heads = lambda t: t.reshape(b, n, HEADS, DH).transpose(0, 2, 1, 3)
        q, k, v = (to_heads(q), to_heads(k), to_heads(v))
        q_prime = softmax_kernel(q, Pmat)
        k_prime = softmax_kernel(k, Pmat)
        kv = jnp.einsum('bhnf,bhne->bhfe', k_prime, v)
        k_sum = jnp.sum(k_prime, axis=2) + 1e-06
        z = 1.0 / jnp.einsum('bhnf,bhf->bhn', q_prime, k_sum)[..., None]
        attn = jnp.einsum('bhnf,bhfe->bhne', q_prime, kv) * z
        attn = attn.transpose(0, 2, 1, 3).reshape(b, n, HEADS * DH)
        x = x + attn @ Wproj + bproj
        h2 = layernorm(x, g2, be2)
        mlp = jax.nn.gelu(h2 @ W1 + b1, approximate=False) @ W2 + b2
        return x + mlp

    def _L0_ffn_ref(x, W):
        import jax, jax.numpy as jnp
        import numpy as np
        BINS = jnp.array([-1.5, -1.0, -0.5, 0.0, 0.5, 1.0, 1.5], dtype=jnp.float32)
        N_BINS = BINS.shape[0] + 1
        INDEX = 0
        y = x[..., INDEX]
        mem = jnp.sum(y[..., None] > BINS, axis=-1)
        B, T, D = x.shape
        xf = x.reshape(B * T, D)
        memf = mem.reshape(B * T)
        out = jnp.zeros((B * T, W.shape[-1]), dtype=x.dtype)
        for k in range(N_BINS):
            sel = (memf == k)[:, None].astype(x.dtype)
            out = out + sel * (xf @ W[k])
        return out.reshape(B, T, W.shape[-1])
    edge_index = jnp.stack([src, dst])
    xn = _layernorm(x, axis=-1)
    x = x + _L0_gnn_ref(xn, edge_index, 1250, L0_gnn_alpha, L0_gnn_W, L0_gnn_b) + _L0_mix_ref(xn[None], L0_mix_Wqkv, L0_mix_bqkv, L0_mix_Pmat, L0_mix_Wproj, L0_mix_bproj, L0_mix_W1, L0_mix_b1, L0_mix_W2, L0_mix_b2, L0_mix_g1, L0_mix_be1, L0_mix_g2, L0_mix_be2)[0]
    x = x + _L0_ffn_ref(_layernorm(x, axis=-1)[None], L0_ffn_W)[0]
    return x

_drawn_inputs = setup_inputs


def setup_inputs(seed=0):
    import zlib

    import numpy as np

    out = dict(_drawn_inputs(seed))
    spreads = {'L0_mix_bqkv': (0.0, 0.1),
     'L0_mix_bproj': (0.0, 0.1),
     'L0_mix_b1': (0.0, 0.1),
     'L0_mix_b2': (0.0, 0.1),
     'L0_mix_g1': (1.0, 0.2),
     'L0_mix_be1': (0.0, 0.1),
     'L0_mix_g2': (1.0, 0.2),
     'L0_mix_be2': (0.0, 0.1)}
    factors = {'L0_gnn_b': 3.013}
    for name, (base, spread) in spreads.items():
        noise = np.random.default_rng([zlib.crc32(name.encode()), seed]).standard_normal(out[name].shape)
        drawn = base * np.exp(spread * noise) if base else spread * noise
        out[name] = jnp.asarray(drawn.astype(out[name].dtype))
    for name, factor in factors.items():
        out[name] = (out[name] * factor).astype(out[name].dtype)
    return out
```

```python
from contextlib import ExitStack

import concourse.bass as bass
from concourse import mybir

F32 = mybir.dt.float32
F16 = mybir.dt.float16
BF16 = mybir.dt.bfloat16
I32 = mybir.dt.int32
F32R = mybir.dt.float32r
ALU = mybir.AluOpType
ACT = mybir.ActivationFunctionType
AX = mybir.AxisListType.X

EPS = 1e-5
KSUM_EPS = 1e-6
BINS = [-1.5, -1.0, -0.5, 0.0, 0.5, 1.0, 1.5]


def up(n):
    return (n + 31) // 32 * 32


def row_broadcast(row, n):
    return bass.AP(tensor=row.tensor, offset=row.offset, ap=[[0, n]] + [list(d) for d in row.ap])


class PsumPlan:

    def __init__(self):
        self.order, self.uses, self.next = {}, [0] * 8, 0

    def add(self, key, banks=tuple(range(8))):
        while self.next % 8 not in banks:
            self.next += 1
        b = self.next % 8
        self.next += 1
        self.order[key] = (len(self.order), b, self.uses[b])
        self.uses[b] += 1


def build(nc, x, src, dst, alpha, gW, gb, Wqkv, bqkv, Pm, Wp, bp, W1, b1, W2, b2, g1, be1, g2, be2, FW, out):
    N, D = x.shape
    E = src.shape[0]
    T = 125
    NT = N // T
    EH = 4
    ER = E // (EH * T)
    C = D // 128
    DH, NF = Pm.shape
    H = D // DH
    PAIRS = H // 2
    M = W1.shape[1]
    MC = M // 128
    NB = len(BINS) + 1
    ST = 128
    SLOT_TILES = (N + NB * (ST - 1)) // ST
    GROUPS = [(0, 4), (4, 4), (8, 2)]
    CH = [(t * T, n * T) for t, n in GROUPS]
    NW = N + 2
    assert N == NT * T and E == ER * EH * T and DH == 64 and NF == 256 and CH[-1][0] + CH[-1][1] == N
    FC = NF // 128

    def tiles(g):
        return range(GROUPS[g][0], GROUPS[g][0] + GROUPS[g][1])

    plan = PsumPlan()
    plan.add("edge_cols")
    plan.add("edge_range")
    for t in range(NT + 1):
        if t < NT:
            for j in range(3):
                plan.add(("A", t, j))
        if t >= 1:
            for j in range(3):
                plan.add(("AT", t - 1, j))
    for k in range(C):
        plan.add(("gWT", k))
    for n in range(4):
        if n < 3:
            for c in range(C):
                plan.add(("agg", n, c))
        if n >= 1:
            for t in tiles(n - 1):
                plan.add(("gnn", t))
    for c in range(C):
        for j in range(3):
            plan.add(("hT", c, j))
    for t in range(NT):
        plan.add(("v", t))
    work = (0, 1, 2, 3, 4, 5)
    for p in range(PAIRS):
        for n in range(3):
            for w in range(2):
                plan.add(("qk", p, n, w), work)
        for t in range(NT):
            plan.add(("kf", p, t), work)
            plan.add(("qf", p, t), work)
            if t >= 1:
                plan.add(("qT", p, t - 1), work)
        for i in range(2):
            plan.add(("kv", p, i), (6 + i,))
        plan.add(("qT", p, NT - 1), work)
        plan.add(("kvT", p), work)
        for i in range(2):
            for n in range(3):
                plan.add(("att", p, i, n), work)
    for t in range(NT):
        plan.add(("proj", t))
    for n in range(4):
        if n < 3:
            for c in range(C):
                plan.add(("h2T", c, n))
        if n >= 1:
            for t in tiles(n - 1):
                plan.add(("down", t))
        if n < 3:
            for m in range(MC):
                plan.add(("up", n, m))
    plan.add("rank")
    for s in range(SLOT_TILES + 1):
        if s < SLOT_TILES:
            plan.add(("yT", s))
        if s >= 1:
            plan.add(("ffn", s - 1))

    base = 16512
    top = [base]

    def at(name, shape, dtype, offset):
        return nc.alloc_sbuf_tensor_at(name, shape, dtype, offset=offset)

    def place(size):
        o = top[0]
        top[0] += (size + 31) // 32 * 32
        return o

    o_xn = place(NT * D * 4)
    o_x = place(up(NT * D * 4))
    o_hT = place(C * N * 4)
    o_v = place(21120)
    o_qk = place(2 * N * 4)
    o_att = place(PAIRS * N * 4)
    o_wp = place(C * D * 4)
    o_wv = place(2 * N * 4)
    o_kv = place(2 * NF * 4 + 4 * 65 * 4)
    o_hn = place(NT * D * 4)
    o_acc = place(NT * D * 4)
    o_ring = place(max(4 * 2 * NF * 4, EH * (up(2 * NW) + 256)))

    xn = at("xn", [T, NT, D], F32, o_xn)
    wqk = at("wqk", [128, C, 2 * D], F32, o_x)
    o_w = o_x
    w1s = at("w1s", [128, C * M], F32, o_w)
    w1l = at("w1l", [128, C * M], F32R, o_w)
    w1h = at("w1h", [128, C * M], F32R, o_w + C * M * 4)
    w2s = at("w2s", [128, MC * D], F32, o_w + 2 * C * M * 4)
    w2l = at("w2l", [128, MC * D], F32R, o_w + 2 * C * M * 4)
    w2h = at("w2h", [128, MC * D], F32R, o_w + 3 * C * M * 4)
    hT = at("hT", [128, C, N], F32, o_hT)
    v65 = at("v65", [T, NT, H, DH + 1], F32, o_v)
    qkT = at("qkT", [128, 2, N], F32, o_qk)
    attT = at("attT", [128, PAIRS, N], F32, o_att)
    wps = at("wps", [128, C, D], F32, o_wp)
    wvs = at("wvs", [128, C, D], F32, o_wv)
    den = at("den", [1, 2 * N], F32, o_wv)
    kvT = at("kvT", [DH + 1, 2, NF], F32, o_kv)
    kv = at("kv", [128, 2 * FC, DH + 1], F32, o_kv + 2 * NF * 4)
    hn = at("hn", [T, NT, D], F32, o_hn)
    eqT = at("eqT", [128, 2 * FC, N], F32, o_hn)
    acc = at("acc", [T, NT, D], F32, o_acc)
    ering = at("ering", [T, 4, 2 * NF], F32, o_ring)
    ohs = at("ohs", [T, EH, NW], BF16, o_ring)
    ohd = at("ohd", [T, EH, 128], BF16, o_ring + up(EH * NW * 2))
    xh = at("xh", [T, NT, D], F32R, o_hn)
    xl = at("xl", [T, NT, D], F32R, o_xn)
    ath = at("ath", [T, NT, CH[0][1]], F32R, o_x)
    atl = at("atl", [T, NT, N], F32R, o_hT)
    AT = at("AT", [T, NT, N], F32, o_hT)
    arow = at("arow", [T, 2, N], F32, o_hT + up(NT * N * 4))
    o_gw = o_hT + up(NT * N * 4) + up(2 * N * 4)
    gws = at("gws", [128, C, D], F32, o_gw)
    gwT = at("gwT", [128, C, D], F32, o_gw + C * D * 4)
    assert o_gw + 2 * C * D * 4 <= o_wv
    aggT = [at("aggT0", [128, C, CH[0][1]], F32, o_gw),
            at("aggT1", [128, C, CH[0][1]], F32, o_hT + up(NT * N * 4))]
    W_END = o_w + 4 * C * M * 4
    GC = CH[0][1]
    gf = at("gf", [128, MC, GC], F32, up(W_END))
    gl = at("gl", [128, MC, GC], F32R, up(W_END))
    gh = at("gh", [128, MC, GC], F32R, up(W_END) + MC * GC * 4)
    h2h = at("h2h", [128, C, GC], F32R, up(W_END) + 2 * MC * GC * 4)
    h2f = at("h2f", [128, C, GC], F32, o_ring)
    h2l = at("h2l", [128, C, GC], F32R, o_ring)
    assert W_END > o_qk and up(W_END) + (2 * MC + C) * GC * 4 <= o_hn
    fw = at("fw", [128, NB * C * D], F32, o_xn)
    ys = at("ys", [ST, SLOT_TILES, D], F32, o_qk)
    yT = at("yT", [128, 2, C * ST], F32, o_qk + SLOT_TILES * D * 4)
    ob = at("ob", [ST, 2, D], F32, o_qk + (SLOT_TILES + 2) * D * 4)
    assert o_qk + (SLOT_TILES + 4) * D * 4 <= o_hn

    def small(name, shape, dtype):
        size = 4 if dtype in (F32, I32) else 2
        for n in shape[1:]:
            size *= n
        return at(name, shape, dtype, place(size))

    ident = small("ident", [128, 128], F32)
    ones = small("ones", [128, 128], F32)
    iota = small("iota", [T, NW], F16)
    dcol = small("dcol", [T, ER, EH], F32)
    scol = small("scol", [T, ER, EH], F32)
    pbd = small("pbd", [128, 2, NF], F32)
    gbb = small("gbb", [T, D], F32)
    bvb = small("bvb", [T, D], F32)
    bpb = small("bpb", [T, D], F32)
    b2b = small("b2b", [T, D], F32)
    zb = small("zb", [128, N], F32)
    zt = small("zt", [T, 2 * NT], F32)
    zr = small("zr", [T, 2 * NT], F32)
    g1c = small("g1c", [128, C], F32)
    be1c = small("be1c", [128, C], F32)
    g2c = small("g2c", [128, C], F32)
    be2c = small("be2c", [128, C], F32)
    bqkc = small("bqkc", [128, 2 * C], F32)
    b1c = small("b1c", [128, MC], F32)
    alc = small("alc", [T, 1], F32)
    st = small("st", [T, NT, 6], F32)
    mv = small("mv", [T, NT, 2], F32)
    kse = small("kse", [DH + 1, 1], F32)
    half = small("half", [T, NT], F32)
    rstd = small("rstd", [T, NT], F32)
    nmr = small("nmr", [T, NT], F32)
    tmp = small("tmp", [T, NT], F32)
    sums = small("sums", [T, NT], F32)
    sqs = small("sqs", [T, NT], F32)
    nmean = small("nmean", [T, NT], F32)
    deg3 = small("deg3", [T, NT, 3], F32)
    deg = small("deg", [T, NT], F32)
    coef = small("coef", [T, NT], F32)
    bounds = small("bounds", [NT, 2], I32)
    nmax = small("nmax", [T, 4, 2], F32)
    posi = small("posi", [T, NT], I32)
    exr = small("exr", [T, SLOT_TILES + 1], I32)
    edi = at("edi", [ER, 2, EH * T], I32, o_x)
    edf = at("edf", [ER, 2, EH * T], F32, o_x + up(2 * EH * T * 4))
    mm = at("mm", [ER, 2], F32, o_x + 8064)
    mdiag = at("mdiag", [ER, 2, ER], F32, o_x + 8096)
    rrow = at("rrow", [NT, 8, ER], F32, o_x + 9440)
    rsm = at("rsm", [NT, 8], F32, o_x + 14592)
    arow_e = at("arow_e", [NT, 2, ER], F32, o_x + 14624)
    t0 = at("t0", [NT, 2], F32, o_x + 15296)
    mem = at("mem", [T, NT], F32, o_ring)
    cmp = at("cmp", [T, len(BINS), NT], F32, o_ring + 64)
    boh = at("boh", [T, NT, NB], BF16, o_ring + 384)
    cnt = at("cnt", [T, 2, NB], F32, o_ring + 704)
    below = at("below", [T, NB, NB], F32, o_ring + 1376)
    tl = at("tl", [T, NT, NB], F32, o_ring + 1760)
    ctl = at("ctl", [T, 2, NB + 1], F32, o_ring + 2112)
    pr = at("pr", [T, NT, NB], F32, o_ring + 2208)
    posf = at("posf", [T, NT], F32, o_ring + 2560)
    slotc = at("slotc", [T, NB, SLOT_TILES], F32, o_ring + 2624)
    exf = at("exf", [T, SLOT_TILES], F32, o_ring + 3200)
    jrow = small("jrow", [T, SLOT_TILES], F32)
    krow = small("krow", [T, NB], F32)
    lower = small("lower", [T, NB, NB], F32)
    many = small("many", [T, NT, NB], F32)
    trib = small("trib", [T, 128], BF16)
    onesb = small("onesb", [T, 128], BF16)
    assert top[0] <= nc.sbuf_usable_end, (top[0], nc.sbuf_usable_end)

    d_den = nc.dram_tensor("den_scratch", (PAIRS, 2 * N), F32, kind="Internal").ap()
    d_z = nc.dram_tensor("z_scratch", (PAIRS, 2 * N), F32, kind="Internal").ap()
    d_y = nc.dram_tensor("y_sorted", (SLOT_TILES * ST, D), F32, kind="Internal").ap()
    d_o = nc.dram_tensor("o_sorted", (SLOT_TILES * ST, D), F32, kind="Internal").ap()

    with ExitStack() as ctx:
        P = [ctx.enter_context(nc.psum_tensor(f"bank{i}", [128, 512], F32)) for i in range(8)]

        def sem(name):
            return ctx.enter_context(nc.semaphore(name))

        psum_filled = sem("psum_filled")
        bank_read = [sem(f"bank_read{i}") for i in range(8)]
        ld = {k: sem("ld_" + k) for k in ("edges", "x", "gw", "bias", "pbd", "wqk", "wv", "wp", "w1", "w2", "fw",
                                          "den", "dent", "z", "zb", "zero", "out")}
        gathered = [sem(f"gathered{i}") for i in range(NT)]
        ld_ys = [sem(f"ld_ys{i}") for i in range(SLOT_TILES)]
        st_o = [sem(f"st_o{i}") for i in range(2)]
        scattered = sem("scattered")
        consts = sem("consts")
        zeros_ready = sem("zeros_ready")
        edge_tab = sem("edge_tab")
        bounds_ready = sem("bounds_ready")
        oh_ready = [sem(f"oh_ready{b}") for b in range(EH)]
        oh_used = [sem(f"oh_used{b}") for b in range(EH)]
        dve = sem("dve")
        pool = sem("pool")
        stats = sem("stats")
        rstd_ready = sem("rstd_ready")
        normed = sem("normed")
        acc_pre = sem("acc_pre")
        x_high = sem("x_high")
        x_low = sem("x_low")
        x_whole = sem("x_whole")
        at_high = sem("at_high")
        at_low = sem("at_low")
        at_used = sem("at_used")
        xnb_ready = sem("xnb_ready")
        max_ready = sem("max_ready")
        e_ready = [sem("ek_ready"), sem("eq_ready")]
        z_ready = sem("z_ready")
        attn_ready = sem("attn_ready")
        acc_x2 = sem("acc_x2")
        summed = sem("summed")
        squared = sem("squared")
        mean_ready = sem("mean_ready")
        act = sem("act")
        w_high = sem("w_high")
        w_low = sem("w_low")
        h2_split = sem("h2_split")
        g_split = sem("g_split")
        boh_ready = sem("boh_ready")
        slots_ready = sem("slots_ready")
        final = sem("final")
        block = ctx.enter_context(nc.Block())

        def filled(eng, key):
            place_, bank, _ = plan.order[key]
            eng.wait_ge(psum_filled, place_ + 1)
            return P[bank]

        def read_out(ins, key):
            ins.then_inc(bank_read[plan.order[key][1]], 1)

        def evacuated(eng, key):
            _, bank, before = plan.order[key]
            eng.wait_ge(bank_read[bank], before + 1)

        @block.sync
        def _(sp):
            sp.dma_start(edi[:, 0, :], dst.rearrange("(a e) -> a e", a=ER)).then_inc(ld["edges"], 16)
            sp.dma_start(edi[:, 1, :], src.rearrange("(a e) -> a e", a=ER)).then_inc(ld["edges"], 16)
            sp.dma_start(acc[:, :, :], x.rearrange("(t p) d -> p t d", p=T)).then_inc(ld["x"], 16)
            sp.dma_start(alc[:, :], row_broadcast(alpha, T)).then_inc(ld["bias"], 16)
            for tile, row in ((gbb, gb), (bvb, bqkv[2 * D:3 * D]), (bpb, bp), (b2b, b2)):
                sp.dma_start(tile[:, :], row_broadcast(row, T)).then_inc(ld["bias"], 16)
            for tile, row in ((g1c, g1), (be1c, be1), (g2c, g2), (be2c, be2), (bqkc, bqkv[0:2 * D]), (b1c, b1)):
                sp.dma_start(tile[:, :], row.rearrange("(c p) -> p c", p=128),
                             allow_slow_non_contiguous=True).then_inc(ld["bias"], 16)
            sp.dma_start(gws[:, :, :], gW.rearrange("(c p) d -> p c d", p=128)).then_inc(ld["gw"], 16)
            sp.wait_ge(consts, 2)
            for i in range(2):
                sp.dma_start(pbd[DH * i:DH * i + DH, i, :], Pm).then_inc(ld["pbd"], 16)
            sp.dma_start(wvs[:, :, :], Wqkv[:, 2 * D:3 * D].rearrange("(c p) n -> p c n", p=128)).then_inc(ld["wv"], 16)
            sp.wait_ge(zeros_ready, 1)
            for s in range(SLOT_TILES):
                sp.dma_start(d_y[s * ST:(s + 1) * ST, :], zb[:, 0:D]).then_inc(ld["zero"], 16)
            filled(sp, ("agg", 2, C - 1))
            sp.dma_start(wqk[:, :, :], Wqkv[:, 0:2 * D].rearrange("(c p) n -> p c n", p=128)).then_inc(ld["wqk"], 16)
            evacuated(sp, ("gnn", NT - 1))
            sp.dma_start(wps[:, :, :], Wp.rearrange("(c p) n -> p c n", p=128)).then_inc(ld["wp"], 16)
            for p in range(PAIRS):
                if p == PAIRS - 1:
                    filled(sp, ("qk", p, 2, 1))
                    sp.dma_start(w1s[:, :].rearrange("p (c n) -> p c n", n=M),
                                 W1.rearrange("(c p) n -> p c n", p=128)).then_inc(ld["w1"], 16)
                evacuated(sp, ("att", p, 1, 2))
                sp.dma_start(d_den[p:p + 1, :], den[0:1, :]).then_inc(ld["den"], 16)
                sp.wait_ge(ld["den"], 16 * (p + 1))
                sp.dma_start(zt[:, :], d_den[p, :].rearrange("(q j) -> q j", q=T)).then_inc(ld["dent"], 16)
                sp.wait_ge(z_ready, p + 1)
                sp.dma_start(d_z[p, :].rearrange("(q j) -> q j", q=T), zr[:, :]).then_inc(ld["z"], 16)
                sp.wait_ge(ld["z"], 16 * (p + 1))
                if p:
                    sp.wait_ge(attn_ready, p)
                for i in range(2):
                    sp.dma_start(zb[DH * i:DH * i + DH, :],
                                 row_broadcast(d_z[p, i * N:(i + 1) * N], DH)).then_inc(ld["zb"], 16)
            sp.dma_start(w2s[:, :].rearrange("p (c n) -> p c n", n=D),
                         W2.rearrange("(c p) n -> p c n", p=128)).then_inc(ld["w2"], 16)
            sp.wait_ge(acc_x2, NT)
            sp.wait_ge(normed, 3 * NT)
            fwv = FW.rearrange("k (c p) n -> p (k c) n", p=128)
            fws = fw[:, :].rearrange("p (k n) -> p k n", n=D)
            sp.dma_start(fws[:, 0:2 * C, :], fwv[:, 0:2 * C, :]).then_inc(ld["fw"], 16)
            filled(sp, ("up", 2, MC - 1))
            for k in range(2, NB):
                if k == 6:
                    filled(sp, ("down", NT - 1))
                sp.dma_start(fws[:, k * C:(k + 1) * C, :], fwv[:, k * C:(k + 1) * C, :]).then_inc(ld["fw"], 16)
            sp.wait_ge(scattered, 16 * NT)
            for s in range(SLOT_TILES):
                sp.dma_start(ys[:, s, :], d_y[s * ST:(s + 1) * ST, :]).then_inc(ld_ys[s], 16)
            for s in range(SLOT_TILES):
                evacuated(sp, ("ffn", s))
                sp.dma_start(d_o[s * ST:(s + 1) * ST, :], ob[:, s % 2, :]).then_inc(st_o[s % 2], 16)
            for t in range(NT):
                sp.wait_ge(final, t + 1)
                sp.dma_start(out[t * T:(t + 1) * T, :], acc[:, t, :]).then_inc(ld["out"], 16)
            sp.wait_ge(ld["out"], 16 * NT)

        @block.gpsimd
        def _(gp):
            chain = [0]

            def link(ins):
                chain[0] += 1
                ins.then_inc(pool, 1)
                gp.wait_ge(pool, chain[0])

            nc.gpsimd.memset(ident[:, :], 0.0)
            nc.gpsimd.memset(onesb[:, :], 1.0)
            nc.gpsimd.memset(lower[:, :, :], 1.0)
            link(nc.gpsimd.memset(trib[:, :], 0.0))
            nc.gpsimd.affine_select(out=ident[:, :], in_=ident[:, :], compare_op=ALU.not_equal, fill=1.0, base=0,
                                    pattern=[[-1, 128]], channel_multiplier=1)
            nc.gpsimd.affine_select(out=trib[:, :], in_=trib[:, :], compare_op=ALU.is_ge, fill=1.0, base=0,
                                    pattern=[[-1, 128]], channel_multiplier=1)
            nc.gpsimd.affine_select(out=lower[:, :, :], in_=lower[:, :, :], compare_op=ALU.is_gt, fill=0.0, base=0,
                                    pattern=[[1, NB], [-1, NB]], channel_multiplier=0)
            nc.gpsimd.memset(ones[:, :], 1.0)
            small_ok = {"allow_small_or_imprecise_dtypes": True}
            nc.gpsimd.iota(krow[:, :], pattern=[[1, NB]], base=0, channel_multiplier=0, **small_ok)
            nc.gpsimd.iota(many[:, :, :], pattern=[[ST, NT], [0, NB]], base=0, channel_multiplier=0, **small_ok)
            nc.gpsimd.iota(iota[:, :], pattern=[[1, NW]], base=0, channel_multiplier=0, **small_ok)
            nc.gpsimd.iota(jrow[:, :], pattern=[[1, SLOT_TILES]], base=0, channel_multiplier=0, **small_ok)
            nc.gpsimd.iota(arow_e[:, 0, :], pattern=[[1, ER]], base=1, channel_multiplier=0, **small_ok)
            nc.gpsimd.iota(arow_e[:, 1, :], pattern=[[-1, ER]], base=ER, channel_multiplier=0, **small_ok)
            nc.gpsimd.iota(t0[:, 0:1], pattern=[[1, 1]], base=0, channel_multiplier=T, **small_ok)
            nc.gpsimd.iota(t0[:, 1:2], pattern=[[1, 1]], base=T - 1, channel_multiplier=T, **small_ok)
            link(nc.gpsimd.memset(kse[:, :], 0.0))
            link(nc.gpsimd.memset(kse[DH:DH + 1, :], NF * KSUM_EPS / 16))
            nc.gpsimd.memset(half[:, :], -0.5).then_inc(consts, 1)
            nc.gpsimd.memset(pbd[:, :, :], 0.0).then_inc(consts, 1)

            def rstd_by_sums(n, links):
                gp.wait_ge(summed, n)
                if n > 1:
                    gp.wait_ge(normed, NT * (n - 1))
                nc.gpsimd.tensor_scalar(nmean[:, :], sums[:, :], -1.0 / D, None, ALU.mult).then_inc(mean_ready, 1)
                gp.wait_ge(squared, n)
                link(nc.gpsimd.tensor_scalar(tmp[:, :], sqs[:, :], 1.0 / D, EPS, ALU.mult, ALU.add))
                link(nc.gpsimd.tensor_tensor(rstd[:, :], tmp[:, :], half[:, :], ALU.pow))
                nc.gpsimd.tensor_tensor(nmr[:, :], nmean[:, :], rstd[:, :], ALU.mult).then_inc(rstd_ready, 3)

            def rstd_by_stats(n, g):
                t0_, tn = GROUPS[g]
                s_ = slice(t0_, t0_ + tn)
                gp.wait_ge(stats, 3 * (n - 3) + g + 1)
                gp.wait_ge(normed, NT * (n - 1))
                nc.gpsimd.tensor_scalar(nmean[:, s_], mv[:, s_, 0], -1.0, None, ALU.mult)
                link(nc.gpsimd.tensor_scalar(tmp[:, s_], mv[:, s_, 1], EPS, None, ALU.add))
                link(nc.gpsimd.tensor_tensor(rstd[:, s_], tmp[:, s_], half[:, s_], ALU.pow))
                nc.gpsimd.tensor_tensor(nmr[:, s_], nmean[:, s_], rstd[:, s_], ALU.mult).then_inc(rstd_ready, 1)

            rstd_by_sums(1, link)
            rstd_by_sums(2, link)
            gp.wait_ge(ld["bias"], 16 * 11)
            link(nc.gpsimd.tensor_scalar(gbb[:, :], gbb[:, :], alc[:, 0:1], None, ALU.mult))
            for t in range(NT):
                link(nc.gpsimd.tensor_tensor(acc[:, t, :], acc[:, t, :], xn[:, t, :], ALU.add))
                add_b = nc.gpsimd.tensor_tensor(acc[:, t, :], acc[:, t, :], gbb[:, :], ALU.add)
            add_b.then_inc(acc_pre, 1)
            gp.wait_ge(x_high, 1)
            nc.gpsimd.tensor_tensor(xl[:, :, :], xn[:, :, :], xh[:, :, :].bitcast(F32), ALU.subtract).then_inc(x_low, 1)
            filled(gp, ("agg", 2, C - 1))
            for t in range(NT):
                nc.gpsimd.tensor_tensor(xn[:, t, :], xl[:, t, :].bitcast(F32), xh[:, t, :].bitcast(F32),
                                        ALU.add).then_inc(x_whole, 1)
            gp.wait_ge(normed, 2 * NT)
            for t in range(NT):
                add_b = nc.gpsimd.tensor_tensor(xn[:, t, :], xn[:, t, :], bpb[:, :], ALU.add)
            add_b.then_inc(xnb_ready, 1)
            gp.wait_ge(w_high, 1)
            nc.gpsimd.tensor_tensor(w1l[:, :], w1s[:, :], w1h[:, :].bitcast(F32), ALU.subtract).then_inc(w_low, 1)
            evacuated(gp, ("gnn", NT - 1))
            for g in range(3):
                rstd_by_stats(3, g)
                for t in tiles(g):
                    evacuated(gp, ("proj", t))
                    link(nc.gpsimd.tensor_tensor(acc[:, t, :], acc[:, t, :], xn[:, t, :], ALU.add))
                    nc.gpsimd.tensor_tensor(acc[:, t, :], acc[:, t, :], b2b[:, :], ALU.add).then_inc(acc_x2, 1)
                if g == 1:
                    gp.wait_ge(w_high, 2)
                    nc.gpsimd.tensor_tensor(w2l[:, :], w2s[:, :], w2h[:, :].bitcast(F32),
                                            ALU.subtract).then_inc(w_low, 1)
            for g in range(3):
                rstd_by_stats(4, g)
            gp.wait_ge(slots_ready, 1)
            gp.wait_ge(ld["zero"], 16 * SLOT_TILES)
            gp.wait_ge(normed, 4 * NT)
            for t in range(NT):
                gp.indirect_dma_start(out=d_y, out_offset=bass.IndirectOffsetOnAxis(ap=posi[:, t:t + 1], axis=0),
                                      in_=hn[:, t, :], in_offset=None).then_inc(scattered, 16)
            for i in range(2):
                gp.wait_ge(st_o[i], 16 * ((SLOT_TILES + 1 - i) // 2))
            for t in range(NT):
                gp.indirect_dma_start(out=ys[0:T, t, :], out_offset=None, in_=d_o,
                                      in_offset=bass.IndirectOffsetOnAxis(ap=posi[:, t:t + 1], axis=0)
                                      ).then_inc(gathered[t], 16)

        @block.scalar
        def _(sc):
            def normalise(rows, to, n, g):
                sc.wait_ge(rstd_ready, 3 * (n - 1) + g + 1)
                for t in tiles(g):
                    nc.scalar.activation(to[:, t, :], rows[:, t, :], ACT.Identity, scale=rstd[:, t:t + 1],
                                         bias=nmr[:, t:t + 1]).then_inc(normed, 1)

            def square_rows(rows, to, n):
                sc.wait_ge(mean_ready, n)
                for t in range(NT):
                    ins = nc.scalar.activation(to[:, t, :], rows[:, t, :], ACT.Square, bias=nmean[:, t:t + 1],
                                               accum_out=sqs[:, t:t + 1])
                ins.then_inc(squared, 1)

            def sum_rows(rows, to, n):
                if n > 1:
                    sc.wait_ge(normed, NT * (n - 1))
                for t in range(NT):
                    ins = nc.scalar.activation(to[:, t, :], rows[:, t, :], ACT.Identity, accum_out=sums[:, t:t + 1])
                ins.then_inc(summed, 1)

            def counts_by_src(t):
                for j, (s0, sn) in enumerate(GROUPS):
                    bank = filled(sc, ("AT", t, j))
                    read_out(nc.scalar.copy(AT[:, s0:s0 + sn, t * T:(t + 1) * T],
                                            bank[0:T, 0:sn * T].rearrange("p (s d) -> p s d", d=T)), ("AT", t, j))

            sc.wait_ge(ld["x"], 16)
            sum_rows(acc, xn, 1)
            square_rows(acc, xn, 1)
            for t in range(NT):
                if t >= 2:
                    filled(sc, ("AT", t - 2, 2))
                for j, (c0, cn) in enumerate(CH):
                    bank = filled(sc, ("A", t, j))
                    read_out(nc.scalar.activation(arow[:, t % 2, c0:c0 + cn], bank[0:T, 0:cn], ACT.Identity,
                                                  accum_out=deg3[:, t, j:j + 1]), ("A", t, j))
                if t >= 1:
                    counts_by_src(t - 1)
                if t == 0:
                    for g in range(3):
                        normalise(acc, xn, 1, g)
                if t == 1:
                    sum_rows(xn, hn, 2)
                if t == 2:
                    square_rows(xn, hn, 2)
                if t == 3:
                    sc.wait_ge(squared, 2)
                    nc.scalar.copy(xh[:, :, :], xn[:, :, :]).then_inc(x_high, 1)
            counts_by_src(NT - 1)
            for k in range(C):
                bank = filled(sc, ("gWT", k))
                read_out(nc.scalar.copy(gwT[:, k, :], bank[:, :]), ("gWT", k))
            evacuated(sc, ("AT", NT - 1, 2))
            for n, (c0, cn) in enumerate(CH):
                for s in range(NT):
                    if n and s < NT - 1:
                        sc.wait_ge(at_used, (NT - 1) * (n - 1) + s + 1)
                    elif n:
                        filled(sc, ("agg", n - 1, C - 1))
                    nc.scalar.copy(ath[:, s, 0:cn], AT[:, s, c0:c0 + cn]).then_inc(at_high, 1)
            for g in range(3):
                sc.wait_ge(x_whole, tiles(g)[-1] + 1)
                normalise(xn, hn, 2, g)
            filled(sc, ("gnn", NT - 1))
            sc.wait_ge(ld["bias"], 16 * 11)
            for c in range(C):
                for j, (c0, cn) in enumerate(CH):
                    bank = filled(sc, ("hT", c, j))
                    read_out(nc.scalar.activation(hT[:, c, c0:c0 + cn], bank[:, 0:cn], ACT.Identity,
                                                  scale=g1c[:, c:c + 1], bias=be1c[:, c:c + 1]), ("hT", c, j))
            for p in range(PAIRS):
                if p:
                    filled(sc, ("qT", p - 1, NT - 1))
                for n, (c0, cn) in enumerate(CH):
                    for w in range(2):
                        bank = filled(sc, ("qk", p, n, w))
                        read_out(nc.scalar.activation(qkT[:, w, c0:c0 + cn], bank[:, 0:cn], ACT.Identity,
                                                      bias=bqkc[:, w * C + p:w * C + p + 1]), ("qk", p, n, w))
                for t in range(NT):
                    for w, name in enumerate(("kf", "qf")):
                        g = 2 * (p * NT + t) + w
                        bank = filled(sc, (name, p, t))
                        sc.wait_ge(max_ready, g + 1)
                        if t >= 2:
                            filled(sc, ("qT", p, t - 2))
                        elif p:
                            filled(sc, ("qT", p - 1, NT - 2 + t))
                        else:
                            filled(sc, ("A", NT - 1, 2))
                        for i in range(2):
                            e = nc.scalar.activation(ering[:, 2 * (t % 2) + w, i * NF:(i + 1) * NF],
                                                     bank[0:T, i * NF:(i + 1) * NF], ACT.Exp,
                                                     bias=nmax[:, g % 4, i:i + 1])
                            if i:
                                read_out(e, (name, p, t))
                if p:
                    sc.wait_ge(ld["den"], 16 * p)
                for i in range(2):
                    for n, (c0, cn) in enumerate(CH):
                        bank = filled(sc, ("att", p, i, n))
                        nc.scalar.copy(attT[DH * i:DH * i + DH, p, c0:c0 + cn], bank[0:DH, 0:cn])
                        read_out(nc.scalar.copy(den[0:1, i * N + c0:i * N + c0 + cn], bank[DH:DH + 1, 0:cn]),
                                 ("att", p, i, n))
            def second_rows(g):
                _, cn = CH[g]
                if g:
                    filled(sc, ("up", g - 1, MC - 1))
                for c in range(C):
                    bank = filled(sc, ("h2T", c, g))
                    nc.scalar.activation(h2h[:, c, 0:cn], bank[:, 0:cn], ACT.Identity, scale=g2c[:, c:c + 1],
                                         bias=be2c[:, c:c + 1])
                    read_out(nc.scalar.activation(h2f[:, c, 0:cn], bank[:, 0:cn], ACT.Identity,
                                                  scale=g2c[:, c:c + 1], bias=be2c[:, c:c + 1]), ("h2T", c, g))

            normalise(xn, hn, 3, 0)
            second_rows(0)
            normalise(xn, hn, 3, 1)
            normalise(xn, hn, 3, 2)
            for n, (c0, cn) in enumerate(CH):
                if n:
                    filled(sc, ("down", GROUPS[n][0] - 1))
                for m in range(MC):
                    bank = filled(sc, ("up", n, m))
                    read_out(nc.scalar.activation(gf[:, m, 0:cn], bank[:, 0:cn], ACT.Gelu,
                                                  bias=b1c[:, m:m + 1]), ("up", n, m))
                if n < 2:
                    second_rows(n + 1)
            for g in range(3):
                normalise(acc, hn, 4, g)
            for s in range(SLOT_TILES):
                bank = filled(sc, ("yT", s))
                if s >= 2:
                    filled(sc, ("ffn", s - 2))
                read_out(nc.scalar.copy(yT[:, s % 2, :], bank[:, :]), ("yT", s))

        @block.vector
        def _(ve):
            chain = [0]

            def link(ins):
                chain[0] += 1
                ins.then_inc(dve, 1)
                ve.wait_ge(dve, chain[0])

            def statistics(rows, g):
                for t in tiles(g):
                    ins = nc.vector.bn_stats(st[:, t, :], rows[:, t, :])
                link(ins)
                for t in tiles(g):
                    ins = nc.vector.bn_aggr(mv[:, t, :], st[:, t, :])
                ins.then_inc(stats, 1)

            nc.vector.memset(zb[:, :], 0.0).then_inc(zeros_ready, 1)
            ve.wait_ge(ld["edges"], 32)
            link(nc.vector.tensor_copy(edf[:, :, :], edi[:, :, :]))
            nc.vector.tensor_reduce(out=mm[:, 0:1], in_=edf[:, 0, :], op=ALU.min, axis=AX)
            link(nc.vector.tensor_reduce(out=mm[:, 1:2], in_=edf[:, 0, :], op=ALU.max, axis=AX))
            ve.wait_ge(consts, 1)
            nc.vector.tensor_scalar(mdiag[:, 0, :], ident[0:ER, 0:ER], mm[:, 0:1], None, ALU.mult)
            nc.vector.tensor_scalar(mdiag[:, 1, :], ident[0:ER, 0:ER], mm[:, 1:2], None,
                                    ALU.mult).then_inc(edge_tab, 1)
            bank = filled(ve, "edge_cols")
            cols = bank[0:T, 0:2 * EH * ER].rearrange("p (w b a) -> p w a b", w=2, b=EH)
            nc.vector.tensor_copy(dcol[:, :, :], cols[:, 0])
            read_out(nc.vector.tensor_copy(scol[:, :, :], cols[:, 1]), "edge_cols")
            bank = filled(ve, "edge_range")
            nc.vector.tensor_scalar(rrow[:, 0, :], bank[0:NT, 0:ER], t0[:, 1:2], None, ALU.is_le)
            read_out(nc.vector.tensor_scalar(rrow[:, 1, :], bank[0:NT, ER:2 * ER], t0[:, 0:1], None, ALU.is_ge),
                     "edge_range")
            evacuated(ve, "edge_range")
            link(nc.vector.tensor_tensor(rrow[:, 2, :], rrow[:, 0, :], rrow[:, 1, :], ALU.mult))
            nc.vector.tensor_tensor(rrow[:, 3, :], rrow[:, 2, :], arow_e[:, 0, :], ALU.mult)
            link(nc.vector.tensor_tensor(rrow[:, 4, :], rrow[:, 2, :], arow_e[:, 1, :], ALU.mult))
            nc.vector.reduce_max(rsm[:, 0:1], rrow[:, 3, :], AX)
            link(nc.vector.reduce_max(rsm[:, 1:2], rrow[:, 4, :], AX))
            link(nc.vector.tensor_scalar(rsm[:, 2:3], rsm[:, 1:2], -1.0, float(ER), ALU.mult, ALU.add))
            link(nc.vector.tensor_scalar(rsm[:, 3:4], rsm[:, 2:3], float(ER - 3), None, ALU.min))
            nc.vector.tensor_scalar(rsm[:, 4:5], rsm[:, 3:4], 2.0, None, ALU.add)
            link(nc.vector.tensor_scalar(rsm[:, 5:6], rsm[:, 0:1], -1.0, None, ALU.add))
            link(nc.vector.tensor_tensor(rsm[:, 6:7], rsm[:, 4:5], rsm[:, 5:6], ALU.max))
            nc.vector.tensor_copy(bounds[:, 0:1], rsm[:, 3:4])
            nc.vector.tensor_copy(bounds[:, 1:2], rsm[:, 6:7]).then_inc(bounds_ready, 1)
            ve.wait_ge(bounds_ready, 1)
            evacuated(ve, "edge_cols")
            turn = ve.alloc_register("dve_turn")
            ve.reg_mov(turn, 0)
            for t in range(NT):
                first = ve.value_load(bounds[t:t + 1, 0:1], min_val=0, max_val=ER - 3)
                last = ve.value_load(bounds[t:t + 1, 1:2], min_val=2, max_val=ER - 1)
                with ve.Fori(first, last + 1) as a:
                    ve.reg_add(turn, turn, 1)
                    for b in range(EH):
                        ve.wait_ge(oh_used[b], turn)
                        nc.vector.tensor_scalar(ohd[:, b, :], iota[:, 0:128], float(t * T),
                                                dcol[:, bass.ds(a, 1), b], ALU.add, ALU.is_equal)
                        nc.vector.tensor_scalar(ohs[:, b, :], iota[:, :], scol[:, bass.ds(a, 1), b], None,
                                                ALU.is_equal).then_inc(oh_ready[b], 1)
            def gnn_rows(t):
                bank = filled(ve, ("gnn", t))
                read_out(nc.vector.scalar_tensor_tensor(out=acc[:, t, :], in0=bank[0:T, :], scalar=coef[:, t:t + 1],
                                                        in1=acc[:, t, :], op0=ALU.mult, op1=ALU.add), ("gnn", t))

            evacuated(ve, ("A", NT - 1, 2))
            link(nc.vector.reduce_sum(deg[:, :], deg3[:, :, :], AX))
            link(nc.vector.tensor_scalar(deg[:, :], deg[:, :], 1.0, None, ALU.max))
            link(nc.vector.reciprocal(coef[:, :], deg[:, :]))
            ve.wait_ge(ld["bias"], 16 * 11)
            link(nc.vector.tensor_scalar(coef[:, :], coef[:, :], alc[:, 0:1], None, ALU.mult))
            ve.wait_ge(acc_pre, 1)

            def counts_rest(n):
                c0, cn = CH[n]
                for s in range(NT):
                    ve.wait_ge(at_high, n * NT + s + 1)
                    nc.vector.tensor_tensor(atl[:, s, c0:c0 + cn], AT[:, s, c0:c0 + cn],
                                            ath[:, s, 0:cn].bitcast(F32), ALU.subtract).then_inc(at_low, 1)

            counts_rest(0)
            for n, (c0, cn) in enumerate(CH):
                if n < 2:
                    counts_rest(n + 1)
                if n == 2:
                    filled(ve, ("gnn", GROUPS[1][0] - 1))
                filled(ve, ("gWT", C - 1))
                for c in range(C):
                    bank = filled(ve, ("agg", n, c))
                    read_out(nc.vector.tensor_copy(aggT[n % 2][:, c, 0:cn], bank[:, 0:cn]), ("agg", n, c))
                for t in (tiles(n - 1) if n else ()):
                    gnn_rows(t)
            for t in tiles(2):
                gnn_rows(t)
            nc.vector.memset(v65[:, :, :, DH:DH + 1], 1.0)
            for t in range(NT):
                bank = filled(ve, ("v", t))
                read_out(nc.vector.tensor_tensor(v65[:, t, :, 0:DH],
                                                 bank[0:T, :].rearrange("p (h e) -> p h e", e=DH),
                                                 bvb[:, :].rearrange("p (h e) -> p h e", e=DH), ALU.add), ("v", t))

            def reciprocals(p):
                ve.wait_ge(ld["dent"], 16 * (p + 1))
                nc.vector.reciprocal(zr[:, :], zt[:, :]).then_inc(z_ready, 1)

            def normalise_attention(p):
                ve.wait_ge(ld["zb"], 32 * (p + 1))
                nc.vector.tensor_tensor(attT[:, p, :], attT[:, p, :], zb[:, :], ALU.mult).then_inc(attn_ready, 1)

            def q_features_by_feature(p, t):
                bank = filled(ve, ("qT", p, t))
                read_out(nc.vector.tensor_copy(eqT[:, :, t * T:(t + 1) * T],
                                               bank[:, 0:2 * FC * T].rearrange("p (f t) -> p f t", t=T)), ("qT", p, t))

            for p in range(PAIRS):
                for t in range(NT):
                    for w, name in enumerate(("kf", "qf")):
                        g = 2 * (p * NT + t) + w
                        bank = filled(ve, (name, p, t))
                        if g >= 4:
                            q = g - 4
                            evacuated(ve, (("kf", "qf")[q % 2], q // 2 // NT, q // 2 % NT))
                        nc.vector.tensor_reduce(out=nmax[:, g % 4, :],
                                                in_=bank[0:T, :].rearrange("p (i f) -> p i f", i=2), op=ALU.max,
                                                axis=AX, negate=True).then_inc(max_ready, 1)
                    if t >= 1:
                        q_features_by_feature(p, t - 1)
                    if p and t == 4:
                        reciprocals(p - 1)
                    if p and t == NT - 1:
                        normalise_attention(p - 1)
                q_features_by_feature(p, NT - 1)
                for i in range(2):
                    bank = filled(ve, ("kv", p, i))
                    read_out(nc.vector.tensor_scalar(kvT[:, i, :], bank[0:DH + 1, 0:NF], kse[:, 0:1], None, ALU.add),
                             ("kv", p, i))
                bank = filled(ve, ("kvT", p))
                read_out(nc.vector.tensor_copy(kv[:, :, :],
                                               bank[:, 0:2 * FC * (DH + 1)].rearrange("p (f e) -> p f e", e=DH + 1)),
                         ("kvT", p))
            ve.wait_ge(ld["w1"], 16)
            nc.vector.tensor_copy(w1h[:, :], w1s[:, :]).then_inc(w_high, 1)
            reciprocals(PAIRS - 1)
            normalise_attention(PAIRS - 1)
            ve.wait_ge(xnb_ready, 1)
            for g in range(3):
                for t in tiles(g):
                    bank = filled(ve, ("proj", t))
                    read_out(nc.vector.tensor_tensor(xn[:, t, :], bank[0:T, :], xn[:, t, :], ALU.add), ("proj", t))
                evacuated(ve, ("proj", tiles(g)[-1]))
                statistics(xn, g)
            ve.wait_ge(ld["w2"], 16)
            nc.vector.tensor_copy(w2h[:, :], w2s[:, :]).then_inc(w_high, 1)

            def second_rest(g):
                _, cn = CH[g]
                for c in range(C):
                    evacuated(ve, ("h2T", c, g))
                    nc.vector.tensor_tensor(h2l[:, c, 0:cn], h2f[:, c, 0:cn], h2h[:, c, 0:cn].bitcast(F32),
                                            ALU.subtract).then_inc(h2_split, 1)

            second_rest(0)
            for n, (c0, cn) in enumerate(CH):
                for m in range(MC):
                    evacuated(ve, ("up", n, m))
                    link(nc.vector.tensor_copy(gh[:, m, 0:cn], gf[:, m, 0:cn]))
                    nc.vector.tensor_tensor(gl[:, m, 0:cn], gf[:, m, 0:cn], gh[:, m, 0:cn].bitcast(F32),
                                            ALU.subtract).then_inc(g_split, 1)
                if n < 2:
                    second_rest(n + 1)
                for t in tiles(n):
                    ve.wait_ge(acc_x2, t + 1)
                    bank = filled(ve, ("down", t))
                    read_out(nc.vector.tensor_tensor(acc[:, t, :], bank[0:T, :], acc[:, t, :], ALU.add),
                             ("down", t))
                evacuated(ve, ("down", tiles(n)[-1]))
                statistics(acc, n)
            ve.wait_ge(normed, 4 * NT)
            for j, edge in enumerate(BINS):
                ins = nc.vector.tensor_scalar(cmp[:, j, :], hn[:, :, 0], edge, None, ALU.is_gt)
            link(ins)
            link(nc.vector.reduce_sum(mem[:, :], cmp[:, :, :].rearrange("p j t -> p t j"), AX))
            nc.vector.tensor_tensor(boh[:, :, :], mem[:, :].unsqueeze(2).to_broadcast([T, NT, NB]),
                                    krow[:, :].unsqueeze(1).to_broadcast([T, NT, NB]), ALU.is_equal
                                    ).then_inc(boh_ready, 1)
            bank = filled(ve, "rank")
            link(nc.vector.tensor_copy(cnt[:, 0, :], bank[0:T, NT * NB:(NT + 1) * NB]))
            link(nc.vector.tensor_tensor(tl[:, :, :], cnt[:, 0, :].unsqueeze(1).to_broadcast([T, NT, NB]),
                                         many[:, :, :], ALU.is_gt))
            link(nc.vector.reduce_sum(cnt[:, 1, :], tl[:, :, :].rearrange("p j k -> p k j"), AX))
            link(nc.vector.tensor_tensor(below[:, :, :], cnt[:, 1, :].unsqueeze(1).to_broadcast([T, NB, NB]),
                                         lower[:, :, :], ALU.mult))
            link(nc.vector.reduce_sum(ctl[:, 0, 0:NB], below[:, :, :], AX))
            link(nc.vector.tensor_scalar(ctl[:, 1, 0:NB], ctl[:, 0, 0:NB], float(ST), None, ALU.mult))
            read_out(nc.vector.tensor_tensor(pr[:, :, :], bank[0:T, 0:NT * NB].rearrange("p (t k) -> p t k", k=NB),
                                             ctl[:, 1, 0:NB].unsqueeze(1).to_broadcast([T, NT, NB]), ALU.add), "rank")
            evacuated(ve, "rank")
            link(nc.vector.tensor_tensor(pr[:, :, :], pr[:, :, :], boh[:, :, :], ALU.mult))
            link(nc.vector.reduce_sum(posf[:, :], pr[:, :, :], AX))
            nc.vector.tensor_copy(posi[:, :], posf[:, :]).then_inc(slots_ready, 1)
            link(nc.vector.tensor_tensor(slotc[:, :, :], jrow[:, :].unsqueeze(1).to_broadcast([T, NB, SLOT_TILES]),
                                         ctl[:, 0, 0:NB].unsqueeze(2).to_broadcast([T, NB, SLOT_TILES]), ALU.is_ge))
            link(nc.vector.reduce_sum(exf[:, :], slotc[:, 1:NB, :].rearrange("p k j -> p j k"), AX))
            nc.vector.tensor_copy(exr[:, 0:SLOT_TILES], exf[:, :]).then_inc(slots_ready, 1)
            for s in range(SLOT_TILES):
                bank = filled(ve, ("ffn", s))
                if s >= 2:
                    ve.wait_ge(st_o[s % 2], 16 * (s // 2))
                read_out(nc.vector.tensor_copy(ob[:, s % 2, :], bank[:, :]), ("ffn", s))
            for t in range(NT):
                ve.wait_ge(gathered[t], 16)
                nc.vector.tensor_tensor(acc[:, t, :], acc[:, t, :], ys[0:T, t, :], ALU.add).then_inc(final, 1)

        @block.tensor
        def _(pe):
            def begin(key):
                _, bank, before = plan.order[key]
                if before:
                    pe.wait_ge(bank_read[bank], before)
                return P[bank]

            def product(out_, pairs):
                for n, (a, b) in enumerate(pairs):
                    ins = nc.tensor.matmul(out_, a, b, start=(n == 0), stop=(n == len(pairs) - 1))
                return ins

            def split_product(out_, high_low, start=True, stop=True):
                n = 3 * len(high_low)
                for i, (ah, al, bh, bl) in enumerate(high_low):
                    for j, (a, b) in enumerate(((ah, bh), (ah, bl), (al, bh))):
                        ins = nc.tensor.matmul(out_, a, b, start=(start and i + j == 0),
                                               stop=(stop and 3 * i + j == n - 1))
                return ins

            def transposes(key, blocks, rows, cols):
                bank = begin(key)
                for n, block_ in enumerate(blocks):
                    ins = nc.tensor.transpose(bank[0:cols, n * rows:(n + 1) * rows], block_, ident[0:rows, 0:rows])
                ins.then_inc(psum_filled, 1)

            pe.wait_ge(consts, 1)
            pe.wait_ge(edge_tab, 1)
            transposes("edge_cols", [edf[:, w, b * T:(b + 1) * T] for w in range(2) for b in range(EH)], ER, T)
            bank = begin("edge_range")
            product(bank[0:NT, 0:2 * ER], [(ones[0:ER, 0:NT], mdiag[:, :, :].rearrange("p w a -> p (w a)"))]
                    ).then_inc(psum_filled, 1)
            pe.wait_ge(bounds_ready, 1)
            first, last, turn, used = (pe.alloc_register(f"pe_{k}") for k in ("first", "last", "turn", "used"))
            pe.reg_mov(turn, 0)
            for b in range(EH):
                pe.sem_inc(oh_used[b], 1)

            def count_row(banks, start, stop):
                pe.reg_add(turn, turn, 1)
                for b in range(EH):
                    pe.wait_ge(oh_ready[b], turn)
                    for j, (c0, cn) in enumerate(CH):
                        ins = nc.tensor.matmul(banks[j][0:T, 0:cn], ohd[:, b, 0:T], ohs[:, b, c0:c0 + cn],
                                               start=start and b == 0, stop=stop and b == EH - 1)
                    ins.then_inc(oh_used[b], 1)

            for t in range(NT):
                banks = [begin(("A", t, j)) for j in range(3)]
                pe.reg_load(first, bounds[t:t + 1, 0:1])
                pe.reg_load(last, bounds[t:t + 1, 1:2])
                pe.reg_add(first, first, 1)
                count_row(banks, True, False)
                with pe.Fori(first, last) as _a:
                    count_row(banks, False, False)
                count_row(banks, False, True)
                pe.reg_add(used, turn, 1)
                pe.wait_ge(oh_used[EH - 1], used)
                pe.sem_inc(psum_filled, 3)
                if t >= 1:
                    for j, (s0, sn) in enumerate(GROUPS):
                        for jj in range(3):
                            evacuated(pe, ("A", t - 1, jj))
                        transposes(("AT", t - 1, j), [arow[:, (t - 1) % 2, s * T:(s + 1) * T]
                                                      for s in range(s0, s0 + sn)], T, T)
            for jj in range(3):
                evacuated(pe, ("A", NT - 1, jj))
            for j, (s0, sn) in enumerate(GROUPS):
                transposes(("AT", NT - 1, j), [arow[:, (NT - 1) % 2, s * T:(s + 1) * T]
                                               for s in range(s0, s0 + sn)], T, T)
            pe.wait_ge(ld["gw"], 16)
            for k in range(C):
                transposes(("gWT", k), [gws[:, o, k * 128:(k + 1) * 128] for o in range(C)], 128, 128)
            for j in range(3):
                for t in (NT - 2, NT - 1):
                    evacuated(pe, ("AT", t, j))
            pe.wait_ge(x_low, 1)
            for n in range(4):
                if n < 3:
                    c0, cn = CH[n]
                    banks = [begin(("agg", n, c)) for c in range(C)]
                    for s in range(NT):
                        pe.wait_ge(at_low, n * NT + s + 1)
                        low = atl[:, s, c0:c0 + cn]
                        for c in range(C):
                            k = slice(c * 128, (c + 1) * 128)
                            ins = split_product(banks[c][:, 0:cn], [(xh[:, s, k], xl[:, s, k], ath[:, s, 0:cn], low)],
                                                s == 0, s == NT - 1)
                            if s == NT - 1:
                                ins.then_inc(psum_filled, 1)
                        if s < NT - 1:
                            ins.then_inc(at_used, 1)
                if n == 0:
                    continue
                for k in range(C):
                    evacuated(pe, ("gWT", k))
                    evacuated(pe, ("agg", n - 1, k))
                for t in tiles(n - 1):
                    bank = begin(("gnn", t))
                    r0 = (t - GROUPS[n - 1][0]) * T
                    product(bank[0:T, :], [(aggT[(n - 1) % 2][:, c, r0:r0 + T], gwT[:, c, :]) for c in range(C)]
                            ).then_inc(psum_filled, 1)

            pe.wait_ge(normed, 2 * NT)
            for c in range(C):
                for j in range(3):
                    transposes(("hT", c, j), [hn[:, t, c * 128:(c + 1) * 128] for t in tiles(j)], T, 128)
            for j in range(3):
                for c in range(C):
                    evacuated(pe, ("hT", c, j))
            pe.wait_ge(ld["wv"], 16)
            for t in range(NT):
                bank = begin(("v", t))
                product(bank[0:T, :], [(hT[:, c, t * T:(t + 1) * T], wvs[:, c, :]) for c in range(C)]
                        ).then_inc(psum_filled, 1)
            pe.wait_ge(ld["wqk"], 16)
            pe.wait_ge(ld["pbd"], 32)
            for t in range(NT):
                evacuated(pe, ("v", t))
            for p in range(PAIRS):
                for n, (c0, cn) in enumerate(CH):
                    for w in range(2):
                        bank = begin(("qk", p, n, w))
                        q0 = w * D + p * 128
                        product(bank[:, 0:cn], [(wqk[:, c, q0:q0 + 128], hT[:, c, c0:c0 + cn]) for c in range(C)]
                                ).then_inc(psum_filled, 1)
                for n in range(3):
                    for w in range(2):
                        evacuated(pe, ("qk", p, n, w))
                kvb = [begin(("kv", p, i)) for i in range(2)]

                def sum_and_transpose(t):
                    evacuated(pe, ("kf", p, t))
                    for i in range(2):
                        ins = nc.tensor.matmul(kvb[i][0:DH + 1, 0:NF], v65[:, t, 2 * p + i, :],
                                               ering[:, 2 * (t % 2), i * NF:(i + 1) * NF],
                                               start=(t == 0), stop=(t == NT - 1))
                        if t == NT - 1:
                            ins.then_inc(psum_filled, 1)
                    evacuated(pe, ("qf", p, t))
                    transposes(("qT", p, t), [ering[:, 2 * (t % 2) + 1, f * 128:(f + 1) * 128]
                                              for f in range(2 * FC)], T, 128)

                for t in range(NT):
                    for w, name in ((1, "kf"), (0, "qf")):
                        bank = begin((name, p, t))
                        product(bank[0:T, :], [(qkT[:, w, t * T:(t + 1) * T],
                                                pbd[:, :, :].rearrange("p i f -> p (i f)"))]).then_inc(psum_filled, 1)
                    if t >= 1:
                        sum_and_transpose(t - 1)
                sum_and_transpose(NT - 1)
                for i in range(2):
                    evacuated(pe, ("kv", p, i))
                transposes(("kvT", p), [kvT[:, i, f * 128:(f + 1) * 128] for i in range(2) for f in range(FC)],
                           DH + 1, 128)
                evacuated(pe, ("kvT", p))
                evacuated(pe, ("qT", p, NT - 1))
                for i in range(2):
                    for n, (c0, cn) in enumerate(CH):
                        bank = begin(("att", p, i, n))
                        product(bank[0:DH + 1, 0:cn], [(kv[:, i * FC + f, :], eqT[:, i * FC + f, c0:c0 + cn])
                                                       for f in range(FC)]).then_inc(psum_filled, 1)
            pe.wait_ge(ld["wp"], 16)
            pe.wait_ge(attn_ready, PAIRS - 1)
            for t in range(8):
                bank = begin(("proj", t))
                for p in range(PAIRS - 1):
                    nc.tensor.matmul(bank[0:T, :], attT[:, p, t * T:(t + 1) * T], wps[:, p, :], start=(p == 0),
                                     stop=False)
            pe.wait_ge(attn_ready, PAIRS)
            for t in range(NT):
                bank = begin(("proj", t)) if t >= 8 else P[plan.order[("proj", t)][1]]
                for p in range(PAIRS if t >= 8 else 1):
                    p = p if t >= 8 else PAIRS - 1
                    ins = nc.tensor.matmul(bank[0:T, :], attT[:, p, t * T:(t + 1) * T], wps[:, p, :],
                                           start=(t >= 8 and p == 0), stop=(p == PAIRS - 1))
                ins.then_inc(psum_filled, 1)

            for n in range(4):
                if n < 3:
                    _, cn = CH[n]
                    pe.wait_ge(normed, 2 * NT + tiles(n)[-1] + 1)
                    for c in range(C):
                        transposes(("h2T", c, n), [hn[:, t, c * 128:(c + 1) * 128] for t in tiles(n)], T, 128)
                if n >= 1:
                    pe.wait_ge(w_low, 2)
                    pe.wait_ge(g_split, MC * n)
                    for t in tiles(n - 1):
                        r = slice((t - GROUPS[n - 1][0]) * T, (t - GROUPS[n - 1][0] + 1) * T)
                        bank = begin(("down", t))
                        split_product(bank[0:T, :], [(gh[:, m, r], gl[:, m, r], w2h[:, m * D:(m + 1) * D],
                                                      w2l[:, m * D:(m + 1) * D]) for m in range(MC)]
                                      ).then_inc(psum_filled, 1)
                if n < 3:
                    pe.wait_ge(w_low, 1)
                    pe.wait_ge(h2_split, C * (n + 1))
                    for m in range(MC):
                        bank = begin(("up", n, m))
                        w = [slice(c * M + m * 128, c * M + (m + 1) * 128) for c in range(C)]
                        split_product(bank[:, 0:cn], [(w1h[:, w[c]], w1l[:, w[c]], h2h[:, c, 0:cn], h2l[:, c, 0:cn])
                                                      for c in range(C)]).then_inc(psum_filled, 1)
            pe.wait_ge(boh_ready, 1)
            bank = begin("rank")
            all_bins = boh[:, :, :].rearrange("p t k -> p (t k)")
            nc.tensor.matmul(bank[0:T, 0:NT * NB], trib[:, 0:T], all_bins, start=True, stop=False)
            for t in range(NT - 1):
                nc.tensor.matmul(bank[0:T, (t + 1) * NB:NT * NB], onesb[:, 0:T],
                                 boh[:, t:t + 1, :].to_broadcast([T, NT - 1 - t, NB]), start=False,
                                 stop=(t == NT - 2))
            for t in range(NT):
                ins = nc.tensor.matmul(bank[0:T, NT * NB:(NT + 1) * NB], onesb[:, 0:T], boh[:, t, :],
                                       start=(t == 0), stop=(t == NT - 1))
            ins.then_inc(psum_filled, 1)
            pe.wait_ge(slots_ready, 2)
            pe.wait_ge(ld["fw"], 16 * (NB - 1))
            expert = pe.alloc_register("pe_expert")
            for s in range(SLOT_TILES + 1):
                if s < SLOT_TILES:
                    pe.wait_ge(ld_ys[s], 16)
                    transposes(("yT", s), [ys[:, s, c * 128:(c + 1) * 128] for c in range(C)], ST, 128)
                if s == 0:
                    continue
                s -= 1
                evacuated(pe, ("yT", s))
                pe.reg_load(expert, exr[0:1, s:s + 1])
                e = pe.snap(expert, min_val=0, max_val=NB - 1)
                bank = begin(("ffn", s))
                product(bank[:, :], [(yT[:, s % 2, c * ST:(c + 1) * ST], fw[:, bass.ds((e * C + c) * D, D)])
                                     for c in range(C)]).then_inc(psum_filled, 1)


_INS = ['x', 'src', 'dst', 'L0_gnn_alpha', 'L0_gnn_W', 'L0_gnn_b', 'L0_mix_Wqkv', 'L0_mix_bqkv', 'L0_mix_Pmat',
        'L0_mix_Wproj', 'L0_mix_bproj', 'L0_mix_W1', 'L0_mix_b1', 'L0_mix_W2', 'L0_mix_b2', 'L0_mix_g1', 'L0_mix_be1',
        'L0_mix_g2', 'L0_mix_be2', 'L0_ffn_W']


def kernel(**inputs):
    import numpy as np
    import concourse.bacc as bacc
    from concourse.bass_utils import run_bass_kernel_spmd

    nc = bacc.Bacc("TRN2", target_bir_lowering=False, num_devices=1)
    arrays, args = {}, []
    for name in _INS:
        a = np.ascontiguousarray(inputs[name])
        if a.ndim == 0:
            a = a.reshape(1)
        arrays["in_" + name] = a
        args.append(nc.dram_tensor("in_" + name, a.shape, mybir.dt.from_np(a.dtype), kind="ExternalInput").ap())
    out = nc.dram_tensor("out", arrays["in_x"].shape, F32, kind="ExternalOutput").ap()
    build(nc, *args, out)
    r = run_bass_kernel_spmd(nc, [arrays], core_ids=[0])
    return r.results[0]["out"]
```

```python
from contextlib import ExitStack, nullcontext

import concourse.bass as bass
from concourse import mybir

F32 = mybir.dt.float32
F16 = mybir.dt.float16
BF16 = mybir.dt.bfloat16
I32 = mybir.dt.int32
F32R = mybir.dt.float32r
ALU = mybir.AluOpType
ACT = mybir.ActivationFunctionType
AX = mybir.AxisListType.X

EPS = 1e-5
KSUM_EPS = 1e-6
BINS = [-1.5, -1.0, -0.5, 0.0, 0.5, 1.0, 1.5]


def up(n):
    return (n + 31) // 32 * 32


def row_broadcast(row, n):
    return bass.AP(tensor=row.tensor, offset=row.offset, ap=[[0, n]] + [list(d) for d in row.ap])


class PsumPlan:

    def __init__(self):
        self.order, self.uses, self.next = {}, [0] * 8, 0

    def add(self, key, banks=tuple(range(8))):
        while self.next % 8 not in banks:
            self.next += 1
        b = self.next % 8
        self.next += 1
        self.order[key] = (len(self.order), b, self.uses[b])
        self.uses[b] += 1


def build(nc, x, src, dst, alpha, gW, gb, Wqkv, bqkv, Pm, Wp, bp, W1, b1, W2, b2, g1, be1, g2, be2, FW, out):
    N, D = x.shape
    E = src.shape[0]
    T = 125
    NT = N // T
    EH = 4
    ER = E // (EH * T)
    C = D // 128
    DH, NF = Pm.shape
    H = D // DH
    PAIRS = H // 2
    M = W1.shape[1]
    MC = M // 128
    NB = len(BINS) + 1
    ST = 128
    SLOT_TILES = (N + NB * (ST - 1)) // ST
    SURE_TILES = (N + ST - 1) // ST
    GROUPS = [(0, 4), (4, 4), (8, 2)]
    CH = [(t * T, n * T) for t, n in GROUPS]
    NW = N + 2
    assert N == NT * T and E == ER * EH * T and DH == 64 and NF == 256 and CH[-1][0] + CH[-1][1] == N
    FC = NF // 128
    MAX_ROWS = 4096 // (EH * T)

    def tiles(g):
        return range(GROUPS[g][0], GROUPS[g][0] + GROUPS[g][1])

    plan = PsumPlan()
    plan.add("edge_cols")
    plan.add("edge_range")
    for t in range(NT + 1):
        if t < NT:
            for j in range(3):
                plan.add(("A", t, j))
        if t >= 1:
            for j in range(3):
                plan.add(("AT", t - 1, j))
    for k in range(C):
        plan.add(("gWT", k))
    for n in range(4):
        if n < 3:
            for c in range(C):
                plan.add(("agg", n, c))
        if n >= 1:
            for t in tiles(n - 1):
                plan.add(("gnn", t))
    for j in range(3):
        for c in range(C):
            plan.add(("hT", c, j))
    for t in range(NT):
        plan.add(("v", t))
    work = (0, 1, 2, 3, 4, 5)
    qk_groups = [(n, w) for n in range(3) for w in range(2)]
    for n, w in qk_groups:
        plan.add(("qk", 0, n, w), work)
    for p in range(PAIRS):
        for t in range(NT):
            plan.add(("kf", p, t), work)
            plan.add(("qf", p, t), work)
            if t >= 1:
                plan.add(("qT", p, t - 1), work)
        for i in range(2):
            plan.add(("kv", p, i), (6 + i,))
        plan.add(("qT", p, NT - 1), work)
        for n, w in (qk_groups if p < PAIRS - 1 else ()):
            plan.add(("qk", p + 1, n, w), work)
        plan.add(("kvT", p), work)
        for i in range(2):
            for n in range(3):
                plan.add(("att", p, i, n), work)
    for t in range(NT):
        plan.add(("proj", t))
    for n in range(4):
        if n < 3:
            for c in range(C):
                plan.add(("h2T", c, n))
        if n >= 1:
            for t in tiles(n - 1):
                plan.add(("down", t))
        if n < 3:
            for m in range(MC):
                plan.add(("up", n, m))
    plan.add("rank")
    for s in range(SLOT_TILES + 1):
        if s < SLOT_TILES:
            plan.add(("yT", s))
        if s >= 1:
            plan.add(("ffn", s - 1))

    base = 16512
    top = [base]

    def at(name, shape, dtype, offset):
        return nc.alloc_sbuf_tensor_at(name, shape, dtype, offset=offset)

    def place(size):
        o = top[0]
        top[0] += (size + 31) // 32 * 32
        return o

    o_xn = place(NT * D * 4)
    o_x = place(up(NT * D * 4))
    o_hT = place(C * N * 4)
    o_v = place(21120)
    o_qk = place(2 * N * 4)
    o_att = place(PAIRS * N * 4)
    o_den = place(2 * N * 4)
    o_q = place(2 * N * 4)
    o_kv = place(2 * NF * 4 + 4 * 65 * 4)
    o_hn = place(NT * D * 4)
    o_acc = place(NT * D * 4)
    o_ring = place(max(4 * 2 * NF * 4, EH * (up(2 * NW) + 256)))

    xn = at("xn", [T, NT, D], F32, o_xn)
    wqk = at("wqk", [128, C, 2 * D], F32, o_x)
    wqkl = at("wqkl", [128, C, 2 * D], F32R, o_x)
    wqkh = at("wqkh", [128, C, 2 * D], F32R, o_acc)
    o_w = o_x
    w1s = at("w1s", [128, C * M], F32, o_w)
    w1l = at("w1l", [128, C * M], F32R, o_w)
    w1h = at("w1h", [128, C * M], F32R, o_w + C * M * 4)
    w2s = at("w2s", [128, MC * D], F32, o_w + 2 * C * M * 4)
    w2l = at("w2l", [128, MC * D], F32R, o_w + 2 * C * M * 4)
    w2h = at("w2h", [128, MC * D], F32R, o_w + 3 * C * M * 4)
    hTh = at("hTh", [128, C, N], F32R, o_hT)
    hTf = at("hTf", [128, C, N], F32, o_xn)
    hTl = at("hTl", [128, C, N], F32R, o_xn)
    v65 = at("v65", [T, NT, H, DH + 1], F32, o_v)
    qkT = [at("qT2", [128, 2, N], F32R, o_q), at("kT2", [128, 2, N], F32R, o_qk)]
    attT = at("attT", [128, PAIRS, N], F32, o_att)
    wps = at("wps", [128, C, D], F32, o_qk)
    wvs = at("wvs", [128, C, D], F32, o_q)
    wvl = at("wvl", [128, C, D], F32R, o_q)
    wvh = at("wvh", [128, C, D], F32R, o_ring)
    den = at("den", [1, 2 * N], F32, o_den)
    kvT = at("kvT", [DH + 1, 2, NF], F32, o_kv)
    kv = at("kv", [128, 2 * FC, DH + 1], F32, o_kv + 2 * NF * 4)
    hn = at("hn", [T, NT, D], F32, o_hn)
    eqT = at("eqT", [128, 2 * FC, N], F32, o_hn)
    acc = at("acc", [T, NT, D], F32, o_acc)
    ering = at("ering", [T, 4, 2 * NF], F32, o_ring)
    ohs = at("ohs", [T, EH, NW], BF16, o_ring)
    ohd = at("ohd", [T, EH, 128], BF16, o_ring + up(EH * NW * 2))
    xh = at("xh", [T, NT, D], F32R, o_hn)
    xl = at("xl", [T, NT, D], F32R, o_xn)
    ath = at("ath", [T, NT, CH[0][1]], F32R, o_x)
    atl = at("atl", [T, NT, N], F32R, o_hT)
    AT = at("AT", [T, NT, N], F32, o_hT)
    arow = at("arow", [T, 2, N], F32, o_hT + up(NT * N * 4))
    o_gw = o_hT + up(NT * N * 4) + up(2 * N * 4)
    gws = at("gws", [128, C, D], F32, o_gw)
    gwT = at("gwT", [128, C, D], F32, o_gw + C * D * 4)
    assert o_gw + 2 * C * D * 4 <= o_q
    aggT = [at("aggT0", [128, C, CH[0][1]], F32, o_gw),
            at("aggT1", [128, C, CH[0][1]], F32, o_hT + up(NT * N * 4))]
    W_END = o_w + 4 * C * M * 4
    GC = CH[0][1]
    gf = at("gf", [128, MC, GC], F32, up(W_END))
    gl = at("gl", [128, MC, GC], F32R, up(W_END))
    gh = at("gh", [128, MC, GC], F32R, up(W_END) + MC * GC * 4)
    h2h = at("h2h", [128, C, GC], F32R, up(W_END) + 2 * MC * GC * 4)
    h2f = at("h2f", [128, C, GC], F32, o_ring)
    h2l = at("h2l", [128, C, GC], F32R, o_ring)
    assert W_END > o_qk and up(W_END) + (2 * MC + C) * GC * 4 <= o_hn
    fw = at("fw", [128, NB * C * D], F32, o_xn)
    ys = at("ys", [ST, SLOT_TILES, D], F32, o_qk)
    yT = at("yT", [128, 2, C * ST], F32, o_qk + SLOT_TILES * D * 4)
    ob = at("ob", [ST, 2, D], F32, o_qk + (SLOT_TILES + 2) * D * 4)
    assert o_qk + (SLOT_TILES + 4) * D * 4 <= o_hn

    def small(name, shape, dtype):
        size = 2 if dtype in (F16, BF16) else 4
        for n in shape[1:]:
            size *= n
        return at(name, shape, dtype, place(size))

    ident = small("ident", [128, 128], F32)
    ones = small("ones", [128, 128], F32)
    iota = small("iota", [T, NW], F16)
    dcol = small("dcol", [T, ER, EH], F32)
    scol = small("scol", [T, ER, EH], F32)
    o_p = top[0]
    pms = small("pms", [128, NF], F32)
    pml = at("pml", [128, NF], F32R, o_p)
    pmh = small("pmh", [128, NF], F32R)
    gbb = small("gbb", [T, D], F32)
    bvb = small("bvb", [T, D], F32)
    bpb = small("bpb", [T, D], F32)
    b2b = small("b2b", [T, D], F32)
    zb = small("zb", [128, N], F32)
    zt = small("zt", [T, 2 * NT], F32)
    zr = small("zr", [T, 2 * NT], F32)
    g1c = small("g1c", [128, C], F32)
    be1c = small("be1c", [128, C], F32)
    g2c = small("g2c", [128, C], F32)
    be2c = small("be2c", [128, C], F32)
    bqkc = small("bqkc", [128, 2 * C], F32)
    b1c = small("b1c", [128, MC], F32)
    alc = small("alc", [T, 1], F32)
    st = small("st", [T, NT, 6], F32)
    mv = small("mv", [T, NT, 2], F32)
    kse = small("kse", [DH + 1, 1], F32)
    half = small("half", [T, NT], F32)
    rstd = small("rstd", [T, NT], F32)
    nmr = small("nmr", [T, NT], F32)
    tmp = small("tmp", [T, NT], F32)
    sums = small("sums", [T, NT], F32)
    sqs = small("sqs", [T, NT], F32)
    nmean = small("nmean", [T, NT], F32)
    deg3 = small("deg3", [T, NT, 3], F32)
    deg = small("deg", [T, NT], F32)
    coef = small("coef", [T, NT], F32)
    bounds = small("bounds", [NT, 2], I32)
    nmax = small("nmax", [T, 4, 2], F32)
    posi = small("posi", [T, NT], I32)
    exr = small("exr", [T, SLOT_TILES + 1], I32)
    edi = at("edi", [ER, 2, EH * T], I32, o_x)
    edf = at("edf", [ER, 2, EH * T], F32, o_x + up(2 * EH * T * 4))
    mm = at("mm", [ER, 2], F32, o_x + 8064)
    mdiag = at("mdiag", [ER, 2, ER], F32, o_x + 8096)
    rrow = at("rrow", [NT, 8, ER], F32, o_x + 9440)
    rsm = at("rsm", [NT, 8], F32, o_x + 14592)
    arow_e = at("arow_e", [NT, 2, ER], F32, o_x + 14624)
    t0 = at("t0", [NT, 2], F32, o_x + 15296)
    mem = at("mem", [T, NT], F32, o_ring)
    cmp = at("cmp", [T, len(BINS), NT], F32, o_ring + 64)
    boh = at("boh", [T, NT, NB], BF16, o_ring + 384)
    cnt = at("cnt", [T, 2, NB], F32, o_ring + 704)
    below = at("below", [T, NB, NB], F32, o_ring + 1376)
    tl = at("tl", [T, NT, NB], F32, o_ring + 1760)
    ctl = at("ctl", [T, 2, NB + 1], F32, o_ring + 2112)
    pr = at("pr", [T, NT, NB], F32, o_ring + 2208)
    posf = at("posf", [T, NT], F32, o_ring + 2560)
    slotc = at("slotc", [T, NB, SLOT_TILES], F32, o_ring + 2624)
    exf = at("exf", [T, SLOT_TILES + 1], F32, o_ring + 3200)
    jrow = small("jrow", [T, SLOT_TILES], F32)
    krow = small("krow", [T, NB], F32)
    lower = small("lower", [T, NB, NB], F32)
    many = small("many", [T, NT, NB], F32)
    trib = small("trib", [T, 128], BF16)
    onesb = small("onesb", [T, 128], BF16)
    assert top[0] <= nc.sbuf_usable_end, (top[0], nc.sbuf_usable_end)

    d_xn = nc.dram_tensor("xn_kept", (T, NT * D), F32, kind="Internal").ap()
    d_acc = nc.dram_tensor("acc_kept", (T, NT * D), F32, kind="Internal").ap()
    d_den = nc.dram_tensor("den_scratch", (PAIRS, 2 * N), F32, kind="Internal").ap()
    d_z = nc.dram_tensor("z_scratch", (PAIRS, 2 * N), F32, kind="Internal").ap()
    d_y = nc.dram_tensor("y_sorted", (SLOT_TILES * ST, D), F32, kind="Internal").ap()
    d_o = nc.dram_tensor("o_sorted", (SLOT_TILES * ST, D), F32, kind="Internal").ap()

    with ExitStack() as ctx:
        P = [ctx.enter_context(nc.psum_tensor(f"bank{i}", [128, 512], F32)) for i in range(8)]

        def sem(name):
            return ctx.enter_context(nc.semaphore(name))

        psum_filled = sem("psum_filled")
        ffn_filled = {k: sem(k + "_filled") for k in ("yT", "ffn")}
        bank_read = [sem(f"bank_read{i}") for i in range(8)]
        ld = {k: sem("ld_" + k) for k in ("edges", "x", "gw", "bias", "pm", "wqk", "wv", "wp", "w1", "w2", "fw",
                                          "xn_out", "acc_out", "xn", "acc", "den", "dent", "z", "zb", "zero", "out")}
        gathered = [sem(f"gathered{i}") for i in range(NT)]
        ld_ys = [sem(f"ld_ys{i}") for i in range(SLOT_TILES)]
        st_o = [sem(f"st_o{i}") for i in range(2)]
        scattered = sem("scattered")
        consts = sem("consts")
        zeros_ready = sem("zeros_ready")
        edge_tab = sem("edge_tab")
        bounds_ready = sem("bounds_ready")
        oh_ready = [sem(f"oh_ready{b}") for b in range(EH)]
        oh_used = [sem(f"oh_used{b}") for b in range(EH)]
        dve = sem("dve")
        pool = sem("pool")
        stats = sem("stats")
        rstd_ready = sem("rstd_ready")
        normed = sem("normed")
        acc_pre = sem("acc_pre")
        x_high = sem("x_high")
        x_low = sem("x_low")
        x_whole = sem("x_whole")
        at_high = sem("at_high")
        at_low = sem("at_low")
        at_used = sem("at_used")
        xnb_ready = sem("xnb_ready")
        max_ready = sem("max_ready")
        e_ready = [sem("ek_ready"), sem("eq_ready")]
        z_ready = sem("z_ready")
        attn_ready = sem("attn_ready")
        acc_x2 = sem("acc_x2")
        summed = sem("summed")
        squared = sem("squared")
        mean_ready = sem("mean_ready")
        act = sem("act")
        p_split = sem("p_split")
        wv_split = sem("wv_split")
        wqk_split = sem("wqk_split")
        h_split = sem("h_split")
        q_high = sem("q_high")
        w_high = sem("w_high")
        w_low = sem("w_low")
        h2_split = sem("h2_split")
        g_split = sem("g_split")
        boh_ready = sem("boh_ready")
        slots_ready = sem("slots_ready")
        final = sem("final")
        block = ctx.enter_context(nc.Block())

        def filled(eng, key):
            place_, bank, _ = plan.order[key]
            if key[0] in ffn_filled:
                eng.wait_ge(ffn_filled[key[0]], key[1] + 1)
            else:
                eng.wait_ge(psum_filled, place_ + 1)
            return P[bank]

        def slot_tiles(eng):
            eng.wait_ge(slots_ready, 2)
            return eng.value_load(exr[0:1, SLOT_TILES:SLOT_TILES + 1], min_val=SURE_TILES, max_val=SLOT_TILES)

        def if_used(eng, s, used):
            return eng.If(used > s) if s >= SURE_TILES else nullcontext()

        def read_out(ins, key):
            ins.then_inc(bank_read[plan.order[key][1]], 1)

        def evacuated(eng, key):
            _, bank, before = plan.order[key]
            eng.wait_ge(bank_read[bank], before + 1)

        @block.sync
        def _(sp):
            sp.dma_start(edi[:, 0, :], dst.rearrange("(a e) -> a e", a=ER)).then_inc(ld["edges"], 16)
            sp.dma_start(edi[:, 1, :], src.rearrange("(a e) -> a e", a=ER)).then_inc(ld["edges"], 16)
            sp.dma_start(acc[:, :, :], x.rearrange("(t p) d -> p t d", p=T)).then_inc(ld["x"], 16)
            sp.dma_start(alc[:, :], row_broadcast(alpha, T)).then_inc(ld["bias"], 16)
            for tile, row in ((gbb, gb), (bvb, bqkv[2 * D:3 * D]), (bpb, bp), (b2b, b2)):
                sp.dma_start(tile[:, :], row_broadcast(row, T)).then_inc(ld["bias"], 16)
            for tile, row in ((g1c, g1), (be1c, be1), (g2c, g2), (be2c, be2), (bqkc, bqkv[0:2 * D]), (b1c, b1)):
                sp.dma_start(tile[:, :], row.rearrange("(c p) -> p c", p=128),
                             allow_slow_non_contiguous=True).then_inc(ld["bias"], 16)
            sp.dma_start(gws[:, :, :], gW.rearrange("(c p) d -> p c d", p=128)).then_inc(ld["gw"], 16)
            for i in range(2):
                sp.dma_start(pms[DH * i:DH * i + DH, :], Pm).then_inc(ld["pm"], 16)
            sp.dma_start(wvs[:, :, :], Wqkv[:, 2 * D:3 * D].rearrange("(c p) n -> p c n", p=128)).then_inc(ld["wv"], 16)
            sp.wait_ge(zeros_ready, 1)
            for s in range(SLOT_TILES):
                sp.dma_start(d_y[s * ST:(s + 1) * ST, :], zb[:, 0:D]).then_inc(ld["zero"], 16)
            for s in range(SURE_TILES, SLOT_TILES):
                sp.dma_start(d_o[s * ST:(s + 1) * ST, :], zb[:, 0:D]).then_inc(ld["zero"], 16)
            filled(sp, ("agg", 2, C - 1))
            sp.dma_start(wqk[:, :, :], Wqkv[:, 0:2 * D].rearrange("(c p) n -> p c n", p=128)).then_inc(ld["wqk"], 16)
            sp.wait_ge(x_whole, NT)
            sp.dma_start(d_xn, xn[:, :, :].rearrange("p t d -> p (t d)")).then_inc(ld["xn_out"], 16)
            evacuated(sp, ("gnn", NT - 1))
            sp.dma_start(d_acc, acc[:, :, :].rearrange("p t d -> p (t d)")).then_inc(ld["acc_out"], 16)
            for p in range(PAIRS):
                if p == PAIRS - 2:
                    filled(sp, ("qk", p + 1, 2, 1))
                    sp.dma_start(xn[:, :, :].rearrange("p t d -> p (t d)"), d_xn).then_inc(ld["xn"], 16)
                    sp.dma_start(acc[:, :, :].rearrange("p t d -> p (t d)"), d_acc).then_inc(ld["acc"], 16)
                if p == PAIRS - 1:
                    filled(sp, ("kv", p, 1))
                    sp.dma_start(wps[:, :, :], Wp.rearrange("(c p) n -> p c n", p=128)).then_inc(ld["wp"], 16)
                if p == PAIRS - 2:
                    sp.dma_start(w1s[:, :].rearrange("p (c n) -> p c n", n=M),
                                 W1.rearrange("(c p) n -> p c n", p=128)).then_inc(ld["w1"], 16)
                evacuated(sp, ("att", p, 1, 2))
                sp.dma_start(d_den[p:p + 1, :], den[0:1, :]).then_inc(ld["den"], 16)
                sp.wait_ge(ld["den"], 16 * (p + 1))
                sp.dma_start(zt[:, :], d_den[p, :].rearrange("(q j) -> q j", q=T)).then_inc(ld["dent"], 16)
                sp.wait_ge(z_ready, p + 1)
                sp.dma_start(d_z[p, :].rearrange("(q j) -> q j", q=T), zr[:, :]).then_inc(ld["z"], 16)
                sp.wait_ge(ld["z"], 16 * (p + 1))
                if p:
                    sp.wait_ge(attn_ready, p)
                for i in range(2):
                    sp.dma_start(zb[DH * i:DH * i + DH, :],
                                 row_broadcast(d_z[p, i * N:(i + 1) * N], DH)).then_inc(ld["zb"], 16)
            sp.dma_start(w2s[:, :].rearrange("p (c n) -> p c n", n=D),
                         W2.rearrange("(c p) n -> p c n", p=128)).then_inc(ld["w2"], 16)
            sp.wait_ge(acc_x2, NT)
            sp.wait_ge(normed, 3 * NT)
            fwv = FW.rearrange("k (c p) n -> p (k c) n", p=128)
            fws = fw[:, :].rearrange("p (k n) -> p k n", n=D)
            sp.dma_start(fws[:, 0:2 * C, :], fwv[:, 0:2 * C, :]).then_inc(ld["fw"], 16)
            filled(sp, ("up", 2, MC - 1))
            for k in range(2, NB):
                if k == 6:
                    filled(sp, ("down", NT - 1))
                sp.dma_start(fws[:, k * C:(k + 1) * C, :], fwv[:, k * C:(k + 1) * C, :]).then_inc(ld["fw"], 16)
            sp.wait_ge(scattered, 16 * NT)
            used = slot_tiles(sp)
            for s in range(SLOT_TILES):
                with if_used(sp, s, used):
                    sp.dma_start(ys[:, s, :], d_y[s * ST:(s + 1) * ST, :]).then_inc(ld_ys[s], 16)
            for s in range(SLOT_TILES):
                with if_used(sp, s, used):
                    evacuated(sp, ("ffn", s))
                    sp.dma_start(d_o[s * ST:(s + 1) * ST, :], ob[:, s % 2, :]).then_inc(st_o[s % 2], 16)
            for t in range(NT):
                sp.wait_ge(final, t + 1)
                sp.dma_start(out[t * T:(t + 1) * T, :], acc[:, t, :]).then_inc(ld["out"], 16)
            sp.wait_ge(ld["out"], 16 * NT)

        @block.gpsimd
        def _(gp):
            chain = [0]

            def link(ins):
                chain[0] += 1
                ins.then_inc(pool, 1)
                gp.wait_ge(pool, chain[0])

            nc.gpsimd.memset(ident[:, :], 0.0)
            nc.gpsimd.memset(onesb[:, :], 1.0)
            nc.gpsimd.memset(lower[:, :, :], 1.0)
            link(nc.gpsimd.memset(trib[:, :], 0.0))
            nc.gpsimd.affine_select(out=ident[:, :], in_=ident[:, :], compare_op=ALU.not_equal, fill=1.0, base=0,
                                    pattern=[[-1, 128]], channel_multiplier=1)
            nc.gpsimd.affine_select(out=trib[:, :], in_=trib[:, :], compare_op=ALU.is_ge, fill=1.0, base=0,
                                    pattern=[[-1, 128]], channel_multiplier=1)
            nc.gpsimd.affine_select(out=lower[:, :, :], in_=lower[:, :, :], compare_op=ALU.is_gt, fill=0.0, base=0,
                                    pattern=[[1, NB], [-1, NB]], channel_multiplier=0)
            nc.gpsimd.memset(ones[:, :], 1.0)
            small_ok = {"allow_small_or_imprecise_dtypes": True}
            nc.gpsimd.iota(krow[:, :], pattern=[[1, NB]], base=0, channel_multiplier=0, **small_ok)
            nc.gpsimd.iota(many[:, :, :], pattern=[[ST, NT], [0, NB]], base=0, channel_multiplier=0, **small_ok)
            nc.gpsimd.iota(iota[:, :], pattern=[[1, NW]], base=0, channel_multiplier=0, **small_ok)
            nc.gpsimd.iota(jrow[:, :], pattern=[[1, SLOT_TILES]], base=0, channel_multiplier=0, **small_ok)
            nc.gpsimd.iota(arow_e[:, 0, :], pattern=[[1, ER]], base=1, channel_multiplier=0, **small_ok)
            nc.gpsimd.iota(arow_e[:, 1, :], pattern=[[-1, ER]], base=ER, channel_multiplier=0, **small_ok)
            nc.gpsimd.iota(t0[:, 0:1], pattern=[[1, 1]], base=0, channel_multiplier=T, **small_ok)
            nc.gpsimd.iota(t0[:, 1:2], pattern=[[1, 1]], base=T - 1, channel_multiplier=T, **small_ok)
            link(nc.gpsimd.memset(kse[:, :], 0.0))
            link(nc.gpsimd.memset(kse[DH:DH + 1, :], NF * KSUM_EPS / 16))
            nc.gpsimd.memset(half[:, :], -0.5).then_inc(consts, 1)

            def rstd_by_sums(n, links):
                gp.wait_ge(summed, n)
                if n > 1:
                    gp.wait_ge(normed, NT * (n - 1))
                nc.gpsimd.tensor_scalar(nmean[:, :], sums[:, :], -1.0 / D, None, ALU.mult).then_inc(mean_ready, 1)
                gp.wait_ge(squared, n)
                link(nc.gpsimd.tensor_scalar(tmp[:, :], sqs[:, :], 1.0 / D, EPS, ALU.mult, ALU.add))
                link(nc.gpsimd.tensor_tensor(rstd[:, :], tmp[:, :], half[:, :], ALU.pow))
                nc.gpsimd.tensor_tensor(nmr[:, :], nmean[:, :], rstd[:, :], ALU.mult).then_inc(rstd_ready, 3)

            def rstd_by_stats(n, g):
                t0_, tn = GROUPS[g]
                s_ = slice(t0_, t0_ + tn)
                gp.wait_ge(stats, 3 * (n - 3) + g + 1)
                gp.wait_ge(normed, NT * (n - 1))
                nc.gpsimd.tensor_scalar(nmean[:, s_], mv[:, s_, 0], -1.0, None, ALU.mult)
                link(nc.gpsimd.tensor_scalar(tmp[:, s_], mv[:, s_, 1], EPS, None, ALU.add))
                link(nc.gpsimd.tensor_tensor(rstd[:, s_], tmp[:, s_], half[:, s_], ALU.pow))
                nc.gpsimd.tensor_tensor(nmr[:, s_], nmean[:, s_], rstd[:, s_], ALU.mult).then_inc(rstd_ready, 1)

            rstd_by_sums(1, link)
            rstd_by_sums(2, link)
            gp.wait_ge(ld["bias"], 16 * 11)
            link(nc.gpsimd.tensor_scalar(gbb[:, :], gbb[:, :], alc[:, 0:1], None, ALU.mult))
            for t in range(NT):
                link(nc.gpsimd.tensor_tensor(acc[:, t, :], acc[:, t, :], xn[:, t, :], ALU.add))
                add_b = nc.gpsimd.tensor_tensor(acc[:, t, :], acc[:, t, :], gbb[:, :], ALU.add)
            add_b.then_inc(acc_pre, 1)
            gp.wait_ge(x_high, 1)
            nc.gpsimd.tensor_tensor(xl[:, :, :], xn[:, :, :], xh[:, :, :].bitcast(F32), ALU.subtract).then_inc(x_low, 1)

            def split(whole, high, low):
                link(nc.gpsimd.tensor_copy(high, whole))
                return nc.gpsimd.tensor_tensor(low, whole, high.bitcast(F32), ALU.subtract)

            gp.wait_ge(ld["pm"], 32)
            split(pms[:, :], pmh[:, :], pml[:, :]).then_inc(p_split, 1)
            gp.wait_ge(ld["wv"], 16)
            filled(gp, ("A", NT - 1, 2))
            split(wvs[:, :, :], wvh[:, :, :], wvl[:, :, :]).then_inc(wv_split, 1)
            filled(gp, ("agg", 2, C - 1))
            for t in range(NT):
                nc.gpsimd.tensor_tensor(xn[:, t, :], xl[:, t, :].bitcast(F32), xh[:, t, :].bitcast(F32),
                                        ALU.add).then_inc(x_whole, 1)
            gp.wait_ge(ld["wqk"], 16)
            gp.wait_ge(ld["acc_out"], 16)
            split(wqk[:, :, :], wqkh[:, :, :], wqkl[:, :, :]).then_inc(wqk_split, 1)
            gp.wait_ge(ld["xn"], 16)
            for t in range(NT):
                add_b = nc.gpsimd.tensor_tensor(xn[:, t, :], xn[:, t, :], bpb[:, :], ALU.add)
            add_b.then_inc(xnb_ready, 1)
            gp.wait_ge(w_high, 1)
            nc.gpsimd.tensor_tensor(w1l[:, :], w1s[:, :], w1h[:, :].bitcast(F32), ALU.subtract).then_inc(w_low, 1)
            gp.wait_ge(ld["acc"], 16)
            for g in range(3):
                rstd_by_stats(3, g)
            for t in range(NT):
                if t == 2:
                    gp.wait_ge(w_high, 2)
                    nc.gpsimd.tensor_tensor(w2l[:, :], w2s[:, :], w2h[:, :].bitcast(F32),
                                            ALU.subtract).then_inc(w_low, 1)
                evacuated(gp, ("proj", t))
                link(nc.gpsimd.tensor_tensor(acc[:, t, :], acc[:, t, :], xn[:, t, :], ALU.add))
                nc.gpsimd.tensor_tensor(acc[:, t, :], acc[:, t, :], b2b[:, :], ALU.add).then_inc(acc_x2, 1)
            for g in range(3):
                rstd_by_stats(4, g)
            gp.wait_ge(slots_ready, 1)
            gp.wait_ge(ld["zero"], 16 * (2 * SLOT_TILES - SURE_TILES))
            gp.wait_ge(normed, 4 * NT)
            for t in range(NT):
                gp.indirect_dma_start(out=d_y, out_offset=bass.IndirectOffsetOnAxis(ap=posi[:, t:t + 1], axis=0),
                                      in_=hn[:, t, :], in_offset=None).then_inc(scattered, 16)
            used = slot_tiles(gp)
            for s in range(SURE_TILES - 2, SLOT_TILES):
                with if_used(gp, s, used):
                    gp.wait_ge(st_o[s % 2], 16 * (s // 2 + 1))
            for t in range(NT):
                gp.indirect_dma_start(out=ys[0:T, t, :], out_offset=None, in_=d_o,
                                      in_offset=bass.IndirectOffsetOnAxis(ap=posi[:, t:t + 1], axis=0)
                                      ).then_inc(gathered[t], 16)

        @block.scalar
        def _(sc):
            def normalise(rows, to, n, g):
                sc.wait_ge(rstd_ready, 3 * (n - 1) + g + 1)
                for t in tiles(g):
                    nc.scalar.activation(to[:, t, :], rows[:, t, :], ACT.Identity, scale=rstd[:, t:t + 1],
                                         bias=nmr[:, t:t + 1]).then_inc(normed, 1)

            def square_rows(rows, to, n):
                sc.wait_ge(mean_ready, n)
                for t in range(NT):
                    ins = nc.scalar.activation(to[:, t, :], rows[:, t, :], ACT.Square, bias=nmean[:, t:t + 1],
                                               accum_out=sqs[:, t:t + 1])
                ins.then_inc(squared, 1)

            def sum_rows(rows, to, n):
                if n > 1:
                    sc.wait_ge(normed, NT * (n - 1))
                for t in range(NT):
                    ins = nc.scalar.activation(to[:, t, :], rows[:, t, :], ACT.Identity, accum_out=sums[:, t:t + 1])
                ins.then_inc(summed, 1)

            def counts_by_src(t):
                for j, (s0, sn) in enumerate(GROUPS):
                    bank = filled(sc, ("AT", t, j))
                    read_out(nc.scalar.copy(AT[:, s0:s0 + sn, t * T:(t + 1) * T],
                                            bank[0:T, 0:sn * T].rearrange("p (s d) -> p s d", d=T)), ("AT", t, j))

            sc.wait_ge(ld["x"], 16)
            sum_rows(acc, xn, 1)
            square_rows(acc, xn, 1)
            for t in range(NT):
                if t >= 2:
                    filled(sc, ("AT", t - 2, 2))
                for j, (c0, cn) in enumerate(CH):
                    bank = filled(sc, ("A", t, j))
                    read_out(nc.scalar.activation(arow[:, t % 2, c0:c0 + cn], bank[0:T, 0:cn], ACT.Identity,
                                                  accum_out=deg3[:, t, j:j + 1]), ("A", t, j))
                if t >= 1:
                    counts_by_src(t - 1)
                if t == 0:
                    for g in range(3):
                        normalise(acc, xn, 1, g)
                if t == 1:
                    sum_rows(xn, hn, 2)
                if t == 2:
                    square_rows(xn, hn, 2)
                if t == 3:
                    sc.wait_ge(squared, 2)
                    nc.scalar.copy(xh[:, :, :], xn[:, :, :]).then_inc(x_high, 1)
            counts_by_src(NT - 1)
            for k in range(C):
                bank = filled(sc, ("gWT", k))
                read_out(nc.scalar.copy(gwT[:, k, :], bank[:, :]), ("gWT", k))
            evacuated(sc, ("AT", NT - 1, 2))
            for n, (c0, cn) in enumerate(CH):
                for s in range(NT):
                    if n:
                        sc.wait_ge(at_low, NT * (n - 1) + s + 1)
                    if n and s < NT - 1:
                        sc.wait_ge(at_used, (NT - 1) * (n - 1) + s + 1)
                    elif n:
                        filled(sc, ("agg", n - 1, C - 1))
                    nc.scalar.copy(ath[:, s, 0:cn], AT[:, s, c0:c0 + cn]).then_inc(at_high, 1)
            for g in range(3):
                sc.wait_ge(x_whole, tiles(g)[-1] + 1)
                normalise(xn, hn, 2, g)
            filled(sc, ("gnn", NT - 1))
            sc.wait_ge(ld["bias"], 16 * 11)
            sc.wait_ge(ld["xn_out"], 16)
            for j, (c0, cn) in enumerate(CH):
                for c in range(C):
                    bank = filled(sc, ("hT", c, j))
                    nc.scalar.activation(hTh[:, c, c0:c0 + cn], bank[:, 0:cn], ACT.Identity,
                                         scale=g1c[:, c:c + 1], bias=be1c[:, c:c + 1])
                    read_out(nc.scalar.activation(hTf[:, c, c0:c0 + cn], bank[:, 0:cn], ACT.Identity,
                                                  scale=g1c[:, c:c + 1], bias=be1c[:, c:c + 1]), ("hT", c, j))

            def round_qk(p):
                for n, w in qk_groups:
                    c0, cn = CH[n]
                    bank = filled(sc, ("qk", p, n, w))
                    for i in range(2):
                        r = slice(DH * i, DH * i + DH)
                        ins = nc.scalar.activation(qkT[w][r, i, c0:c0 + cn], bank[r, 0:cn], ACT.Identity,
                                                   bias=bqkc[r, w * C + p:w * C + p + 1])
                    ins.then_inc(q_high, 1)

            round_qk(0)
            for p in range(PAIRS):
                for t in range(NT):
                    for w, name in enumerate(("kf", "qf")):
                        g = 2 * (p * NT + t) + w
                        bank = filled(sc, (name, p, t))
                        sc.wait_ge(max_ready, g + 1)
                        if t >= 2:
                            filled(sc, ("qT", p, t - 2))
                        elif p:
                            filled(sc, ("qT", p - 1, NT - 2 + t))
                        for i in range(2):
                            e = nc.scalar.activation(ering[:, 2 * (t % 2) + w, i * NF:(i + 1) * NF],
                                                     bank[0:T, i * NF:(i + 1) * NF], ACT.Exp,
                                                     bias=nmax[:, g % 4, i:i + 1])
                            if i:
                                read_out(e, (name, p, t))
                if p < PAIRS - 1:
                    round_qk(p + 1)
                if p:
                    sc.wait_ge(ld["den"], 16 * p)
                for i in range(2):
                    for n, (c0, cn) in enumerate(CH):
                        bank = filled(sc, ("att", p, i, n))
                        nc.scalar.copy(attT[DH * i:DH * i + DH, p, c0:c0 + cn], bank[0:DH, 0:cn])
                        read_out(nc.scalar.copy(den[0:1, i * N + c0:i * N + c0 + cn], bank[DH:DH + 1, 0:cn]),
                                 ("att", p, i, n))
            def second_rows(g):
                _, cn = CH[g]
                if g:
                    filled(sc, ("up", g - 1, MC - 1))
                for c in range(C):
                    bank = filled(sc, ("h2T", c, g))
                    nc.scalar.activation(h2h[:, c, 0:cn], bank[:, 0:cn], ACT.Identity, scale=g2c[:, c:c + 1],
                                         bias=be2c[:, c:c + 1])
                    read_out(nc.scalar.activation(h2f[:, c, 0:cn], bank[:, 0:cn], ACT.Identity,
                                                  scale=g2c[:, c:c + 1], bias=be2c[:, c:c + 1]), ("h2T", c, g))

            normalise(xn, hn, 3, 0)
            second_rows(0)
            normalise(xn, hn, 3, 1)
            normalise(xn, hn, 3, 2)
            for n, (c0, cn) in enumerate(CH):
                if n:
                    filled(sc, ("down", GROUPS[n][0] - 1))
                for m in range(MC):
                    bank = filled(sc, ("up", n, m))
                    read_out(nc.scalar.activation(gf[:, m, 0:cn], bank[:, 0:cn], ACT.Gelu,
                                                  bias=b1c[:, m:m + 1]), ("up", n, m))
                if n < 2:
                    second_rows(n + 1)
            for g in range(3):
                normalise(acc, hn, 4, g)
            used = slot_tiles(sc)
            for s in range(SLOT_TILES):
                with if_used(sc, s, used):
                    bank = filled(sc, ("yT", s))
                    if s >= 2:
                        filled(sc, ("ffn", s - 2))
                    read_out(nc.scalar.copy(yT[:, s % 2, :], bank[:, :]), ("yT", s))

        @block.vector
        def _(ve):
            chain = [0]

            def link(ins):
                chain[0] += 1
                ins.then_inc(dve, 1)
                ve.wait_ge(dve, chain[0])

            def statistics(rows, g):
                for t in tiles(g):
                    ins = nc.vector.bn_stats(st[:, t, :], rows[:, t, :])
                link(ins)
                for t in tiles(g):
                    ins = nc.vector.bn_aggr(mv[:, t, :], st[:, t, :])
                ins.then_inc(stats, 1)

            nc.vector.memset(zb[:, :], 0.0).then_inc(zeros_ready, 1)
            ve.wait_ge(ld["edges"], 32)
            link(nc.vector.tensor_copy(edf[:, :, :], edi[:, :, :]))
            nc.vector.tensor_reduce(out=mm[:, 0:1], in_=edf[:, 0, :], op=ALU.min, axis=AX)
            link(nc.vector.tensor_reduce(out=mm[:, 1:2], in_=edf[:, 0, :], op=ALU.max, axis=AX))
            ve.wait_ge(consts, 1)
            nc.vector.tensor_scalar(mdiag[:, 0, :], ident[0:ER, 0:ER], mm[:, 0:1], None, ALU.mult)
            nc.vector.tensor_scalar(mdiag[:, 1, :], ident[0:ER, 0:ER], mm[:, 1:2], None,
                                    ALU.mult).then_inc(edge_tab, 1)
            bank = filled(ve, "edge_cols")
            cols = bank[0:T, 0:2 * EH * ER].rearrange("p (w b a) -> p w a b", w=2, b=EH)
            nc.vector.tensor_copy(dcol[:, :, :], cols[:, 0])
            read_out(nc.vector.tensor_copy(scol[:, :, :], cols[:, 1]), "edge_cols")
            bank = filled(ve, "edge_range")
            nc.vector.tensor_scalar(rrow[:, 0, :], bank[0:NT, 0:ER], t0[:, 1:2], None, ALU.is_le)
            read_out(nc.vector.tensor_scalar(rrow[:, 1, :], bank[0:NT, ER:2 * ER], t0[:, 0:1], None, ALU.is_ge),
                     "edge_range")
            evacuated(ve, "edge_range")
            link(nc.vector.tensor_tensor(rrow[:, 2, :], rrow[:, 0, :], rrow[:, 1, :], ALU.mult))
            nc.vector.tensor_tensor(rrow[:, 3, :], rrow[:, 2, :], arow_e[:, 0, :], ALU.mult)
            link(nc.vector.tensor_tensor(rrow[:, 4, :], rrow[:, 2, :], arow_e[:, 1, :], ALU.mult))
            nc.vector.reduce_max(rsm[:, 0:1], rrow[:, 3, :], AX)
            link(nc.vector.reduce_max(rsm[:, 1:2], rrow[:, 4, :], AX))
            link(nc.vector.tensor_scalar(rsm[:, 2:3], rsm[:, 1:2], -1.0, float(ER), ALU.mult, ALU.add))
            link(nc.vector.tensor_scalar(rsm[:, 3:4], rsm[:, 2:3], float(ER - 3), None, ALU.min))
            nc.vector.tensor_scalar(rsm[:, 4:5], rsm[:, 3:4], 2.0, None, ALU.add)
            link(nc.vector.tensor_scalar(rsm[:, 5:6], rsm[:, 0:1], -1.0, None, ALU.add))
            link(nc.vector.tensor_tensor(rsm[:, 6:7], rsm[:, 4:5], rsm[:, 5:6], ALU.max))
            nc.vector.tensor_copy(bounds[:, 0:1], rsm[:, 3:4])
            nc.vector.tensor_copy(bounds[:, 1:2], rsm[:, 6:7]).then_inc(bounds_ready, 1)
            ve.wait_ge(bounds_ready, 1)
            evacuated(ve, "edge_cols")
            turn = ve.alloc_register("dve_turn")
            ve.reg_mov(turn, 0)
            for t in range(NT):
                first = ve.value_load(bounds[t:t + 1, 0:1], min_val=0, max_val=ER - 3)
                last = ve.value_load(bounds[t:t + 1, 1:2], min_val=2, max_val=ER - 1)
                with ve.Fori(first, last + 1) as a:
                    ve.reg_add(turn, turn, 1)
                    for b in range(EH):
                        ve.wait_ge(oh_used[b], turn)
                        nc.vector.tensor_scalar(ohd[:, b, :], iota[:, 0:128], float(t * T),
                                                dcol[:, bass.ds(a, 1), b], ALU.add, ALU.is_equal)
                        nc.vector.tensor_scalar(ohs[:, b, :], iota[:, :], scol[:, bass.ds(a, 1), b], None,
                                                ALU.is_equal).then_inc(oh_ready[b], 1)
            def gnn_rows(t):
                bank = filled(ve, ("gnn", t))
                read_out(nc.vector.scalar_tensor_tensor(out=acc[:, t, :], in0=bank[0:T, :], scalar=coef[:, t:t + 1],
                                                        in1=acc[:, t, :], op0=ALU.mult, op1=ALU.add), ("gnn", t))

            evacuated(ve, ("A", NT - 1, 2))
            link(nc.vector.reduce_sum(deg[:, :], deg3[:, :, :], AX))
            link(nc.vector.tensor_scalar(deg[:, :], deg[:, :], 1.0, None, ALU.max))
            link(nc.vector.reciprocal(coef[:, :], deg[:, :]))
            ve.wait_ge(ld["bias"], 16 * 11)
            link(nc.vector.tensor_scalar(coef[:, :], coef[:, :], alc[:, 0:1], None, ALU.mult))
            ve.wait_ge(acc_pre, 1)

            def counts_rest(n):
                c0, cn = CH[n]
                for s in range(NT):
                    ve.wait_ge(at_high, n * NT + s + 1)
                    nc.vector.tensor_tensor(atl[:, s, c0:c0 + cn], AT[:, s, c0:c0 + cn],
                                            ath[:, s, 0:cn].bitcast(F32), ALU.subtract).then_inc(at_low, 1)

            counts_rest(0)
            for n, (c0, cn) in enumerate(CH):
                if n < 2:
                    counts_rest(n + 1)
                if n == 2:
                    filled(ve, ("gnn", GROUPS[1][0] - 1))
                filled(ve, ("gWT", C - 1))
                for c in range(C):
                    bank = filled(ve, ("agg", n, c))
                    read_out(nc.vector.tensor_copy(aggT[n % 2][:, c, 0:cn], bank[:, 0:cn]), ("agg", n, c))
                for t in (tiles(n - 1) if n else ()):
                    gnn_rows(t)
            for t in tiles(2):
                gnn_rows(t)
            nc.vector.memset(v65[:, :, :, DH:DH + 1], 1.0)
            for j, (c0, cn) in enumerate(CH):
                for c in range(C):
                    evacuated(ve, ("hT", c, j))
                    nc.vector.tensor_tensor(hTl[:, c, c0:c0 + cn], hTf[:, c, c0:c0 + cn],
                                            hTh[:, c, c0:c0 + cn].bitcast(F32), ALU.subtract).then_inc(h_split, 1)
            for t in range(NT):
                bank = filled(ve, ("v", t))
                read_out(nc.vector.tensor_tensor(v65[:, t, :, 0:DH],
                                                 bank[0:T, :].rearrange("p (h e) -> p h e", e=DH),
                                                 bvb[:, :].rearrange("p (h e) -> p h e", e=DH), ALU.add), ("v", t))

            def reciprocals(p):
                ve.wait_ge(ld["dent"], 16 * (p + 1))
                nc.vector.reciprocal(zr[:, :], zt[:, :]).then_inc(z_ready, 1)

            def normalise_attention(p):
                ve.wait_ge(ld["zb"], 32 * (p + 1))
                nc.vector.tensor_tensor(attT[:, p, :], attT[:, p, :], zb[:, :], ALU.mult).then_inc(attn_ready, 1)

            def q_features_by_feature(p, t):
                bank = filled(ve, ("qT", p, t))
                read_out(nc.vector.tensor_copy(eqT[:, :, t * T:(t + 1) * T],
                                               bank[:, 0:2 * FC * T].rearrange("p (f t) -> p f t", t=T)), ("qT", p, t))

            def qk_rest(p):
                for g, (n, w) in enumerate(qk_groups):
                    c0, cn = CH[n]
                    ve.wait_ge(q_high, p * len(qk_groups) + g + 1)
                    bank = filled(ve, ("qk", p, n, w))
                    for i in range(2):
                        r, o = slice(DH * i, DH * i + DH), slice(DH * (1 - i), DH * (1 - i) + DH)
                        ins = nc.vector.scalar_tensor_tensor(
                            out=qkT[w][o, i, c0:c0 + cn], in0=bank[r, 0:cn], scalar=bqkc[r, w * C + p:w * C + p + 1],
                            in1=qkT[w][r, i, c0:c0 + cn].bitcast(F32), op0=ALU.add, op1=ALU.subtract)
                    read_out(ins, ("qk", p, n, w))

            qk_rest(0)
            for p in range(PAIRS):
                for t in range(NT):
                    for w, name in enumerate(("kf", "qf")):
                        g = 2 * (p * NT + t) + w
                        bank = filled(ve, (name, p, t))
                        if g >= 4:
                            q = g - 4
                            evacuated(ve, (("kf", "qf")[q % 2], q // 2 // NT, q // 2 % NT))
                        nc.vector.tensor_reduce(out=nmax[:, g % 4, :],
                                                in_=bank[0:T, :].rearrange("p (i f) -> p i f", i=2), op=ALU.max,
                                                axis=AX, negate=True).then_inc(max_ready, 1)
                    if t >= 1:
                        q_features_by_feature(p, t - 1)
                    if p and t == 4:
                        reciprocals(p - 1)
                    if p and t == NT - 1:
                        normalise_attention(p - 1)
                q_features_by_feature(p, NT - 1)
                for i in range(2):
                    bank = filled(ve, ("kv", p, i))
                    read_out(nc.vector.tensor_scalar(kvT[:, i, :], bank[0:DH + 1, 0:NF], kse[:, 0:1], None, ALU.add),
                             ("kv", p, i))
                if p < PAIRS - 1:
                    qk_rest(p + 1)
                bank = filled(ve, ("kvT", p))
                read_out(nc.vector.tensor_copy(kv[:, :, :],
                                               bank[:, 0:2 * FC * (DH + 1)].rearrange("p (f e) -> p f e", e=DH + 1)),
                         ("kvT", p))
            ve.wait_ge(ld["w1"], 16)
            nc.vector.tensor_copy(w1h[:, :], w1s[:, :]).then_inc(w_high, 1)
            reciprocals(PAIRS - 1)
            normalise_attention(PAIRS - 1)
            ve.wait_ge(xnb_ready, 1)
            for g in range(3):
                for t in tiles(g):
                    bank = filled(ve, ("proj", t))
                    read_out(nc.vector.tensor_tensor(xn[:, t, :], bank[0:T, :], xn[:, t, :], ALU.add), ("proj", t))
                evacuated(ve, ("proj", tiles(g)[-1]))
                statistics(xn, g)

            def second_rest(g):
                _, cn = CH[g]
                for c in range(C):
                    evacuated(ve, ("h2T", c, g))
                    nc.vector.tensor_tensor(h2l[:, c, 0:cn], h2f[:, c, 0:cn], h2h[:, c, 0:cn].bitcast(F32),
                                            ALU.subtract).then_inc(h2_split, 1)

            second_rest(0)
            ve.wait_ge(ld["w2"], 16)
            nc.vector.tensor_copy(w2h[:, :], w2s[:, :]).then_inc(w_high, 1)
            for n, (c0, cn) in enumerate(CH):
                for m in range(MC):
                    evacuated(ve, ("up", n, m))
                    link(nc.vector.tensor_copy(gh[:, m, 0:cn], gf[:, m, 0:cn]))
                    nc.vector.tensor_tensor(gl[:, m, 0:cn], gf[:, m, 0:cn], gh[:, m, 0:cn].bitcast(F32),
                                            ALU.subtract).then_inc(g_split, 1)
                if n < 2:
                    second_rest(n + 1)
                for t in tiles(n):
                    ve.wait_ge(acc_x2, t + 1)
                    bank = filled(ve, ("down", t))
                    read_out(nc.vector.tensor_tensor(acc[:, t, :], bank[0:T, :], acc[:, t, :], ALU.add),
                             ("down", t))
                evacuated(ve, ("down", tiles(n)[-1]))
                statistics(acc, n)
            ve.wait_ge(normed, 4 * NT)
            for j, edge in enumerate(BINS):
                ins = nc.vector.tensor_scalar(cmp[:, j, :], hn[:, :, 0], edge, None, ALU.is_gt)
            link(ins)
            link(nc.vector.reduce_sum(mem[:, :], cmp[:, :, :].rearrange("p j t -> p t j"), AX))
            nc.vector.tensor_tensor(boh[:, :, :], mem[:, :].unsqueeze(2).to_broadcast([T, NT, NB]),
                                    krow[:, :].unsqueeze(1).to_broadcast([T, NT, NB]), ALU.is_equal
                                    ).then_inc(boh_ready, 1)
            bank = filled(ve, "rank")
            link(nc.vector.tensor_copy(cnt[:, 0, :], bank[0:T, NT * NB:(NT + 1) * NB]))
            link(nc.vector.tensor_tensor(tl[:, :, :], cnt[:, 0, :].unsqueeze(1).to_broadcast([T, NT, NB]),
                                         many[:, :, :], ALU.is_gt))
            link(nc.vector.reduce_sum(cnt[:, 1, :], tl[:, :, :].rearrange("p j k -> p k j"), AX))
            link(nc.vector.tensor_tensor(below[:, :, :], cnt[:, 1, :].unsqueeze(1).to_broadcast([T, NB, NB]),
                                         lower[:, :, :], ALU.mult))
            link(nc.vector.reduce_sum(ctl[:, 0, 0:NB], below[:, :, :], AX))
            link(nc.vector.tensor_scalar(ctl[:, 1, 0:NB], ctl[:, 0, 0:NB], float(ST), None, ALU.mult))
            read_out(nc.vector.tensor_tensor(pr[:, :, :], bank[0:T, 0:NT * NB].rearrange("p (t k) -> p t k", k=NB),
                                             ctl[:, 1, 0:NB].unsqueeze(1).to_broadcast([T, NT, NB]), ALU.add), "rank")
            evacuated(ve, "rank")
            link(nc.vector.tensor_tensor(pr[:, :, :], pr[:, :, :], boh[:, :, :], ALU.mult))
            link(nc.vector.reduce_sum(posf[:, :], pr[:, :, :], AX))
            nc.vector.tensor_copy(posi[:, :], posf[:, :]).then_inc(slots_ready, 1)
            link(nc.vector.tensor_tensor(slotc[:, :, :], jrow[:, :].unsqueeze(1).to_broadcast([T, NB, SLOT_TILES]),
                                         ctl[:, 0, 0:NB].unsqueeze(2).to_broadcast([T, NB, SLOT_TILES]), ALU.is_ge))
            nc.vector.reduce_sum(exf[:, 0:SLOT_TILES], slotc[:, 1:NB, :].rearrange("p k j -> p j k"), AX)
            link(nc.vector.reduce_sum(exf[:, SLOT_TILES:SLOT_TILES + 1], cnt[:, 1, :], AX))
            nc.vector.tensor_copy(exr[:, :], exf[:, :]).then_inc(slots_ready, 1)
            used = slot_tiles(ve)
            for s in range(SLOT_TILES):
                with if_used(ve, s, used):
                    bank = filled(ve, ("ffn", s))
                    if s >= 2:
                        ve.wait_ge(st_o[s % 2], 16 * (s // 2))
                    read_out(nc.vector.tensor_copy(ob[:, s % 2, :], bank[:, :]), ("ffn", s))
            for t in range(NT):
                ve.wait_ge(gathered[t], 16)
                nc.vector.tensor_tensor(acc[:, t, :], acc[:, t, :], ys[0:T, t, :], ALU.add).then_inc(final, 1)

        @block.tensor
        def _(pe):
            def begin(key):
                _, bank, before = plan.order[key]
                if before:
                    pe.wait_ge(bank_read[bank], before)
                return P[bank]

            def product(out_, pairs):
                for n, (a, b) in enumerate(pairs):
                    ins = nc.tensor.matmul(out_, a, b, start=(n == 0), stop=(n == len(pairs) - 1))
                return ins

            def split_product(out_, high_low, start=True, stop=True):
                n = 3 * len(high_low)
                for i, (ah, al, bh, bl) in enumerate(high_low):
                    for j, (a, b) in enumerate(((ah, bh), (ah, bl), (al, bh))):
                        ins = nc.tensor.matmul(out_, a, b, start=(start and i + j == 0),
                                               stop=(stop and 3 * i + j == n - 1))
                return ins

            def transposes(key, blocks, rows, cols, signal=psum_filled):
                bank = begin(key)
                for n, block_ in enumerate(blocks):
                    ins = nc.tensor.transpose(bank[0:cols, n * rows:(n + 1) * rows], block_, ident[0:rows, 0:rows])
                ins.then_inc(signal, 1)

            pe.wait_ge(consts, 1)
            pe.wait_ge(edge_tab, 1)
            transposes("edge_cols", [edf[:, w, b * T:(b + 1) * T] for w in range(2) for b in range(EH)], ER, T)
            bank = begin("edge_range")
            product(bank[0:NT, 0:2 * ER], [(ones[0:ER, 0:NT], mdiag[:, :, :].rearrange("p w a -> p (w a)"))]
                    ).then_inc(psum_filled, 1)
            pe.wait_ge(bounds_ready, 1)
            first, last, turn, used, rows, large = (pe.alloc_register(f"pe_{k}") for k in
                                                    ("first", "last", "turn", "used", "rows", "large"))
            pe.reg_mov(large, 0)
            pe.reg_mov(turn, 0)
            for b in range(EH):
                pe.sem_inc(oh_used[b], 1)

            def count_row(banks, start, stop):
                pe.reg_add(turn, turn, 1)
                for b in range(EH):
                    pe.wait_ge(oh_ready[b], turn)
                    for j, (c0, cn) in enumerate(CH):
                        ins = nc.tensor.matmul(banks[j][0:T, 0:cn], ohd[:, b, 0:T], ohs[:, b, c0:c0 + cn],
                                               start=start and b == 0, stop=stop and b == EH - 1)
                    ins.then_inc(oh_used[b], 1)

            for t in range(NT):
                banks = [begin(("A", t, j)) for j in range(3)]
                pe.reg_load(first, bounds[t:t + 1, 0:1])
                pe.reg_load(last, bounds[t:t + 1, 1:2])
                pe.reg_sub(rows, last, first)
                many_rows = pe.snap(rows, min_val=0, max_val=ER)
                with pe.If(many_rows > MAX_ROWS - 1):
                    pe.reg_mov(large, 1)
                pe.reg_add(first, first, 1)
                count_row(banks, True, False)
                with pe.Fori(first, last) as _a:
                    count_row(banks, False, False)
                count_row(banks, False, True)
                pe.reg_add(used, turn, 1)
                pe.wait_ge(oh_used[EH - 1], used)
                pe.sem_inc(psum_filled, 3)
                if t >= 1:
                    for j, (s0, sn) in enumerate(GROUPS):
                        for jj in range(3):
                            evacuated(pe, ("A", t - 1, jj))
                        transposes(("AT", t - 1, j), [arow[:, (t - 1) % 2, s * T:(s + 1) * T]
                                                      for s in range(s0, s0 + sn)], T, T)
            for jj in range(3):
                evacuated(pe, ("A", NT - 1, jj))
            for j, (s0, sn) in enumerate(GROUPS):
                transposes(("AT", NT - 1, j), [arow[:, (NT - 1) % 2, s * T:(s + 1) * T]
                                               for s in range(s0, s0 + sn)], T, T)
            pe.wait_ge(ld["gw"], 16)
            for k in range(C):
                transposes(("gWT", k), [gws[:, o, k * 128:(k + 1) * 128] for o in range(C)], 128, 128)
            for j in range(3):
                for t in (NT - 2, NT - 1):
                    evacuated(pe, ("AT", t, j))
            pe.wait_ge(x_low, 1)
            for n in range(4):
                if n < 3:
                    c0, cn = CH[n]
                    banks = [begin(("agg", n, c)) for c in range(C)]
                    for s in range(NT):
                        pe.wait_ge(at_high, n * NT + s + 1)
                        if s == NT - 1:
                            pe.wait_ge(at_low, (n + 1) * NT)
                            with pe.If(pe.snap(large, min_val=0, max_val=1) > 0):
                                for s2 in range(NT):
                                    for c in range(C):
                                        nc.tensor.matmul(banks[c][:, 0:cn], xh[:, s2, c * 128:(c + 1) * 128],
                                                         atl[:, s2, c0:c0 + cn], start=False, stop=False)
                        for c in range(C):
                            k = slice(c * 128, (c + 1) * 128)
                            nc.tensor.matmul(banks[c][:, 0:cn], xh[:, s, k], ath[:, s, 0:cn], start=(s == 0), stop=False)
                            ins = nc.tensor.matmul(banks[c][:, 0:cn], xl[:, s, k], ath[:, s, 0:cn], start=False,
                                                   stop=(s == NT - 1))
                            if s == NT - 1:
                                ins.then_inc(psum_filled, 1)
                        if s < NT - 1:
                            ins.then_inc(at_used, 1)
                if n == 0:
                    continue
                for k in range(C):
                    evacuated(pe, ("gWT", k))
                    evacuated(pe, ("agg", n - 1, k))
                for t in tiles(n - 1):
                    bank = begin(("gnn", t))
                    r0 = (t - GROUPS[n - 1][0]) * T
                    product(bank[0:T, :], [(aggT[(n - 1) % 2][:, c, r0:r0 + T], gwT[:, c, :]) for c in range(C)]
                            ).then_inc(psum_filled, 1)

            pe.wait_ge(normed, 2 * NT)
            for j in range(3):
                for c in range(C):
                    transposes(("hT", c, j), [hn[:, t, c * 128:(c + 1) * 128] for t in tiles(j)], T, 128)
            pe.wait_ge(wv_split, 1)
            for j in range(3):
                pe.wait_ge(h_split, C * (j + 1))
                for t in tiles(j):
                    r = slice(t * T, (t + 1) * T)
                    bank = begin(("v", t))
                    split_product(bank[0:T, :], [(hTh[:, c, r], hTl[:, c, r], wvh[:, c, :], wvl[:, c, :])
                                                 for c in range(C)]).then_inc(psum_filled, 1)

            def queries_and_keys(p):
                for n, w in qk_groups:
                    c0, cn = CH[n]
                    q = slice(w * D + p * 128, w * D + (p + 1) * 128)
                    bank = begin(("qk", p, n, w))
                    split_product(bank[:, 0:cn], [(wqkh[:, c, q], wqkl[:, c, q], hTh[:, c, c0:c0 + cn],
                                                   hTl[:, c, c0:c0 + cn]) for c in range(C)]
                                  ).then_inc(psum_filled, 1)

            pe.wait_ge(wqk_split, 1)
            queries_and_keys(0)
            pe.wait_ge(p_split, 1)
            for p in range(PAIRS):
                kvb = [begin(("kv", p, i)) for i in range(2)]

                def sum_and_transpose(t):
                    evacuated(pe, ("kf", p, t))
                    for i in range(2):
                        ins = nc.tensor.matmul(kvb[i][0:DH + 1, 0:NF], v65[:, t, 2 * p + i, :],
                                               ering[:, 2 * (t % 2), i * NF:(i + 1) * NF],
                                               start=(t == 0), stop=(t == NT - 1))
                        if t == NT - 1:
                            ins.then_inc(psum_filled, 1)
                    evacuated(pe, ("qf", p, t))
                    transposes(("qT", p, t), [ering[:, 2 * (t % 2) + 1, f * 128:(f + 1) * 128]
                                              for f in range(2 * FC)], T, 128)

                for t in range(NT):
                    for n, w in qk_groups:
                        if t == GROUPS[n][0]:
                            evacuated(pe, ("qk", p, n, w))
                    for w, name in ((1, "kf"), (0, "qf")):
                        bank = begin((name, p, t))
                        for i in range(2):
                            both = qkT[w][:, i, t * T:(t + 1) * T]
                            ins = product(bank[0:T, i * NF:(i + 1) * NF], [(both, pmh[:, :]), (both, pml[:, :])])
                        ins.then_inc(psum_filled, 1)
                    if t >= 1:
                        sum_and_transpose(t - 1)
                sum_and_transpose(NT - 1)
                if p < PAIRS - 1:
                    queries_and_keys(p + 1)
                for i in range(2):
                    evacuated(pe, ("kv", p, i))
                transposes(("kvT", p), [kvT[:, i, f * 128:(f + 1) * 128] for i in range(2) for f in range(FC)],
                           DH + 1, 128)
                evacuated(pe, ("kvT", p))
                evacuated(pe, ("qT", p, NT - 1))
                for i in range(2):
                    for n, (c0, cn) in enumerate(CH):
                        bank = begin(("att", p, i, n))
                        product(bank[0:DH + 1, 0:cn], [(kv[:, i * FC + f, :], eqT[:, i * FC + f, c0:c0 + cn])
                                                       for f in range(FC)]).then_inc(psum_filled, 1)
            pe.wait_ge(ld["wp"], 16)
            pe.wait_ge(attn_ready, PAIRS - 1)
            for t in range(8):
                bank = begin(("proj", t))
                for p in range(PAIRS - 1):
                    nc.tensor.matmul(bank[0:T, :], attT[:, p, t * T:(t + 1) * T], wps[:, p, :], start=(p == 0),
                                     stop=False)
            pe.wait_ge(attn_ready, PAIRS)
            for t in range(NT):
                bank = begin(("proj", t)) if t >= 8 else P[plan.order[("proj", t)][1]]
                for p in range(PAIRS if t >= 8 else 1):
                    p = p if t >= 8 else PAIRS - 1
                    ins = nc.tensor.matmul(bank[0:T, :], attT[:, p, t * T:(t + 1) * T], wps[:, p, :],
                                           start=(t >= 8 and p == 0), stop=(p == PAIRS - 1))
                ins.then_inc(psum_filled, 1)

            for n in range(4):
                if n < 3:
                    _, cn = CH[n]
                    pe.wait_ge(normed, 2 * NT + tiles(n)[-1] + 1)
                    for c in range(C):
                        transposes(("h2T", c, n), [hn[:, t, c * 128:(c + 1) * 128] for t in tiles(n)], T, 128)
                if n >= 1:
                    pe.wait_ge(w_low, 2)
                    for t in tiles(n - 1):
                        r = slice((t - GROUPS[n - 1][0]) * T, (t - GROUPS[n - 1][0] + 1) * T)
                        bank = begin(("down", t))
                        for m in range(MC):
                            if t == GROUPS[n - 1][0]:
                                pe.wait_ge(g_split, MC * (n - 1) + m + 1)
                            w = slice(m * D, (m + 1) * D)
                            ins = split_product(bank[0:T, :], [(gh[:, m, r], gl[:, m, r], w2h[:, w], w2l[:, w])],
                                                m == 0, m == MC - 1)
                        ins.then_inc(psum_filled, 1)
                if n < 3:
                    pe.wait_ge(w_low, 1)
                    for m in range(MC):
                        bank = begin(("up", n, m))
                        for c in range(C):
                            if m == 0:
                                pe.wait_ge(h2_split, C * n + c + 1)
                            w = slice(c * M + m * 128, c * M + (m + 1) * 128)
                            ins = split_product(bank[:, 0:cn], [(w1h[:, w], w1l[:, w], h2h[:, c, 0:cn],
                                                                 h2l[:, c, 0:cn])], c == 0, c == C - 1)
                        ins.then_inc(psum_filled, 1)
            pe.wait_ge(boh_ready, 1)
            bank = begin("rank")
            all_bins = boh[:, :, :].rearrange("p t k -> p (t k)")
            nc.tensor.matmul(bank[0:T, 0:NT * NB], trib[:, 0:T], all_bins, start=True, stop=False)
            for t in range(NT - 1):
                nc.tensor.matmul(bank[0:T, (t + 1) * NB:NT * NB], onesb[:, 0:T],
                                 boh[:, t:t + 1, :].to_broadcast([T, NT - 1 - t, NB]), start=False,
                                 stop=(t == NT - 2))
            for t in range(NT):
                ins = nc.tensor.matmul(bank[0:T, NT * NB:(NT + 1) * NB], onesb[:, 0:T], boh[:, t, :],
                                       start=(t == 0), stop=(t == NT - 1))
            ins.then_inc(psum_filled, 1)
            used = slot_tiles(pe)
            pe.wait_ge(ld["fw"], 16 * (NB - 1))
            expert = pe.alloc_register("pe_expert")

            def transpose_slots(s):
                with if_used(pe, s, used):
                    pe.wait_ge(ld_ys[s], 16)
                    transposes(("yT", s), [ys[:, s, c * 128:(c + 1) * 128] for c in range(C)], ST, 128,
                               ffn_filled["yT"])

            transpose_slots(0)
            for s in range(SLOT_TILES):
                if s + 1 < SLOT_TILES:
                    transpose_slots(s + 1)
                with if_used(pe, s, used):
                    evacuated(pe, ("yT", s))
                    pe.reg_load(expert, exr[0:1, s:s + 1])
                    e = pe.snap(expert, min_val=0, max_val=NB - 1)
                    bank = begin(("ffn", s))
                    product(bank[:, :], [(yT[:, s % 2, c * ST:(c + 1) * ST], fw[:, bass.ds((e * C + c) * D, D)])
                                         for c in range(C)]).then_inc(ffn_filled["ffn"], 1)


_INS = ['x', 'src', 'dst', 'L0_gnn_alpha', 'L0_gnn_W', 'L0_gnn_b', 'L0_mix_Wqkv', 'L0_mix_bqkv', 'L0_mix_Pmat',
        'L0_mix_Wproj', 'L0_mix_bproj', 'L0_mix_W1', 'L0_mix_b1', 'L0_mix_W2', 'L0_mix_b2', 'L0_mix_g1', 'L0_mix_be1',
        'L0_mix_g2', 'L0_mix_be2', 'L0_ffn_W']


def kernel(**inputs):
    import numpy as np
    import concourse.bacc as bacc
    from concourse.bass_utils import run_bass_kernel_spmd

    nc = bacc.Bacc("TRN2", target_bir_lowering=False, num_devices=1)
    arrays, args = {}, []
    for name in _INS:
        a = np.ascontiguousarray(inputs[name])
        if a.ndim == 0:
            a = a.reshape(1)
        arrays["in_" + name] = a
        args.append(nc.dram_tensor("in_" + name, a.shape, mybir.dt.from_np(a.dtype), kind="ExternalInput").ap())
    out = nc.dram_tensor("out", arrays["in_x"].shape, F32, kind="ExternalOutput").ap()
    build(nc, *args, out)
    r = run_bass_kernel_spmd(nc, [arrays], core_ids=[0])
    return r.results[0]["out"]
```

```python
from contextlib import ExitStack, nullcontext

import concourse.bass as bass
from concourse import mybir

F32 = mybir.dt.float32
F16 = mybir.dt.float16
BF16 = mybir.dt.bfloat16
I32 = mybir.dt.int32
F32R = mybir.dt.float32r
ALU = mybir.AluOpType
ACT = mybir.ActivationFunctionType
AX = mybir.AxisListType.X

EPS = 1e-5
KSUM_EPS = 1e-6
BINS = [-1.5, -1.0, -0.5, 0.0, 0.5, 1.0, 1.5]


def up(n):
    return (n + 31) // 32 * 32


def row_broadcast(row, n):
    return bass.AP(tensor=row.tensor, offset=row.offset, ap=[[0, n]] + [list(d) for d in row.ap])


class PsumPlan:

    def __init__(self):
        self.order, self.uses, self.next = {}, [0] * 8, 0

    def add(self, key, banks=tuple(range(8))):
        while self.next % 8 not in banks:
            self.next += 1
        b = self.next % 8
        self.next += 1
        self.order[key] = (len(self.order), b, self.uses[b])
        self.uses[b] += 1


def build(nc, x, src, dst, alpha, gW, gb, Wqkv, bqkv, Pm, Wp, bp, W1, b1, W2, b2, g1, be1, g2, be2, FW, out):
    N, D = x.shape
    E = src.shape[0]
    T = 125
    NT = N // T
    ROW = 4
    ER = E // (ROW * T)
    ET = ER * ROW
    EH = 6
    STEPS = (ET + EH - 1) // EH
    PAD = STEPS * EH - ET
    C = D // 128
    DH, NF = Pm.shape
    H = D // DH
    PAIRS = H // 2
    M = W1.shape[1]
    MC = M // 128
    NB = len(BINS) + 1
    ST = 128
    SLOT_TILES = (N + NB * (ST - 1)) // ST
    SURE_TILES = (N + ST - 1) // ST
    GROUPS = [(0, 4), (4, 4), (8, 2)]
    CH = [(t * T, n * T) for t, n in GROUPS]
    NW = N + 2
    assert N == NT * T and E == ET * T and DH == 64 and NF == 256 and CH[-1][0] + CH[-1][1] == N
    FC = NF // 128
    MAX_STEPS = 4096 // (EH * T)

    def tiles(g):
        return range(GROUPS[g][0], GROUPS[g][0] + GROUPS[g][1])

    plan = PsumPlan()
    plan.add("edge_cols")
    plan.add("edge_range")
    for t in range(NT + 1):
        if t < NT:
            for j in range(3):
                plan.add(("A", t, j))
        if t >= 1:
            for j in range(3):
                plan.add(("AT", t - 1, j))
    for k in range(C):
        plan.add(("gWT", k))
    for n in range(4):
        if n < 3:
            for c in range(C):
                plan.add(("agg", n, c))
        if n >= 1:
            for t in tiles(n - 1):
                plan.add(("gnn", t))
    for j in range(3):
        for c in range(C):
            plan.add(("hT", c, j))
    for t in range(NT):
        plan.add(("v", t))
    work = (0, 1, 2, 3, 4, 5)
    qk_groups = [(n, w) for n in range(3) for w in range(2)]
    before_kvT, after_kvT = qk_groups[:-2], qk_groups[-2:]
    for n, w in qk_groups:
        plan.add(("qk", 0, n, w), work)
    for p in range(PAIRS):
        for t in range(NT):
            plan.add(("kf", p, t), work)
            plan.add(("qf", p, t), work)
            if t >= 1:
                plan.add(("qT", p, t - 1), work)
        for i in range(2):
            plan.add(("kv", p, i), (6 + i,))
        plan.add(("qT", p, NT - 1), work)
        for n, w in (before_kvT if p < PAIRS - 1 else ()):
            plan.add(("qk", p + 1, n, w), work)
        plan.add(("kvT", p), work)
        for n, w in (after_kvT if p < PAIRS - 1 else ()):
            plan.add(("qk", p + 1, n, w), work)
        for i in range(2):
            for n in range(3):
                plan.add(("att", p, i, n), work)
    for t in range(NT):
        plan.add(("proj", t))
    for n in range(4):
        if n < 3:
            for c in range(C):
                plan.add(("h2T", c, n))
        if n >= 1:
            for t in tiles(n - 1):
                plan.add(("down", t))
        if n < 3:
            for m in range(MC):
                plan.add(("up", n, m))
    plan.add("rank")
    plan.add("tokens")
    for s in range(SLOT_TILES + 1):
        if s < SLOT_TILES:
            plan.add(("yT", s))
        if s >= 1:
            plan.add(("ffn", s - 1))

    base = 16512
    top = [base]

    def at(name, shape, dtype, offset):
        return nc.alloc_sbuf_tensor_at(name, shape, dtype, offset=offset)

    def place(size):
        o = top[0]
        top[0] += (size + 31) // 32 * 32
        return o

    o_xn = place(NT * D * 4)
    o_x = place(up(NT * D * 4))
    o_hT = place(C * N * 4)
    o_v = place(21120)
    o_qk = place(2 * N * 4)
    o_att = place(PAIRS * N * 4)
    o_den = place(2 * N * 4)
    o_q = place(2 * N * 4)
    o_kv = place(2 * NF * 4 + 4 * 65 * 4)
    o_hn = place(NT * D * 4)
    o_acc = place(NT * D * 4)
    o_ring = place(max(4 * 2 * NF * 4, (EH - 2) * up(2 * NW) + EH * 256))

    xn = at("xn", [T, NT, D], F32, o_xn)
    wqk = at("wqk", [128, C, 2 * D], F32, o_x)
    wqkl = at("wqkl", [128, C, 2 * D], F32R, o_x)
    wqkh = at("wqkh", [128, C, 2 * D], F32R, o_acc)
    o_w = o_x
    w1s = at("w1s", [128, C * M], F32, o_w)
    w1l = at("w1l", [128, C * M], F32R, o_w)
    w1h = at("w1h", [128, C * M], F32R, o_w + C * M * 4)
    w2s = at("w2s", [128, MC * D], F32, o_w + 2 * C * M * 4)
    w2l = at("w2l", [128, MC * D], F32R, o_w + 2 * C * M * 4)
    w2h = at("w2h", [128, MC * D], F32R, o_w + 3 * C * M * 4)
    hTh = at("hTh", [128, C, N], F32R, o_hT)
    hTf = at("hTf", [128, C, N], F32, o_xn)
    hTl = at("hTl", [128, C, N], F32R, o_xn)
    v65 = at("v65", [T, NT, H, DH + 1], F32, o_v)
    qkT = [at("qT2", [128, 2, N], F32R, o_q), at("kT2", [128, 2, N], F32R, o_qk)]
    attT = at("attT", [128, PAIRS, N], F32, o_att)
    wps = at("wps", [128, C, D], F32, o_qk)
    wvs = at("wvs", [128, C, D], F32, o_q)
    wvl = at("wvl", [128, C, D], F32R, o_q)
    wvh = at("wvh", [128, C, D], F32R, o_ring)
    den = at("den", [1, 2 * N], F32, o_den)
    kvT = at("kvT", [DH + 1, 2, NF], F32, o_kv)
    kv = at("kv", [128, 2 * FC, DH + 1], F32, o_kv + 2 * NF * 4)
    hn = at("hn", [T, NT, D], F32, o_hn)
    eqT = at("eqT", [128, 2 * FC, N], F32, o_hn)
    acc = at("acc", [T, NT, D], F32, o_acc)
    ering = at("ering", [T, 4, 2 * NF], F32, o_ring)
    o_gw = o_hT + up(NT * N * 4) + up(2 * N * 4)
    o_ohs = [o_ring + b * up(2 * NW) for b in range(EH - 2)] + [o_kv, o_gw + 2 * C * D * 4]
    ohs = [at(f"ohs{b}", [T, NW], BF16, o_ohs[b]) for b in range(EH)]
    assert o_gw + 2 * C * D * 4 + 2 * NW <= o_q and 2 * NW <= o_hn - o_kv
    ohd = at("ohd", [T, EH, 128], BF16, o_ring + (EH - 2) * up(2 * NW))
    xh = at("xh", [T, NT, D], F32R, o_hn)
    xl = at("xl", [T, NT, D], F32R, o_xn)
    ath = at("ath", [T, NT, CH[0][1]], F32R, o_x)
    atl = at("atl", [T, NT, N], F32R, o_hT)
    AT = at("AT", [T, NT, N], F32, o_hT)
    arow = at("arow", [T, 2, N], F32, o_hT + up(NT * N * 4))
    gws = at("gws", [128, C, D], F32, o_gw)
    gwT = at("gwT", [128, C, D], F32, o_gw + C * D * 4)
    assert o_gw + 2 * C * D * 4 <= o_q
    aggT = [at("aggT0", [128, C, CH[0][1]], F32, o_gw),
            at("aggT1", [128, C, CH[0][1]], F32, o_hT + up(NT * N * 4))]
    W_END = o_w + 4 * C * M * 4
    GC = CH[0][1]
    gf = at("gf", [128, MC, GC], F32, up(W_END))
    gl = at("gl", [128, MC, GC], F32R, up(W_END))
    gh = at("gh", [128, MC, GC], F32R, up(W_END) + MC * GC * 4)
    h2h = at("h2h", [128, C, GC], F32R, up(W_END) + 2 * MC * GC * 4)
    h2f = at("h2f", [128, C, GC], F32, o_ring)
    h2l = at("h2l", [128, C, GC], F32R, o_ring)
    assert W_END > o_qk and up(W_END) + (2 * MC + C) * GC * 4 <= o_hn
    fw = at("fw", [128, NB * C * D], F32, o_xn)
    EARLY = (o_w - o_xn + 2 * C * M * 4) // (C * D * 4)
    ys = at("ys", [ST, SLOT_TILES, D], F32, o_qk)
    yT = at("yT", [128, 2, C * ST], F32, o_qk + SLOT_TILES * D * 4)
    assert o_qk + (SLOT_TILES + 2) * D * 4 <= o_hn
    res = at("res", [ST, SLOT_TILES, D], F32, o_hn)
    assert SLOT_TILES * D <= 2 * NT * D and o_acc == o_hn + NT * D * 4

    def small(name, shape, dtype):
        size = 2 if dtype in (F16, BF16) else 4
        for n in shape[1:]:
            size *= n
        return at(name, shape, dtype, place(size))

    ident = small("ident", [128, 128], F32)
    ones = small("ones", [128, 128], F32)
    iota = small("iota", [T, NW], F16)
    dcol = small("dcol", [T, ET + PAD], F32)
    scol = small("scol", [T, ET + PAD], F32)
    o_p = top[0]
    pms = small("pms", [128, NF], F32)
    pml = at("pml", [128, NF], F32R, o_p)
    pmh = small("pmh", [128, NF], F32R)
    gbb = small("gbb", [T, D], F32)
    bvb = small("bvb", [T, D], F32)
    bpb = small("bpb", [T, D], F32)
    b2b = small("b2b", [T, D], F32)
    zb = small("zb", [128, N], F32)
    zt = small("zt", [T, 2 * NT], F32)
    zr = small("zr", [T, 2 * NT], F32)
    g1c = small("g1c", [128, C], F32)
    be1c = small("be1c", [128, C], F32)
    g2c = small("g2c", [128, C], F32)
    be2c = small("be2c", [128, C], F32)
    bqkc = small("bqkc", [128, 2 * C], F32)
    b1c = small("b1c", [128, MC], F32)
    alc = small("alc", [T, 1], F32)
    st = small("st", [T, NT, 6], F32)
    mv = small("mv", [T, NT, 2], F32)
    kse = small("kse", [DH + 1, 1], F32)
    half = small("half", [T, NT], F32)
    rstd = small("rstd", [T, NT], F32)
    nmr = small("nmr", [T, NT], F32)
    tmp = small("tmp", [T, NT], F32)
    sums = small("sums", [T, NT], F32)
    sqs = small("sqs", [T, NT], F32)
    nmean = small("nmean", [T, NT], F32)
    deg3 = small("deg3", [T, NT, 3], F32)
    deg = small("deg", [T, NT], F32)
    coef = small("coef", [T, NT], F32)
    bounds = small("bounds", [NT, 2], I32)
    nmax = small("nmax", [T, 4, 2], F32)
    token = small("token", [ST, SLOT_TILES], I32)
    tval = small("tval", [T, NT], F32)
    prow = small("prow", [T, 1], F32)
    starts = small("starts", [T, SLOT_TILES - 1], F32)
    exr = small("exr", [T, SLOT_TILES + 1], I32)
    edi = at("edi", [ER, 2, ROW * T], I32, o_x)
    edf = at("edf", [ER, 2, ROW * T], F32, o_x + 4000)
    mm = at("mm", [ER, 2, ROW], F32, o_x + 8000)
    mdiag = at("mdiag", [ER, 2 * ROW, ER], F32, o_x + 8032)
    rrow = at("rrow", [NT, 5, ET], F32, o_x + 9312)
    rsm = at("rsm", [NT, 8], F32, o_x + 12512)
    order = at("order", [NT, 2, ROW, ER], F32, o_x + 12544)
    steps = at("steps", [NT, 2, STEPS], F32, o_x + 13824)
    t0 = at("t0", [NT, 2], F32, o_x + 14272)
    mem = at("mem", [T, NT], F32, o_ring)
    cmp = at("cmp", [T, len(BINS), NT], F32, o_ring + 64)
    boh = at("boh", [T, NT + 1, NB], BF16, o_ring + 384)
    cnt = at("cnt", [T, 2, NB], F32, o_ring + 704)
    below = at("below", [T, NB, NB], F32, o_ring + 1376)
    tl = at("tl", [T, NT, NB], F32, o_ring + 1760)
    ctl = at("ctl", [T, 2, NB + 1], F32, o_ring + 2112)
    pr = at("pr", [T, NT, NB], F32, o_ring + 2208)
    posf = at("posf", [T, NT], F32, o_ring + 2560)
    slotc = at("slotc", [T, NB, SLOT_TILES], F32, o_ring + 2624)
    exf = at("exf", [T, SLOT_TILES + 1], F32, o_ring + 3200)
    ohb = at("ohb", [T, NT, ST], BF16, o_ring + 3296)
    inv = at("inv", [T, NT, 2, SLOT_TILES], BF16, o_ring + 5856)
    oha = at("oha", [T, NT, SLOT_TILES], F32, o_ring + 6560)
    past = at("past", [T, NT, SLOT_TILES - 1], F32, o_ring + 7264)
    tile_place = at("tile_place", [T, 2, NT], F32, o_ring + 7904)
    tsum = at("tsum", [ST, SLOT_TILES], F32, o_ring + 8000)
    jrow = small("jrow", [T, SLOT_TILES], F32)
    krow = small("krow", [T, NB], F32)
    lower = small("lower", [T, NB, NB], F32)
    many = small("many", [T, NT, NB], F32)
    trib = small("trib", [T, 128], BF16)
    onesb = small("onesb", [T, 128], BF16)
    assert top[0] <= nc.sbuf_usable_end, (top[0], nc.sbuf_usable_end)

    d_xn = nc.dram_tensor("xn_kept", (T, NT * D), F32, kind="Internal").ap()
    d_acc = nc.dram_tensor("acc_kept", (T, NT * D), F32, kind="Internal").ap()
    d_den = nc.dram_tensor("den_scratch", (PAIRS, 2 * N), F32, kind="Internal").ap()
    d_z = nc.dram_tensor("z_scratch", (PAIRS, 2 * N), F32, kind="Internal").ap()
    d_y = nc.dram_tensor("y_rows", (N + 1, D), F32, kind="Internal").ap()
    d_res = nc.dram_tensor("residual_rows", (N + 1, D), F32, kind="Internal").ap()

    with ExitStack() as ctx:
        P = [ctx.enter_context(nc.psum_tensor(f"bank{i}", [128, 512], F32)) for i in range(8)]

        def sem(name):
            return ctx.enter_context(nc.semaphore(name))

        psum_filled = sem("psum_filled")
        ffn_filled = {k: sem(k + "_filled") for k in ("yT", "ffn")}
        bank_read = [sem(f"bank_read{i}") for i in range(8)]
        ld = {k: sem("ld_" + k) for k in ("edges", "x", "gw", "bias", "pm", "wqk", "wv", "wp", "w1", "w2", "fw", "fw_late",
                                          "xn_out", "acc_out", "xn", "acc", "den", "dent", "z", "zb")}
        rows_out = {k: sem(k + "_rows_out") for k in ("y", "res", "zero")}
        ld_ys = [sem(f"ld_ys{i}") for i in range(SLOT_TILES)]
        ld_res = [sem(f"ld_res{i}") for i in range(SLOT_TILES)]
        out_written = sem("out_written")
        consts = sem("consts")
        zeros_ready = sem("zeros_ready")
        edge_tab = sem("edge_tab")
        bounds_ready = sem("bounds_ready")
        oh_ready = [sem(f"oh_ready{b}") for b in range(EH)]
        oh_used = [sem(f"oh_used{b}") for b in range(EH)]
        dve = sem("dve")
        pool = sem("pool")
        stats = sem("stats")
        rstd_ready = sem("rstd_ready")
        normed = sem("normed")
        acc_pre = sem("acc_pre")
        x_high = sem("x_high")
        x_low = sem("x_low")
        x_whole = sem("x_whole")
        at_high = sem("at_high")
        at_low = sem("at_low")
        at_used = sem("at_used")
        xnb_ready = sem("xnb_ready")
        max_ready = sem("max_ready")
        e_ready = [sem("ek_ready"), sem("eq_ready")]
        z_ready = sem("z_ready")
        attn_ready = sem("attn_ready")
        acc_x2 = sem("acc_x2")
        summed = sem("summed")
        squared = sem("squared")
        mean_ready = sem("mean_ready")
        act = sem("act")
        p_split = sem("p_split")
        wv_split = sem("wv_split")
        wqk_split = sem("wqk_split")
        h_split = sem("h_split")
        q_high = sem("q_high")
        w_high = sem("w_high")
        w_low = sem("w_low")
        h2_split = sem("h2_split")
        g_split = sem("g_split")
        boh_ready = sem("boh_ready")
        slots_ready = sem("slots_ready")
        inv_ready = sem("inv_ready")
        block = ctx.enter_context(nc.Block())

        def filled(eng, key):
            place_, bank, _ = plan.order[key]
            if key[0] in ffn_filled:
                eng.wait_ge(ffn_filled[key[0]], key[1] + 1)
            else:
                eng.wait_ge(psum_filled, place_ + 1)
            return P[bank]

        def slot_tiles(eng):
            eng.wait_ge(slots_ready, 1)
            return eng.value_load(exr[0:1, SLOT_TILES:SLOT_TILES + 1], min_val=SURE_TILES, max_val=SLOT_TILES)

        def if_used(eng, s, used):
            return eng.If(used > s) if s >= SURE_TILES else nullcontext()

        def read_out(ins, key):
            ins.then_inc(bank_read[plan.order[key][1]], 1)

        def evacuated(eng, key):
            _, bank, before = plan.order[key]
            eng.wait_ge(bank_read[bank], before + 1)

        @block.sync
        def _(sp):
            sp.dma_start(edi[:, 0, :], dst.rearrange("(a e) -> a e", a=ER)).then_inc(ld["edges"], 16)
            sp.dma_start(edi[:, 1, :], src.rearrange("(a e) -> a e", a=ER)).then_inc(ld["edges"], 16)
            sp.dma_start(acc[:, :, :], x.rearrange("(t p) d -> p t d", p=T)).then_inc(ld["x"], 16)
            sp.dma_start(alc[:, :], row_broadcast(alpha, T)).then_inc(ld["bias"], 16)
            for tile, row in ((gbb, gb), (bvb, bqkv[2 * D:3 * D]), (bpb, bp), (b2b, b2)):
                sp.dma_start(tile[:, :], row_broadcast(row, T)).then_inc(ld["bias"], 16)
            for tile, row in ((g1c, g1), (be1c, be1), (g2c, g2), (be2c, be2), (bqkc, bqkv[0:2 * D]), (b1c, b1)):
                sp.dma_start(tile[:, :], row.rearrange("(c p) -> p c", p=128),
                             allow_slow_non_contiguous=True).then_inc(ld["bias"], 16)
            sp.dma_start(gws[:, :, :], gW.rearrange("(c p) d -> p c d", p=128)).then_inc(ld["gw"], 16)
            for i in range(2):
                sp.dma_start(pms[DH * i:DH * i + DH, :], Pm).then_inc(ld["pm"], 16)
            sp.dma_start(wvs[:, :, :], Wqkv[:, 2 * D:3 * D].rearrange("(c p) n -> p c n", p=128)).then_inc(ld["wv"], 16)
            sp.wait_ge(zeros_ready, 1)
            for rows in (d_y, d_res):
                sp.dma_start(rows[N:N + 1, :], zb[0:1, 0:D]).then_inc(rows_out["zero"], 16)
            filled(sp, ("agg", 2, C - 1))
            sp.dma_start(wqk[:, :, :], Wqkv[:, 0:2 * D].rearrange("(c p) n -> p c n", p=128)).then_inc(ld["wqk"], 16)
            sp.wait_ge(x_whole, NT)
            sp.dma_start(d_xn, xn[:, :, :].rearrange("p t d -> p (t d)")).then_inc(ld["xn_out"], 16)
            evacuated(sp, ("gnn", NT - 1))
            sp.dma_start(d_acc, acc[:, :, :].rearrange("p t d -> p (t d)")).then_inc(ld["acc_out"], 16)
            for p in range(PAIRS):
                if p == PAIRS - 1:
                    sp.dma_start(xn[:, :, :].rearrange("p t d -> p (t d)"), d_xn).then_inc(ld["xn"], 16)
                    sp.dma_start(w1s[:, :].rearrange("p (c n) -> p c n", n=M),
                                 W1.rearrange("(c p) n -> p c n", p=128)).then_inc(ld["w1"], 16)
                    filled(sp, ("kv", p, 1))
                    sp.dma_start(wps[:, :, :], Wp.rearrange("(c p) n -> p c n", p=128)).then_inc(ld["wp"], 16)
                evacuated(sp, ("att", p, 1, 2))
                sp.dma_start(d_den[p:p + 1, :], den[0:1, :]).then_inc(ld["den"], 16)
                sp.wait_ge(ld["den"], 16 * (p + 1))
                sp.dma_start(zt[:, :], d_den[p, :].rearrange("(q j) -> q j", q=T)).then_inc(ld["dent"], 16)
                sp.wait_ge(z_ready, p + 1)
                sp.dma_start(d_z[p, :].rearrange("(q j) -> q j", q=T), zr[:, :]).then_inc(ld["z"], 16)
                sp.wait_ge(ld["z"], 16 * (p + 1))
                if p:
                    sp.wait_ge(attn_ready, p)
                for i in range(2):
                    sp.dma_start(zb[DH * i:DH * i + DH, :],
                                 row_broadcast(d_z[p, i * N:(i + 1) * N], DH)).then_inc(ld["zb"], 16)
            sp.dma_start(acc[:, :, :].rearrange("p t d -> p (t d)"), d_acc).then_inc(ld["acc"], 16)
            sp.dma_start(w2s[:, :].rearrange("p (c n) -> p c n", n=D),
                         W2.rearrange("(c p) n -> p c n", p=128)).then_inc(ld["w2"], 16)
            sp.wait_ge(acc_x2, NT)
            sp.wait_ge(normed, 3 * NT)
            fwv = FW.rearrange("k (c p) n -> p (k c) n", p=128)
            fws = fw[:, :].rearrange("p (k n) -> p k n", n=D)
            sp.dma_start(fws[:, 0:2 * C, :], fwv[:, 0:2 * C, :]).then_inc(ld["fw"], 16)
            filled(sp, ("up", 2, MC - 1))
            for k in range(2, EARLY):
                sp.dma_start(fws[:, k * C:(k + 1) * C, :], fwv[:, k * C:(k + 1) * C, :]).then_inc(ld["fw"], 16)
            for g, (t0_, tn) in enumerate(GROUPS):
                def rows(d):
                    return d[t0_ * T:(t0_ + tn) * T, :].rearrange("(t p) d -> p t d", p=T)

                evacuated(sp, ("down", t0_ + tn - 1))
                sp.dma_start(rows(d_res), acc[:, t0_:t0_ + tn, :]).then_inc(rows_out["res"], 16)
                sp.wait_ge(normed, 3 * NT + t0_ + tn)
                sp.dma_start(rows(d_y), hn[:, t0_:t0_ + tn, :]).then_inc(rows_out["y"], 16)
            sp.wait_ge(ld_ys[2], 16)
            sp.dma_start(fws[:, EARLY * C:, :], fwv[:, EARLY * C:, :]).then_inc(ld["fw_late"], 16)

        @block.gpsimd
        def _(gp):
            chain = [0]

            def link(ins):
                chain[0] += 1
                ins.then_inc(pool, 1)
                gp.wait_ge(pool, chain[0])

            nc.gpsimd.memset(ident[:, :], 0.0)
            nc.gpsimd.memset(onesb[:, :], 1.0)
            nc.gpsimd.memset(lower[:, :, :], 1.0)
            link(nc.gpsimd.memset(trib[:, :], 0.0))
            nc.gpsimd.affine_select(out=ident[:, :], in_=ident[:, :], compare_op=ALU.not_equal, fill=1.0, base=0,
                                    pattern=[[-1, 128]], channel_multiplier=1)
            nc.gpsimd.affine_select(out=trib[:, :], in_=trib[:, :], compare_op=ALU.is_ge, fill=1.0, base=0,
                                    pattern=[[-1, 128]], channel_multiplier=1)
            nc.gpsimd.affine_select(out=lower[:, :, :], in_=lower[:, :, :], compare_op=ALU.is_gt, fill=0.0, base=0,
                                    pattern=[[1, NB], [-1, NB]], channel_multiplier=0)
            nc.gpsimd.memset(ones[:, :], 1.0)
            small_ok = {"allow_small_or_imprecise_dtypes": True}
            nc.gpsimd.iota(krow[:, :], pattern=[[1, NB]], base=0, channel_multiplier=0, **small_ok)
            nc.gpsimd.iota(many[:, :, :], pattern=[[ST, NT], [0, NB]], base=0, channel_multiplier=0, **small_ok)
            nc.gpsimd.iota(iota[:, :], pattern=[[1, NW]], base=0, channel_multiplier=0, **small_ok)
            nc.gpsimd.iota(jrow[:, :], pattern=[[1, SLOT_TILES]], base=0, channel_multiplier=0, **small_ok)
            nc.gpsimd.iota(order[:, 0], pattern=[[1, ROW], [ROW, ER]], base=1, channel_multiplier=0, **small_ok)
            nc.gpsimd.iota(order[:, 1], pattern=[[-1, ROW], [-ROW, ER]], base=ET, channel_multiplier=0, **small_ok)
            nc.gpsimd.iota(steps[:, 0, :], pattern=[[EH, STEPS]], base=0, channel_multiplier=0, **small_ok)
            nc.gpsimd.iota(tval[:, :], pattern=[[-1, NT]], base=NT, channel_multiplier=0, **small_ok)
            nc.gpsimd.iota(prow[:, :], pattern=[[1, 1]], base=0, channel_multiplier=1, **small_ok)
            nc.gpsimd.iota(starts[:, :], pattern=[[ST, SLOT_TILES - 1]], base=ST, channel_multiplier=0, **small_ok)
            nc.gpsimd.iota(t0[:, 0:1], pattern=[[1, 1]], base=0, channel_multiplier=T, **small_ok)
            nc.gpsimd.iota(t0[:, 1:2], pattern=[[1, 1]], base=T - 1, channel_multiplier=T, **small_ok)
            link(nc.gpsimd.memset(kse[:, :], 0.0))
            link(nc.gpsimd.memset(kse[DH:DH + 1, :], NF * KSUM_EPS / 16))
            nc.gpsimd.memset(half[:, :], -0.5).then_inc(consts, 1)

            def rstd_by_sums(n, links):
                gp.wait_ge(summed, n)
                if n > 1:
                    gp.wait_ge(normed, NT * (n - 1))
                nc.gpsimd.tensor_scalar(nmean[:, :], sums[:, :], -1.0 / D, None, ALU.mult).then_inc(mean_ready, 1)
                gp.wait_ge(squared, n)
                link(nc.gpsimd.tensor_scalar(tmp[:, :], sqs[:, :], 1.0 / D, EPS, ALU.mult, ALU.add))
                link(nc.gpsimd.tensor_tensor(rstd[:, :], tmp[:, :], half[:, :], ALU.pow))
                nc.gpsimd.tensor_tensor(nmr[:, :], nmean[:, :], rstd[:, :], ALU.mult).then_inc(rstd_ready, 3)

            def rstd_by_stats(n, g):
                t0_, tn = GROUPS[g]
                s_ = slice(t0_, t0_ + tn)
                gp.wait_ge(stats, 3 * (n - 3) + g + 1)
                gp.wait_ge(normed, NT * (n - 1))
                nc.gpsimd.tensor_scalar(nmean[:, s_], mv[:, s_, 0], -1.0, None, ALU.mult)
                link(nc.gpsimd.tensor_scalar(tmp[:, s_], mv[:, s_, 1], EPS, None, ALU.add))
                link(nc.gpsimd.tensor_tensor(rstd[:, s_], tmp[:, s_], half[:, s_], ALU.pow))
                nc.gpsimd.tensor_tensor(nmr[:, s_], nmean[:, s_], rstd[:, s_], ALU.mult).then_inc(rstd_ready, 1)

            rstd_by_sums(1, link)
            rstd_by_sums(2, link)
            gp.wait_ge(ld["bias"], 16 * 11)
            link(nc.gpsimd.tensor_scalar(gbb[:, :], gbb[:, :], alc[:, 0:1], None, ALU.mult))
            for t in range(NT):
                link(nc.gpsimd.tensor_tensor(acc[:, t, :], acc[:, t, :], xn[:, t, :], ALU.add))
                add_b = nc.gpsimd.tensor_tensor(acc[:, t, :], acc[:, t, :], gbb[:, :], ALU.add)
            add_b.then_inc(acc_pre, 1)
            gp.wait_ge(x_high, 1)
            nc.gpsimd.tensor_tensor(xl[:, :, :], xn[:, :, :], xh[:, :, :].bitcast(F32), ALU.subtract).then_inc(x_low, 1)

            def split(whole, high, low):
                link(nc.gpsimd.tensor_copy(high, whole))
                return nc.gpsimd.tensor_tensor(low, whole, high.bitcast(F32), ALU.subtract)

            gp.wait_ge(ld["pm"], 32)
            split(pms[:, :], pmh[:, :], pml[:, :]).then_inc(p_split, 1)
            gp.wait_ge(ld["wv"], 16)
            filled(gp, ("A", NT - 1, 2))
            split(wvs[:, :, :], wvh[:, :, :], wvl[:, :, :]).then_inc(wv_split, 1)
            filled(gp, ("agg", 2, C - 1))
            for t in range(NT):
                nc.gpsimd.tensor_tensor(xn[:, t, :], xl[:, t, :].bitcast(F32), xh[:, t, :].bitcast(F32),
                                        ALU.add).then_inc(x_whole, 1)
            gp.wait_ge(ld["wqk"], 16)
            gp.wait_ge(ld["acc_out"], 16)
            split(wqk[:, :, :], wqkh[:, :, :], wqkl[:, :, :]).then_inc(wqk_split, 1)
            gp.wait_ge(ld["xn"], 16)
            for t in range(NT):
                add_b = nc.gpsimd.tensor_tensor(xn[:, t, :], xn[:, t, :], bpb[:, :], ALU.add)
            add_b.then_inc(xnb_ready, 1)
            gp.wait_ge(w_high, 1)
            nc.gpsimd.tensor_tensor(w1l[:, :], w1s[:, :], w1h[:, :].bitcast(F32), ALU.subtract).then_inc(w_low, 1)
            gp.wait_ge(ld["acc"], 16)
            for g in range(3):
                rstd_by_stats(3, g)
            for t in range(NT):
                if t == 2:
                    gp.wait_ge(w_high, 2)
                    nc.gpsimd.tensor_tensor(w2l[:, :], w2s[:, :], w2h[:, :].bitcast(F32),
                                            ALU.subtract).then_inc(w_low, 1)
                evacuated(gp, ("proj", t))
                link(nc.gpsimd.tensor_tensor(acc[:, t, :], acc[:, t, :], xn[:, t, :], ALU.add))
                nc.gpsimd.tensor_tensor(acc[:, t, :], acc[:, t, :], b2b[:, :], ALU.add).then_inc(acc_x2, 1)
            for g in range(3):
                rstd_by_stats(4, g)
            evacuated(gp, "tokens")
            gp.wait_ge(rows_out["zero"], 32)
            gp.wait_ge(rows_out["y"], 16 * 3)

            def fetch(rows, to, s, signal, used=None):
                with if_used(gp, s, used):
                    gp.indirect_dma_start(out=to[:, s, :], out_offset=None, in_=rows,
                                          in_offset=bass.IndirectOffsetOnAxis(ap=token[:, s:s + 1], axis=0)
                                          ).then_inc(signal[s], 16)

            ahead = 3
            for s in range(ahead):
                fetch(d_y, ys, s, ld_ys)
            used = slot_tiles(gp)
            gp.wait_ge(rows_out["res"], 16 * 3)
            for s in range(ahead - 1):
                fetch(d_res, res, s, ld_res)
            for s in range(SLOT_TILES):
                if s + ahead < SLOT_TILES:
                    fetch(d_y, ys, s + ahead, ld_ys, used)
                if s + ahead - 1 < SLOT_TILES:
                    fetch(d_res, res, s + ahead - 1, ld_res, used)
                with if_used(gp, s, used):
                    evacuated(gp, ("ffn", s))
                    gp.indirect_dma_start(out=out, out_offset=bass.IndirectOffsetOnAxis(ap=token[:, s:s + 1], axis=0),
                                          in_=res[:, s, :], in_offset=None, bounds_check=N - 1, oob_is_err=False
                                          ).then_inc(out_written, 16)
            written = gp.alloc_register("pool_written")
            gp.reg_mul(written, used, 16)
            gp.wait_ge(out_written, written)

        @block.scalar
        def _(sc):
            def normalise(rows, to, n, g):
                sc.wait_ge(rstd_ready, 3 * (n - 1) + g + 1)
                for t in tiles(g):
                    nc.scalar.activation(to[:, t, :], rows[:, t, :], ACT.Identity, scale=rstd[:, t:t + 1],
                                         bias=nmr[:, t:t + 1]).then_inc(normed, 1)

            def square_rows(rows, to, n):
                sc.wait_ge(mean_ready, n)
                for t in range(NT):
                    ins = nc.scalar.activation(to[:, t, :], rows[:, t, :], ACT.Square, bias=nmean[:, t:t + 1],
                                               accum_out=sqs[:, t:t + 1])
                ins.then_inc(squared, 1)

            def sum_rows(rows, to, n):
                if n > 1:
                    sc.wait_ge(normed, NT * (n - 1))
                for t in range(NT):
                    ins = nc.scalar.activation(to[:, t, :], rows[:, t, :], ACT.Identity, accum_out=sums[:, t:t + 1])
                ins.then_inc(summed, 1)

            def counts_by_src(t):
                for j, (s0, sn) in enumerate(GROUPS):
                    bank = filled(sc, ("AT", t, j))
                    read_out(nc.scalar.copy(AT[:, s0:s0 + sn, t * T:(t + 1) * T],
                                            bank[0:T, 0:sn * T].rearrange("p (s d) -> p s d", d=T)), ("AT", t, j))

            sc.wait_ge(ld["x"], 16)
            sum_rows(acc, xn, 1)
            square_rows(acc, xn, 1)
            for t in range(NT):
                if t >= 2:
                    filled(sc, ("AT", t - 2, 2))
                for j, (c0, cn) in enumerate(CH):
                    bank = filled(sc, ("A", t, j))
                    read_out(nc.scalar.activation(arow[:, t % 2, c0:c0 + cn], bank[0:T, 0:cn], ACT.Identity,
                                                  accum_out=deg3[:, t, j:j + 1]), ("A", t, j))
                if t >= 1:
                    counts_by_src(t - 1)
                if t == 0:
                    for g in range(3):
                        normalise(acc, xn, 1, g)
                if t == 1:
                    sum_rows(xn, hn, 2)
                if t == 2:
                    square_rows(xn, hn, 2)
                if t == 3:
                    sc.wait_ge(squared, 2)
                    nc.scalar.copy(xh[:, :, :], xn[:, :, :]).then_inc(x_high, 1)
            counts_by_src(NT - 1)
            for k in range(C):
                bank = filled(sc, ("gWT", k))
                read_out(nc.scalar.copy(gwT[:, k, :], bank[:, :]), ("gWT", k))
            evacuated(sc, ("AT", NT - 1, 2))
            for n, (c0, cn) in enumerate(CH):
                for s in range(NT):
                    if n:
                        sc.wait_ge(at_low, NT * (n - 1) + s + 1)
                    if n and s < NT - 1:
                        sc.wait_ge(at_used, (NT - 1) * (n - 1) + s + 1)
                    elif n:
                        filled(sc, ("agg", n - 1, C - 1))
                    nc.scalar.copy(ath[:, s, 0:cn], AT[:, s, c0:c0 + cn]).then_inc(at_high, 1)
            for g in range(3):
                sc.wait_ge(x_whole, tiles(g)[-1] + 1)
                normalise(xn, hn, 2, g)
            filled(sc, ("gnn", NT - 1))
            sc.wait_ge(ld["bias"], 16 * 11)
            sc.wait_ge(ld["xn_out"], 16)
            for j, (c0, cn) in enumerate(CH):
                for c in range(C):
                    bank = filled(sc, ("hT", c, j))
                    nc.scalar.activation(hTh[:, c, c0:c0 + cn], bank[:, 0:cn], ACT.Identity,
                                         scale=g1c[:, c:c + 1], bias=be1c[:, c:c + 1])
                    read_out(nc.scalar.activation(hTf[:, c, c0:c0 + cn], bank[:, 0:cn], ACT.Identity,
                                                  scale=g1c[:, c:c + 1], bias=be1c[:, c:c + 1]), ("hT", c, j))

            def round_qk(p):
                for n, w in qk_groups:
                    c0, cn = CH[n]
                    bank = filled(sc, ("qk", p, n, w))
                    for i in range(2):
                        r = slice(DH * i, DH * i + DH)
                        ins = nc.scalar.activation(qkT[w][r, i, c0:c0 + cn], bank[r, 0:cn], ACT.Identity,
                                                   bias=bqkc[r, w * C + p:w * C + p + 1])
                    ins.then_inc(q_high, 1)

            round_qk(0)
            for p in range(PAIRS):
                for t in range(NT):
                    for w, name in enumerate(("kf", "qf")):
                        g = 2 * (p * NT + t) + w
                        bank = filled(sc, (name, p, t))
                        sc.wait_ge(max_ready, g + 1)
                        if t >= 2:
                            filled(sc, ("qT", p, t - 2))
                        elif p:
                            filled(sc, ("qT", p - 1, NT - 2 + t))
                        for i in range(2):
                            e = nc.scalar.activation(ering[:, 2 * (t % 2) + w, i * NF:(i + 1) * NF],
                                                     bank[0:T, i * NF:(i + 1) * NF], ACT.Exp,
                                                     bias=nmax[:, g % 4, i:i + 1])
                            if i:
                                read_out(e, (name, p, t))
                if p < PAIRS - 1:
                    round_qk(p + 1)
                if p:
                    sc.wait_ge(ld["den"], 16 * p)
                for i in range(2):
                    for n, (c0, cn) in enumerate(CH):
                        bank = filled(sc, ("att", p, i, n))
                        nc.scalar.copy(attT[DH * i:DH * i + DH, p, c0:c0 + cn], bank[0:DH, 0:cn])
                        read_out(nc.scalar.copy(den[0:1, i * N + c0:i * N + c0 + cn], bank[DH:DH + 1, 0:cn]),
                                 ("att", p, i, n))
            def second_rows(g):
                _, cn = CH[g]
                if g:
                    filled(sc, ("up", g - 1, MC - 1))
                for c in range(C):
                    bank = filled(sc, ("h2T", c, g))
                    nc.scalar.activation(h2h[:, c, 0:cn], bank[:, 0:cn], ACT.Identity, scale=g2c[:, c:c + 1],
                                         bias=be2c[:, c:c + 1])
                    read_out(nc.scalar.activation(h2f[:, c, 0:cn], bank[:, 0:cn], ACT.Identity,
                                                  scale=g2c[:, c:c + 1], bias=be2c[:, c:c + 1]), ("h2T", c, g))

            normalise(xn, hn, 3, 0)
            second_rows(0)
            normalise(xn, hn, 3, 1)
            normalise(xn, hn, 3, 2)
            for n, (c0, cn) in enumerate(CH):
                if n:
                    filled(sc, ("down", GROUPS[n][0] - 1))
                for m in range(MC):
                    bank = filled(sc, ("up", n, m))
                    read_out(nc.scalar.activation(gf[:, m, 0:cn], bank[:, 0:cn], ACT.Gelu,
                                                  bias=b1c[:, m:m + 1]), ("up", n, m))
                if n < 2:
                    second_rows(n + 1)
            for g in range(3):
                normalise(acc, hn, 4, g)
            used = slot_tiles(sc)
            for s in range(SLOT_TILES):
                with if_used(sc, s, used):
                    bank = filled(sc, ("yT", s))
                    if s >= 2:
                        filled(sc, ("ffn", s - 2))
                    read_out(nc.scalar.copy(yT[:, s % 2, :], bank[:, :]), ("yT", s))

        @block.vector
        def _(ve):
            chain = [0]

            def link(ins):
                chain[0] += 1
                ins.then_inc(dve, 1)
                ve.wait_ge(dve, chain[0])

            def statistics(rows, g):
                for t in tiles(g):
                    ins = nc.vector.bn_stats(st[:, t, :], rows[:, t, :])
                link(ins)
                for t in tiles(g):
                    ins = nc.vector.bn_aggr(mv[:, t, :], st[:, t, :])
                ins.then_inc(stats, 1)

            nc.vector.memset(zb[0:1, 0:D], 0.0).then_inc(zeros_ready, 1)
            ve.wait_ge(ld["edges"], 32)
            link(nc.vector.tensor_copy(edf[:, :, :], edi[:, :, :]))
            by_tile = edf[:, 0, :].rearrange("a (b e) -> a b e", b=ROW)
            nc.vector.tensor_reduce(out=mm[:, 0, :], in_=by_tile, op=ALU.min, axis=AX)
            link(nc.vector.tensor_reduce(out=mm[:, 1, :], in_=by_tile, op=ALU.max, axis=AX))
            ve.wait_ge(consts, 1)
            nc.vector.tensor_tensor(mdiag[:, :, :], ident[0:ER, 0:ER].unsqueeze(1).to_broadcast([ER, 2 * ROW, ER]),
                                    mm[:, :, :].rearrange("a w b -> a (w b)").unsqueeze(2)
                                    .to_broadcast([ER, 2 * ROW, ER]), ALU.mult).then_inc(edge_tab, 1)
            bank = filled(ve, "edge_cols")
            cols = bank[0:T, 0:2 * ET].rearrange("p (w b a) -> p w a b", w=2, b=ROW)
            nc.vector.memset(dcol[:, ET:], -1.0)
            nc.vector.memset(scol[:, ET:], -1.0)
            nc.vector.tensor_copy(dcol[:, 0:ET].rearrange("p (a b) -> p a b", b=ROW), cols[:, 0])
            read_out(nc.vector.tensor_copy(scol[:, 0:ET].rearrange("p (a b) -> p a b", b=ROW), cols[:, 1]), "edge_cols")
            bank = filled(ve, "edge_range")
            nc.vector.tensor_scalar(rrow[:, 0, :], bank[0:NT, 0:ET], t0[:, 1:2], None, ALU.is_le)
            read_out(nc.vector.tensor_scalar(rrow[:, 1, :], bank[0:NT, ET:2 * ET], t0[:, 0:1], None, ALU.is_ge),
                     "edge_range")
            evacuated(ve, "edge_range")
            link(nc.vector.tensor_tensor(rrow[:, 2, :], rrow[:, 0, :], rrow[:, 1, :], ALU.mult))
            nc.vector.tensor_tensor(rrow[:, 3, :], rrow[:, 2, :], order[:, 0].rearrange("t b a -> t (b a)"), ALU.mult)
            link(nc.vector.tensor_tensor(rrow[:, 4, :], rrow[:, 2, :], order[:, 1].rearrange("t b a -> t (b a)"),
                                         ALU.mult))
            nc.vector.reduce_max(rsm[:, 0:1], rrow[:, 3, :], AX)
            link(nc.vector.reduce_max(rsm[:, 1:2], rrow[:, 4, :], AX))
            link(nc.vector.scalar_tensor_tensor(out=rsm[:, 2:3], in0=rsm[:, 0:1], scalar=-float(ET), in1=rsm[:, 1:2],
                                                op0=ALU.add, op1=ALU.add))
            link(nc.vector.tensor_scalar(steps[:, 1, :], steps[:, 0, :], rsm[:, 2:3], None, ALU.is_lt))
            link(nc.vector.reduce_sum(rsm[:, 3:4], steps[:, 1, :], AX))
            link(nc.vector.tensor_scalar(rsm[:, 4:5], rsm[:, 3:4], 3.0, None, ALU.max))
            link(nc.vector.tensor_scalar(rsm[:, 6:7], rsm[:, 4:5], float(EH), -float(PAD), ALU.mult, ALU.add))
            link(nc.vector.tensor_tensor(rsm[:, 5:6], rsm[:, 6:7], rsm[:, 1:2], ALU.max))
            nc.vector.tensor_scalar(bounds[:, 0:1], rsm[:, 5:6], -1.0, float(ET), ALU.mult, ALU.add)
            nc.vector.tensor_copy(bounds[:, 1:2], rsm[:, 4:5]).then_inc(bounds_ready, 1)
            ve.wait_ge(bounds_ready, 1)
            evacuated(ve, "edge_cols")
            turn, place_ = ve.alloc_register("dve_turn"), ve.alloc_register("dve_place")
            ve.reg_mov(turn, 0)
            for t in range(NT):
                ve.reg_load(place_, bounds[t:t + 1, 0:1])
                count = ve.value_load(bounds[t:t + 1, 1:2], min_val=3, max_val=STEPS)
                with ve.Fori(0, count) as _i:
                    ve.reg_add(turn, turn, 1)
                    tile_ = ve.snap(place_, min_val=0, max_val=ET + PAD - EH)
                    for b in range(EH):
                        ve.wait_ge(oh_used[b], turn)
                        nc.vector.tensor_scalar(ohd[:, b, :], iota[:, 0:128], float(t * T),
                                                dcol[:, bass.ds(tile_ + b, 1)], ALU.add, ALU.is_equal)
                        nc.vector.tensor_scalar(ohs[b][:, :], iota[:, :], scol[:, bass.ds(tile_ + b, 1)], None,
                                                ALU.is_equal).then_inc(oh_ready[b], 1)
                    ve.reg_add(place_, place_, EH)

            def gnn_rows(t):
                bank = filled(ve, ("gnn", t))
                read_out(nc.vector.scalar_tensor_tensor(out=acc[:, t, :], in0=bank[0:T, :], scalar=coef[:, t:t + 1],
                                                        in1=acc[:, t, :], op0=ALU.mult, op1=ALU.add), ("gnn", t))

            evacuated(ve, ("A", NT - 1, 2))
            link(nc.vector.reduce_sum(deg[:, :], deg3[:, :, :], AX))
            link(nc.vector.tensor_scalar(deg[:, :], deg[:, :], 1.0, None, ALU.max))
            link(nc.vector.reciprocal(coef[:, :], deg[:, :]))
            ve.wait_ge(ld["bias"], 16 * 11)
            link(nc.vector.tensor_scalar(coef[:, :], coef[:, :], alc[:, 0:1], None, ALU.mult))
            ve.wait_ge(acc_pre, 1)

            def counts_rest(n):
                c0, cn = CH[n]
                for s in range(NT):
                    ve.wait_ge(at_high, n * NT + s + 1)
                    nc.vector.tensor_tensor(atl[:, s, c0:c0 + cn], AT[:, s, c0:c0 + cn],
                                            ath[:, s, 0:cn].bitcast(F32), ALU.subtract).then_inc(at_low, 1)

            counts_rest(0)
            for n, (c0, cn) in enumerate(CH):
                if n < 2:
                    counts_rest(n + 1)
                if n == 2:
                    filled(ve, ("gnn", GROUPS[1][0] - 1))
                filled(ve, ("gWT", C - 1))
                for c in range(C):
                    bank = filled(ve, ("agg", n, c))
                    read_out(nc.vector.tensor_copy(aggT[n % 2][:, c, 0:cn], bank[:, 0:cn]), ("agg", n, c))
                for t in (tiles(n - 1) if n else ()):
                    gnn_rows(t)
            for t in tiles(2):
                gnn_rows(t)
            nc.vector.memset(v65[:, :, :, DH:DH + 1], 1.0)
            for j, (c0, cn) in enumerate(CH):
                for c in range(C):
                    evacuated(ve, ("hT", c, j))
                    nc.vector.tensor_tensor(hTl[:, c, c0:c0 + cn], hTf[:, c, c0:c0 + cn],
                                            hTh[:, c, c0:c0 + cn].bitcast(F32), ALU.subtract).then_inc(h_split, 1)
            for t in range(NT):
                bank = filled(ve, ("v", t))
                read_out(nc.vector.tensor_tensor(v65[:, t, :, 0:DH],
                                                 bank[0:T, :].rearrange("p (h e) -> p h e", e=DH),
                                                 bvb[:, :].rearrange("p (h e) -> p h e", e=DH), ALU.add), ("v", t))

            def reciprocals(p):
                ve.wait_ge(ld["dent"], 16 * (p + 1))
                nc.vector.reciprocal(zr[:, :], zt[:, :]).then_inc(z_ready, 1)

            def normalise_attention(p):
                ve.wait_ge(ld["zb"], 32 * (p + 1))
                nc.vector.tensor_tensor(attT[:, p, :], attT[:, p, :], zb[:, :], ALU.mult).then_inc(attn_ready, 1)

            def q_features_by_feature(p, t):
                bank = filled(ve, ("qT", p, t))
                read_out(nc.vector.tensor_copy(eqT[:, :, t * T:(t + 1) * T],
                                               bank[:, 0:2 * FC * T].rearrange("p (f t) -> p f t", t=T)), ("qT", p, t))

            def qk_rest(p, groups):
                for n, w in groups:
                    c0, cn = CH[n]
                    ve.wait_ge(q_high, p * len(qk_groups) + qk_groups.index((n, w)) + 1)
                    bank = filled(ve, ("qk", p, n, w))
                    for i in range(2):
                        r, o = slice(DH * i, DH * i + DH), slice(DH * (1 - i), DH * (1 - i) + DH)
                        ins = nc.vector.scalar_tensor_tensor(
                            out=qkT[w][o, i, c0:c0 + cn], in0=bank[r, 0:cn], scalar=bqkc[r, w * C + p:w * C + p + 1],
                            in1=qkT[w][r, i, c0:c0 + cn].bitcast(F32), op0=ALU.add, op1=ALU.subtract)
                    read_out(ins, ("qk", p, n, w))

            qk_rest(0, qk_groups)
            for p in range(PAIRS):
                for t in range(NT):
                    for w, name in enumerate(("kf", "qf")):
                        g = 2 * (p * NT + t) + w
                        bank = filled(ve, (name, p, t))
                        if g >= 4:
                            q = g - 4
                            evacuated(ve, (("kf", "qf")[q % 2], q // 2 // NT, q // 2 % NT))
                        nc.vector.tensor_reduce(out=nmax[:, g % 4, :],
                                                in_=bank[0:T, :].rearrange("p (i f) -> p i f", i=2), op=ALU.max,
                                                axis=AX, negate=True).then_inc(max_ready, 1)
                    if t >= 1:
                        q_features_by_feature(p, t - 1)
                    if p and t == 4:
                        reciprocals(p - 1)
                    if p and t == NT - 1:
                        normalise_attention(p - 1)
                q_features_by_feature(p, NT - 1)
                for i in range(2):
                    bank = filled(ve, ("kv", p, i))
                    read_out(nc.vector.tensor_scalar(kvT[:, i, :], bank[0:DH + 1, 0:NF], kse[:, 0:1], None, ALU.add),
                             ("kv", p, i))
                if p < PAIRS - 1:
                    qk_rest(p + 1, before_kvT)
                bank = filled(ve, ("kvT", p))
                read_out(nc.vector.tensor_copy(kv[:, :, :],
                                               bank[:, 0:2 * FC * (DH + 1)].rearrange("p (f e) -> p f e", e=DH + 1)),
                         ("kvT", p))
                if p < PAIRS - 1:
                    qk_rest(p + 1, after_kvT)
            ve.wait_ge(ld["w1"], 16)
            nc.vector.tensor_copy(w1h[:, :], w1s[:, :]).then_inc(w_high, 1)
            reciprocals(PAIRS - 1)
            normalise_attention(PAIRS - 1)
            ve.wait_ge(xnb_ready, 1)
            for g in range(3):
                for t in tiles(g):
                    bank = filled(ve, ("proj", t))
                    read_out(nc.vector.tensor_tensor(xn[:, t, :], bank[0:T, :], xn[:, t, :], ALU.add), ("proj", t))
                evacuated(ve, ("proj", tiles(g)[-1]))
                statistics(xn, g)

            def second_rest(g):
                _, cn = CH[g]
                for c in range(C):
                    evacuated(ve, ("h2T", c, g))
                    nc.vector.tensor_tensor(h2l[:, c, 0:cn], h2f[:, c, 0:cn], h2h[:, c, 0:cn].bitcast(F32),
                                            ALU.subtract).then_inc(h2_split, 1)

            second_rest(0)
            ve.wait_ge(ld["w2"], 16)
            nc.vector.tensor_copy(w2h[:, :], w2s[:, :]).then_inc(w_high, 1)
            for n, (c0, cn) in enumerate(CH):
                for m in range(MC):
                    evacuated(ve, ("up", n, m))
                    link(nc.vector.tensor_copy(gh[:, m, 0:cn], gf[:, m, 0:cn]))
                    nc.vector.tensor_tensor(gl[:, m, 0:cn], gf[:, m, 0:cn], gh[:, m, 0:cn].bitcast(F32),
                                            ALU.subtract).then_inc(g_split, 1)
                if n < 2:
                    second_rest(n + 1)
                for t in tiles(n):
                    ve.wait_ge(acc_x2, t + 1)
                    bank = filled(ve, ("down", t))
                    read_out(nc.vector.tensor_tensor(acc[:, t, :], bank[0:T, :], acc[:, t, :], ALU.add),
                             ("down", t))
                evacuated(ve, ("down", tiles(n)[-1]))
                statistics(acc, n)
            ve.wait_ge(normed, 4 * NT)
            for j, edge in enumerate(BINS):
                ins = nc.vector.tensor_scalar(cmp[:, j, :], hn[:, :, 0], edge, None, ALU.is_gt)
            link(ins)
            link(nc.vector.reduce_sum(mem[:, :], cmp[:, :, :].rearrange("p j t -> p t j"), AX))
            nc.vector.memset(boh[:, NT, :], 0.0)
            nc.vector.tensor_tensor(boh[:, 0:NT, :], mem[:, :].unsqueeze(2).to_broadcast([T, NT, NB]),
                                    krow[:, :].unsqueeze(1).to_broadcast([T, NT, NB]), ALU.is_equal
                                    ).then_inc(boh_ready, 1)
            bank = filled(ve, "rank")
            link(nc.vector.tensor_copy(cnt[:, 0, :], bank[0:T, NT * NB:(NT + 1) * NB]))
            link(nc.vector.tensor_tensor(tl[:, :, :], cnt[:, 0, :].unsqueeze(1).to_broadcast([T, NT, NB]),
                                         many[:, :, :], ALU.is_gt))
            link(nc.vector.reduce_sum(cnt[:, 1, :], tl[:, :, :].rearrange("p j k -> p k j"), AX))
            link(nc.vector.tensor_tensor(below[:, :, :], cnt[:, 1, :].unsqueeze(1).to_broadcast([T, NB, NB]),
                                         lower[:, :, :], ALU.mult))
            link(nc.vector.reduce_sum(ctl[:, 0, 0:NB], below[:, :, :], AX))
            link(nc.vector.tensor_scalar(ctl[:, 1, 0:NB], ctl[:, 0, 0:NB], float(ST), None, ALU.mult))
            read_out(nc.vector.tensor_tensor(pr[:, :, :], bank[0:T, 0:NT * NB].rearrange("p (t k) -> p t k", k=NB),
                                             ctl[:, 1, 0:NB].unsqueeze(1).to_broadcast([T, NT, NB]), ALU.add), "rank")
            evacuated(ve, "rank")
            link(nc.vector.tensor_tensor(pr[:, :, :], pr[:, :, :], boh[:, 0:NT, :], ALU.mult))
            link(nc.vector.reduce_sum(posf[:, :], pr[:, :, :], AX))
            link(nc.vector.tensor_tensor(past[:, :, :],
                                         posf[:, :].unsqueeze(2).to_broadcast([T, NT, SLOT_TILES - 1]),
                                         starts[:, :].unsqueeze(1).to_broadcast([T, NT, SLOT_TILES - 1]), ALU.is_ge))
            link(nc.vector.reduce_sum(tile_place[:, 0, :], past[:, :, :], AX))
            nc.vector.tensor_tensor(oha[:, :, :],
                                    tile_place[:, 0, :].unsqueeze(2).to_broadcast([T, NT, SLOT_TILES]),
                                    jrow[:, :].unsqueeze(1).to_broadcast([T, NT, SLOT_TILES]), ALU.is_equal)
            link(nc.vector.scalar_tensor_tensor(out=tile_place[:, 1, :], in0=tile_place[:, 0, :], scalar=-float(ST),
                                                in1=posf[:, :], op0=ALU.mult, op1=ALU.add))
            nc.vector.tensor_tensor(inv[:, :, 0, :], oha[:, :, :],
                                    tval[:, :].unsqueeze(2).to_broadcast([T, NT, SLOT_TILES]), ALU.mult)
            nc.vector.tensor_scalar(inv[:, :, 1, :], oha[:, :, :], prow[:, 0:1], None, ALU.mult)
            nc.vector.tensor_tensor(ohb[:, :, :], iota[:, 0:ST].unsqueeze(1).to_broadcast([T, NT, ST]),
                                    tile_place[:, 1, :].unsqueeze(2).to_broadcast([T, NT, ST]), ALU.is_equal
                                    ).then_inc(inv_ready, 1)
            link(nc.vector.tensor_tensor(slotc[:, :, :], jrow[:, :].unsqueeze(1).to_broadcast([T, NB, SLOT_TILES]),
                                         ctl[:, 0, 0:NB].unsqueeze(2).to_broadcast([T, NB, SLOT_TILES]), ALU.is_ge))
            nc.vector.reduce_sum(exf[:, 0:SLOT_TILES], slotc[:, 1:NB, :].rearrange("p k j -> p j k"), AX)
            link(nc.vector.reduce_sum(exf[:, SLOT_TILES:SLOT_TILES + 1], cnt[:, 1, :], AX))
            nc.vector.tensor_copy(exr[:, :], exf[:, :]).then_inc(slots_ready, 1)
            bank = filled(ve, "tokens")
            nt_p = bank[:, 0:2 * SLOT_TILES].rearrange("q (w j) -> q w j", w=2)
            link(nc.vector.tensor_scalar(tsum[:, :], nt_p[:, 0], -float(T), float(N), ALU.mult, ALU.add))
            read_out(nc.vector.tensor_tensor(token[:, :], tsum[:, :], nt_p[:, 1], ALU.add), "tokens")
            used = slot_tiles(ve)
            for s in range(SLOT_TILES):
                with if_used(ve, s, used):
                    bank = filled(ve, ("ffn", s))
                    ve.wait_ge(ld_res[s], 16)
                    read_out(nc.vector.tensor_tensor(res[:, s, :], bank[:, :], res[:, s, :], ALU.add), ("ffn", s))

        @block.tensor
        def _(pe):
            def begin(key):
                _, bank, before = plan.order[key]
                if before:
                    pe.wait_ge(bank_read[bank], before)
                return P[bank]

            def product(out_, pairs):
                for n, (a, b) in enumerate(pairs):
                    ins = nc.tensor.matmul(out_, a, b, start=(n == 0), stop=(n == len(pairs) - 1))
                return ins

            def split_product(out_, high_low, start=True, stop=True):
                n = 3 * len(high_low)
                for i, (ah, al, bh, bl) in enumerate(high_low):
                    for j, (a, b) in enumerate(((ah, bh), (ah, bl), (al, bh))):
                        ins = nc.tensor.matmul(out_, a, b, start=(start and i + j == 0),
                                               stop=(stop and 3 * i + j == n - 1))
                return ins

            def transposes(key, blocks, rows, cols, signal=psum_filled):
                bank = begin(key)
                for n, block_ in enumerate(blocks):
                    ins = nc.tensor.transpose(bank[0:cols, n * rows:(n + 1) * rows], block_, ident[0:rows, 0:rows])
                ins.then_inc(signal, 1)

            pe.wait_ge(consts, 1)
            pe.wait_ge(edge_tab, 1)
            transposes("edge_cols", [edf[:, w, b * T:(b + 1) * T] for w in range(2) for b in range(ROW)], ER, T)
            bank = begin("edge_range")
            product(bank[0:NT, 0:2 * ET], [(ones[0:ER, 0:NT], mdiag[:, :, :].rearrange("p w a -> p (w a)"))]
                    ).then_inc(psum_filled, 1)
            pe.wait_ge(bounds_ready, 1)
            count, turn, used, large = (pe.alloc_register(f"pe_{k}") for k in ("count", "turn", "used", "large"))
            pe.reg_mov(large, 0)
            pe.reg_mov(turn, 0)
            for b in range(EH):
                pe.sem_inc(oh_used[b], 1)

            def count_step(banks, start, stop):
                pe.reg_add(turn, turn, 1)
                for b in range(EH):
                    pe.wait_ge(oh_ready[b], turn)
                    for j, (c0, cn) in enumerate(CH):
                        ins = nc.tensor.matmul(banks[j][0:T, 0:cn], ohd[:, b, 0:T], ohs[b][:, c0:c0 + cn],
                                               start=start and b == 0, stop=stop and b == EH - 1)
                    ins.then_inc(oh_used[b], 1)

            for t in range(NT):
                banks = [begin(("A", t, j)) for j in range(3)]
                pe.reg_load(count, bounds[t:t + 1, 1:2])
                with pe.If(pe.snap(count, min_val=3, max_val=STEPS) > MAX_STEPS):
                    pe.reg_mov(large, 1)
                pe.reg_sub(count, count, 2)
                count_step(banks, True, False)
                with pe.Fori(0, count) as _i:
                    count_step(banks, False, False)
                count_step(banks, False, True)
                pe.reg_add(used, turn, 1)
                pe.wait_ge(oh_used[EH - 1], used)
                pe.sem_inc(psum_filled, 3)
                if t >= 1:
                    for j, (s0, sn) in enumerate(GROUPS):
                        for jj in range(3):
                            evacuated(pe, ("A", t - 1, jj))
                        transposes(("AT", t - 1, j), [arow[:, (t - 1) % 2, s * T:(s + 1) * T]
                                                      for s in range(s0, s0 + sn)], T, T)
            for jj in range(3):
                evacuated(pe, ("A", NT - 1, jj))
            for j, (s0, sn) in enumerate(GROUPS):
                transposes(("AT", NT - 1, j), [arow[:, (NT - 1) % 2, s * T:(s + 1) * T]
                                               for s in range(s0, s0 + sn)], T, T)
            pe.wait_ge(ld["gw"], 16)
            for k in range(C):
                transposes(("gWT", k), [gws[:, o, k * 128:(k + 1) * 128] for o in range(C)], 128, 128)
            for j in range(3):
                for t in (NT - 2, NT - 1):
                    evacuated(pe, ("AT", t, j))
            pe.wait_ge(x_low, 1)
            for n in range(4):
                if n < 3:
                    c0, cn = CH[n]
                    banks = [begin(("agg", n, c)) for c in range(C)]
                    for s in range(NT):
                        pe.wait_ge(at_high, n * NT + s + 1)
                        if s == NT - 1:
                            pe.wait_ge(at_low, (n + 1) * NT)
                            with pe.If(pe.snap(large, min_val=0, max_val=1) > 0):
                                for s2 in range(NT):
                                    for c in range(C):
                                        nc.tensor.matmul(banks[c][:, 0:cn], xh[:, s2, c * 128:(c + 1) * 128],
                                                         atl[:, s2, c0:c0 + cn], start=False, stop=False)
                        for c in range(C):
                            k = slice(c * 128, (c + 1) * 128)
                            nc.tensor.matmul(banks[c][:, 0:cn], xh[:, s, k], ath[:, s, 0:cn], start=(s == 0), stop=False)
                            ins = nc.tensor.matmul(banks[c][:, 0:cn], xl[:, s, k], ath[:, s, 0:cn], start=False,
                                                   stop=(s == NT - 1))
                            if s == NT - 1:
                                ins.then_inc(psum_filled, 1)
                        if s < NT - 1:
                            ins.then_inc(at_used, 1)
                if n == 0:
                    continue
                for k in range(C):
                    evacuated(pe, ("gWT", k))
                    evacuated(pe, ("agg", n - 1, k))
                for t in tiles(n - 1):
                    bank = begin(("gnn", t))
                    r0 = (t - GROUPS[n - 1][0]) * T
                    product(bank[0:T, :], [(aggT[(n - 1) % 2][:, c, r0:r0 + T], gwT[:, c, :]) for c in range(C)]
                            ).then_inc(psum_filled, 1)

            pe.wait_ge(normed, 2 * NT)
            for j in range(3):
                for c in range(C):
                    transposes(("hT", c, j), [hn[:, t, c * 128:(c + 1) * 128] for t in tiles(j)], T, 128)
            pe.wait_ge(wv_split, 1)
            for j in range(3):
                pe.wait_ge(h_split, C * (j + 1))
                for t in tiles(j):
                    r = slice(t * T, (t + 1) * T)
                    bank = begin(("v", t))
                    split_product(bank[0:T, :], [(hTh[:, c, r], hTl[:, c, r], wvh[:, c, :], wvl[:, c, :])
                                                 for c in range(C)]).then_inc(psum_filled, 1)

            def queries_and_keys(p, groups):
                for n, w in groups:
                    c0, cn = CH[n]
                    q = slice(w * D + p * 128, w * D + (p + 1) * 128)
                    bank = begin(("qk", p, n, w))
                    split_product(bank[:, 0:cn], [(wqkh[:, c, q], wqkl[:, c, q], hTh[:, c, c0:c0 + cn],
                                                   hTl[:, c, c0:c0 + cn]) for c in range(C)]
                                  ).then_inc(psum_filled, 1)

            pe.wait_ge(wqk_split, 1)
            queries_and_keys(0, qk_groups)
            pe.wait_ge(p_split, 1)
            for p in range(PAIRS):
                kvb = [begin(("kv", p, i)) for i in range(2)]

                def sum_and_transpose(t):
                    evacuated(pe, ("kf", p, t))
                    for i in range(2):
                        ins = nc.tensor.matmul(kvb[i][0:DH + 1, 0:NF], v65[:, t, 2 * p + i, :],
                                               ering[:, 2 * (t % 2), i * NF:(i + 1) * NF],
                                               start=(t == 0), stop=(t == NT - 1))
                        if t == NT - 1:
                            ins.then_inc(psum_filled, 1)
                    evacuated(pe, ("qf", p, t))
                    transposes(("qT", p, t), [ering[:, 2 * (t % 2) + 1, f * 128:(f + 1) * 128]
                                              for f in range(2 * FC)], T, 128)

                for t in range(NT):
                    for n, w in qk_groups:
                        if t == GROUPS[n][0]:
                            evacuated(pe, ("qk", p, n, w))
                    for w, name in ((1, "kf"), (0, "qf")):
                        bank = begin((name, p, t))
                        for i in range(2):
                            both = qkT[w][:, i, t * T:(t + 1) * T]
                            ins = product(bank[0:T, i * NF:(i + 1) * NF], [(both, pmh[:, :]), (both, pml[:, :])])
                        ins.then_inc(psum_filled, 1)
                    if t >= 1:
                        sum_and_transpose(t - 1)
                sum_and_transpose(NT - 1)
                if p < PAIRS - 1:
                    queries_and_keys(p + 1, before_kvT)
                for i in range(2):
                    evacuated(pe, ("kv", p, i))
                transposes(("kvT", p), [kvT[:, i, f * 128:(f + 1) * 128] for i in range(2) for f in range(FC)],
                           DH + 1, 128)
                if p < PAIRS - 1:
                    queries_and_keys(p + 1, after_kvT)
                evacuated(pe, ("kvT", p))
                evacuated(pe, ("qT", p, NT - 1))
                for i in range(2):
                    for n, (c0, cn) in enumerate(CH):
                        bank = begin(("att", p, i, n))
                        product(bank[0:DH + 1, 0:cn], [(kv[:, i * FC + f, :], eqT[:, i * FC + f, c0:c0 + cn])
                                                       for f in range(FC)]).then_inc(psum_filled, 1)
            pe.wait_ge(ld["wp"], 16)
            pe.wait_ge(attn_ready, PAIRS - 1)
            for t in range(8):
                bank = begin(("proj", t))
                for p in range(PAIRS - 1):
                    nc.tensor.matmul(bank[0:T, :], attT[:, p, t * T:(t + 1) * T], wps[:, p, :], start=(p == 0),
                                     stop=False)
            pe.wait_ge(attn_ready, PAIRS)
            for t in range(NT):
                bank = begin(("proj", t)) if t >= 8 else P[plan.order[("proj", t)][1]]
                for p in range(PAIRS if t >= 8 else 1):
                    p = p if t >= 8 else PAIRS - 1
                    ins = nc.tensor.matmul(bank[0:T, :], attT[:, p, t * T:(t + 1) * T], wps[:, p, :],
                                           start=(t >= 8 and p == 0), stop=(p == PAIRS - 1))
                ins.then_inc(psum_filled, 1)

            for n in range(4):
                if n < 3:
                    _, cn = CH[n]
                    pe.wait_ge(normed, 2 * NT + tiles(n)[-1] + 1)
                    for c in range(C):
                        transposes(("h2T", c, n), [hn[:, t, c * 128:(c + 1) * 128] for t in tiles(n)], T, 128)
                if n >= 1:
                    pe.wait_ge(w_low, 2)
                    for t in tiles(n - 1):
                        r = slice((t - GROUPS[n - 1][0]) * T, (t - GROUPS[n - 1][0] + 1) * T)
                        bank = begin(("down", t))
                        for m in range(MC):
                            if t == GROUPS[n - 1][0]:
                                pe.wait_ge(g_split, MC * (n - 1) + m + 1)
                            w = slice(m * D, (m + 1) * D)
                            ins = split_product(bank[0:T, :], [(gh[:, m, r], gl[:, m, r], w2h[:, w], w2l[:, w])],
                                                m == 0, m == MC - 1)
                        ins.then_inc(psum_filled, 1)
                if n < 3:
                    pe.wait_ge(w_low, 1)
                    for m in range(MC):
                        bank = begin(("up", n, m))
                        for c in range(C):
                            if m == 0:
                                pe.wait_ge(h2_split, C * n + c + 1)
                            w = slice(c * M + m * 128, c * M + (m + 1) * 128)
                            ins = split_product(bank[:, 0:cn], [(w1h[:, w], w1l[:, w], h2h[:, c, 0:cn],
                                                                 h2l[:, c, 0:cn])], c == 0, c == C - 1)
                        ins.then_inc(psum_filled, 1)
            pe.wait_ge(boh_ready, 1)
            bank = begin("rank")
            all_bins = boh[:, :, :].rearrange("p t k -> p (t k)")
            nc.tensor.matmul(bank[0:T, 0:(NT + 1) * NB], trib[:, 0:T], all_bins, start=True, stop=False)
            for t in range(NT):
                ins = nc.tensor.matmul(bank[0:T, (t + 1) * NB:(NT + 1) * NB], onesb[:, 0:T],
                                       boh[:, t:t + 1, :].to_broadcast([T, NT - t, NB]), start=False,
                                       stop=(t == NT - 1))
            ins.then_inc(psum_filled, 1)
            bank = begin("tokens")
            pe.wait_ge(inv_ready, 1)
            for t in range(NT):
                ins = nc.tensor.matmul(bank[:, 0:2 * SLOT_TILES], ohb[:, t, :],
                                       inv[:, t, :, :].rearrange("p w j -> p (w j)"), start=(t == 0), stop=(t == NT - 1))
            ins.then_inc(psum_filled, 1)
            used = slot_tiles(pe)
            pe.wait_ge(ld["fw"], 16 * (EARLY - 1))
            expert = pe.alloc_register("pe_expert")

            def transpose_slots(s):
                with if_used(pe, s, used):
                    pe.wait_ge(ld_ys[s], 16)
                    transposes(("yT", s), [ys[:, s, c * 128:(c + 1) * 128] for c in range(C)], ST, 128,
                               ffn_filled["yT"])

            transpose_slots(0)
            for s in range(SLOT_TILES):
                if s + 1 < SLOT_TILES:
                    transpose_slots(s + 1)
                with if_used(pe, s, used):
                    evacuated(pe, ("yT", s))
                    pe.reg_load(expert, exr[0:1, s:s + 1])
                    e = pe.snap(expert, min_val=0, max_val=NB - 1)
                    with pe.If(e > EARLY - 1):
                        pe.wait_ge(ld["fw_late"], 16)
                    bank = begin(("ffn", s))
                    product(bank[:, :], [(yT[:, s % 2, c * ST:(c + 1) * ST], fw[:, bass.ds((e * C + c) * D, D)])
                                         for c in range(C)]).then_inc(ffn_filled["ffn"], 1)


_INS = ['x', 'src', 'dst', 'L0_gnn_alpha', 'L0_gnn_W', 'L0_gnn_b', 'L0_mix_Wqkv', 'L0_mix_bqkv', 'L0_mix_Pmat',
        'L0_mix_Wproj', 'L0_mix_bproj', 'L0_mix_W1', 'L0_mix_b1', 'L0_mix_W2', 'L0_mix_b2', 'L0_mix_g1', 'L0_mix_be1',
        'L0_mix_g2', 'L0_mix_be2', 'L0_ffn_W']


def kernel(**inputs):
    import numpy as np
    import concourse.bacc as bacc
    from concourse.bass_utils import run_bass_kernel_spmd

    nc = bacc.Bacc("TRN2", target_bir_lowering=False, num_devices=1)
    arrays, args = {}, []
    for name in _INS:
        a = np.ascontiguousarray(inputs[name])
        if a.ndim == 0:
            a = a.reshape(1)
        arrays["in_" + name] = a
        args.append(nc.dram_tensor("in_" + name, a.shape, mybir.dt.from_np(a.dtype), kind="ExternalInput").ap())
    out = nc.dram_tensor("out", arrays["in_x"].shape, F32, kind="ExternalOutput").ap()
    build(nc, *args, out)
    r = run_bass_kernel_spmd(nc, [arrays], core_ids=[0])
    return r.results[0]["out"]
```
